# Optimizing a Trainium2 kernel written in Bass

```python
import numpy as np
import jax
import jax.numpy as jnp

def _softmax(x, axis=-1):
    return jax.nn.softmax(x, axis=axis)

def _gelu(x):
    return jax.nn.gelu(x, approximate=True)

def _silu(x):
    return jax.nn.silu(x)

def _sigmoid(x):
    return jax.nn.sigmoid(x)

def _layernorm(x, axis=-1, eps=1e-05):
    m = jnp.mean(x, axis=axis, keepdims=True)
    v = jnp.var(x, axis=axis, keepdims=True)
    return (x - m) / jnp.sqrt(v + eps)

def _scatter_add(tgt, idx, src, axis=0):
    return tgt.at[idx].add(src)

def _segment_sum(src, seg, n):
    return jax.ops.segment_sum(src, seg, n)
kernel_name = 'mk_xattn_ffn_d1_seqx_r8_2118c0'

def setup_inputs(seed: int=0):
    np.random.seed(seed)
    _w = jnp.asarray

    def _rec_inputs():
        import jax
        import jax.numpy as jnp
        _rk = jax.random.key(seed)
        x = 7.22e-05 + 1 * jax.random.normal(jax.random.fold_in(_rk, 1), (32, 64, 256), jnp.float32)
        _lenS = 64 - jax.random.randint(jax.random.fold_in(_rk, 7), (32,), 0, max(1, 64 // 4) + 1, jnp.int32)
        _lenS2 = 64 - jax.random.randint(jax.random.fold_in(_rk, 8), (32,), 0, max(1, 64 // 4) + 1, jnp.int32)
        _ctx_512P = jax.random.normal(jax.random.fold_in(_rk, 11), (32, 16, 64), jnp.float32)
        _ctx_512c = jax.random.dirichlet(jax.random.fold_in(_rk, 511), 0.3 * jnp.ones((16,), jnp.float32), (32, 64))
        _ctx_512t = jnp.einsum('bsk,bkd->bsd', _ctx_512c, _ctx_512P)
        _ctx_512t = _ctx_512t * jax.lax.rsqrt(jnp.mean(jnp.square(_ctx_512t)) + 1e-12) * 0.953939
        ctx_512 = -0.000514642 + 1.00011 * (_ctx_512t + 0.3 * jax.random.normal(jax.random.fold_in(_rk, 611), (32, 64, 64), jnp.float32))
        return (x, ctx_512)
    x, ctx_512 = _rec_inputs()

    def _L0_xattn_setup():
        import jax, jax.numpy as jnp
        import numpy as np
        import math
        NUM_Q_HEADS = 32
        NUM_KV_HEADS = 8
        key = jax.random.key(seed)
        k1, k2, k3 = jax.random.split(key, 3)
        B, S, E = (2, 256, 256)
        kv_E = NUM_KV_HEADS * (E // NUM_Q_HEADS)
        q = jax.random.normal(k1, (B, S, E), dtype=jnp.float32)
        k = jax.random.normal(k2, (B, S, kv_E), dtype=jnp.float32)
        v = jax.random.normal(k3, (B, S, kv_E), dtype=jnp.float32)
        return {'q': q, 'k': k, 'v': v}
    _L0_xattn_all = _L0_xattn_setup()
    _L0_xattn_in = {k: v for k, v in _L0_xattn_all.items() if k in ()}
    del _L0_xattn_all

    def _L0_ffn_setup():
        import jax, jax.numpy as jnp
        import numpy as np
        from jax import lax
        B, S, H = (1, 256, 256)
        E, I, TOP_K = (64, 64, 8)
        SHARED_I = 64
        key = jax.random.key(seed)
        ks = jax.random.split(key, 8)
        sc = 0.02
        return {'hidden_states': jax.random.normal(ks[0], (B, S, H), jnp.float32), 'router_w': jax.random.normal(ks[1], (E, H), jnp.float32) * sc, 'gate_up_proj': jax.random.normal(ks[2], (E, 2 * I, H), jnp.float32) * sc, 'down_proj': jax.random.normal(ks[3], (E, H, I), jnp.float32) * sc, 'shared_gate_w': jax.random.normal(ks[4], (SHARED_I, H), jnp.float32) * sc, 'shared_up_w': jax.random.normal(ks[5], (SHARED_I, H), jnp.float32) * sc, 'shared_down_w': jax.random.normal(ks[6], (H, SHARED_I), jnp.float32) * sc, 'shared_expert_gate_w': jax.random.normal(ks[7], (1, H), jnp.float32) * sc}
    _L0_ffn_all = _L0_ffn_setup()
    _L0_ffn_in = {k: v for k, v in _L0_ffn_all.items() if k in ('router_w', 'gate_up_proj', 'down_proj', 'shared_gate_w', 'shared_up_w', 'shared_down_w', 'shared_expert_gate_w')}
    del _L0_ffn_all
    return {'x': x, 'ctx_512': ctx_512, 'L0_ffn_router_w': _L0_ffn_in['router_w'], 'L0_ffn_gate_up_proj': _L0_ffn_in['gate_up_proj'], 'L0_ffn_down_proj': _L0_ffn_in['down_proj'], 'L0_ffn_shared_gate_w': _L0_ffn_in['shared_gate_w'], 'L0_ffn_shared_up_w': _L0_ffn_in['shared_up_w'], 'L0_ffn_shared_down_w': _L0_ffn_in['shared_down_w'], 'L0_ffn_shared_expert_gate_w': _L0_ffn_in['shared_expert_gate_w']}

def reference(x, ctx_512, L0_ffn_router_w, L0_ffn_gate_up_proj, L0_ffn_down_proj, L0_ffn_shared_gate_w, L0_ffn_shared_up_w, L0_ffn_shared_down_w, L0_ffn_shared_expert_gate_w):
    import jax
    import jax.numpy as jnp

    def _L0_xattn_ref(q, k, v):
        import jax, jax.numpy as jnp
        import numpy as np
        import math
        NUM_Q_HEADS = 32
        NUM_KV_HEADS = 8
        B, S, E = q.shape
        H, KV = (NUM_Q_HEADS, NUM_KV_HEADS)
        D = E // H
        G = H // KV
        scale = math.sqrt(D)
        qh = q.reshape(B, S, KV, G, D).transpose(0, 2, 3, 1, 4)
        kh = k.reshape(B, S, KV, D).transpose(0, 2, 1, 3)
        vh = v.reshape(B, S, KV, D).transpose(0, 2, 1, 3)
        scores = jnp.einsum('bkgsd,bktd->bkgst', qh, kh) / scale
        weights = jax.nn.softmax(scores, axis=-1)
        out = jnp.einsum('bkgst,bktd->bkgsd', weights, vh)
        return out.transpose(0, 3, 1, 2, 4).reshape(B, S, E)

    def _L0_ffn_ref(hidden_states, router_w, gate_up_proj, down_proj, shared_gate_w, shared_up_w, shared_down_w, shared_expert_gate_w):
        import jax, jax.numpy as jnp
        import numpy as np
        from jax import lax
        B, S, H = (1, 256, 256)
        E, I, TOP_K = (64, 64, 8)
        SHARED_I = 64
        b, s, h_dim = hidden_states.shape
        h = hidden_states.reshape(-1, h_dim)
        T = h.shape[0]
        shared = jnp.dot(jax.nn.silu(jnp.dot(h, shared_gate_w.T)) * jnp.dot(h, shared_up_w.T), shared_down_w.T)
        shared = jax.nn.sigmoid(jnp.dot(h, shared_expert_gate_w.T)) * shared
        logits = jnp.dot(h, router_w.T)
        probs = jax.nn.softmax(logits.astype(jnp.float32), axis=-1)
        top_vals, top_idx = lax.top_k(probs, TOP_K)
        top_vals = top_vals / jnp.sum(top_vals, axis=-1, keepdims=True)
        top_vals = top_vals.astype(h.dtype)
        comb = jnp.zeros((T, E), h.dtype).at[jnp.arange(T)[:, None], top_idx].add(top_vals)

        def body(acc, xs):
            wgu, wd, w_e = xs
            g, u = jnp.split(jnp.dot(h, wgu.T), 2, axis=-1)
            eo = jnp.dot(jax.nn.silu(g) * u, wd.T)
            return (acc + eo * w_e[:, None], None)
        expert_out, _ = lax.scan(body, jnp.zeros_like(h), (gate_up_proj, down_proj, comb.T))
        return (expert_out + shared).reshape(b, s, h_dim)
    x = x + _L0_xattn_ref(_layernorm(x, axis=-1), ctx_512, ctx_512)
    x = x + _L0_ffn_ref(_layernorm(x, axis=-1), L0_ffn_router_w, L0_ffn_gate_up_proj, L0_ffn_down_proj, L0_ffn_shared_gate_w, L0_ffn_shared_up_w, L0_ffn_shared_down_w, L0_ffn_shared_expert_gate_w)
    return x

_drawn_inputs = setup_inputs


def setup_inputs(seed=0):
    import zlib

    import numpy as np

    out = dict(_drawn_inputs(seed))
    spreads = {}
    factors = {'L0_ffn_router_w': 8.0,
     'L0_ffn_gate_up_proj': 8.0,
     'L0_ffn_down_proj': 8.0,
     'L0_ffn_shared_gate_w': 8.0,
     'L0_ffn_shared_up_w': 8.0,
     'L0_ffn_shared_down_w': 8.0,
     'L0_ffn_shared_expert_gate_w': 8.0}
    for name, (base, spread) in spreads.items():
        noise = np.random.default_rng([zlib.crc32(name.encode()), seed]).standard_normal(out[name].shape)
        drawn = base * np.exp(spread * noise) if base else spread * noise
        out[name] = jnp.asarray(drawn.astype(out[name].dtype))
    for name, factor in factors.items():
        out[name] = (out[name] * factor).astype(out[name].dtype)
    return out
```

```python
from contextlib import ExitStack

import concourse.bass as bass
from concourse import mybir

F32 = mybir.dt.float32
F32R = mybir.dt.float32r
BF16 = mybir.dt.bfloat16
I32 = mybir.dt.int32
U32 = mybir.dt.uint32
ALU = mybir.AluOpType
ACT = mybir.ActivationFunctionType
AX = mybir.AxisListType.X

P = 128
B, S, C = 32, 64, 256
KS, KD = 64, 64
KV, G, D = 8, 4, 8
T = B * S // P
CH = C // P
E, I, TOPK = 64, 64, 8
N = B * S
EPS = 1e-5
SCALE = float(D) ** -0.5
CAP = P + N
ROW = C + 2 * TOPK
FS = 3 * I + 1
TILES = -(-((N * TOPK + E * (P - 1)) // P) // 4) * 4
BIG = float(1 << 20)
WCH = 4


class Steps:

    def __init__(self, sem, *names):
        self.sem, self.names = sem, names

    def mark(self, ins, name):
        assert name in self.names
        return ins.then_inc(self.sem, 1)

    def wait(self, eng, rnd, name):
        eng.wait_ge(self.sem, rnd * len(self.names) + (self.names.index(name) + 1))


def pipelined(eng, step, rounds, lag, unroll, first):
    for s in range(first):
        step(s, s % unroll)
    with eng.Fori(first // unroll, rounds // unroll) as i:
        for u in range(unroll):
            step(i * unroll + u if u else i * unroll, u)
    for s in range(rounds, rounds + lag):
        step(s, s % unroll)


def hold(eng, passed):
    eng.sem_inc(passed, 1)


def live(s, lag, rounds):
    return not isinstance(s, int) or 0 <= s - lag < rounds


def later(s, n):
    return not isinstance(s, int) or s >= n


RSQRT = ["v", "guess"] + [f"n{i}{c}" for i in range(3) for c in "abc"]


def rsqrt(dve, steps, rnd, out, var, v, a, b):
    def do(ins, name):
        steps.mark(ins, name)
        steps.wait(dve, rnd, name)

    do(dve.tensor_scalar(v, var, EPS, None, ALU.add), "v")
    do(dve.tensor_scalar(out.bitcast(I32), v.bitcast(I32), -0.5, float(0x5f3759df), ALU.mult, ALU.add), "guess")
    for i in range(3):
        do(dve.tensor_tensor(a, out, out, ALU.mult), f"n{i}a")
        do(dve.scalar_tensor_tensor(out=b, in0=a, scalar=-0.5, in1=v, op0=ALU.mult, op1=ALU.mult), f"n{i}b")
        do(dve.scalar_tensor_tensor(out=out, in0=b, scalar=1.5, in1=out, op0=ALU.add, op1=ALU.mult), f"n{i}c")


def at(i):
    return bass.ds(i, 1)


def moe_block(nc, x, ctx_, router_w, gate_up, down, sh_gate, sh_up, sh_down, sh_weight, out):
    lists = nc.dram_tensor("lists", [E * CAP, ROW], F32).ap()
    results = nc.dram_tensor("results", [N * TOPK, C], F32).ap()
    x_tiles = x.rearrange("(n b) s c -> (b s) n c", b=2)
    out_tiles = out.rearrange("(n b) s c -> (b s) n c", b=2)
    with ExitStack() as ctx:
        def sb(name, shape, dt=F32):
            return ctx.enter_context(nc.sbuf_tensor(name, shape, dt))

        keep = dict(
            w_gu=sb("w_gu", [P, E, CH, P]),
            w_dn=sb("w_dn", [I, E, C]),
            acc=sb("acc", [P, T, C]),
            w_fs=sb("w_fs", [P, CH, FS]),
            w_sd=sb("w_sd", [I, C]),
            mean=sb("mean", [P, T, 2]),
            rstd=sb("rstd", [P, T]),
            ident=sb("ident", [P, P]),
            kvmask=sb("kvmask", [P, KV]),
            pick=sb("pick", [64, 32, 64], F32R),
            before=sb("before", [P, P], BF16),
            ones=sb("ones", [P, P], BF16),
            iota_e=sb("iota_e", [P, E]),
            list_base=sb("list_base", [P, E]),
            dest=sb("dest", [P, T, TOPK]),
            weights=sb("weights", [P, T, TOPK]),
            chosen=sb("chosen", [P, 2, E], BF16),
        )
        prepare(nc, keep, lists, x_tiles, router_w, gate_up, down, sh_gate, sh_up, sh_down, sh_weight)
        route(nc, keep, lists, ctx_)
        experts(nc, keep, lists, results)
        combine(nc, keep, results, out_tiles)


def prepare(nc, k, lists, x_tiles, router_w, gate_up, down, sh_gate, sh_up, sh_down, sh_weight):
    w_gu, w_dn, acc, w_fs, w_sd = k["w_gu"], k["w_dn"], k["acc"], k["w_fs"], k["w_sd"]
    mean, rstd, ident, kvmask, pick = k["mean"], k["rstd"], k["ident"], k["kvmask"], k["pick"]
    before, ones, iota_e, list_base, dest = k["before"], k["ones"], k["iota_e"], k["list_base"], k["dest"]
    chunks = E // WCH
    with ExitStack() as ctx:
        def sb(name, shape, dt=F32):
            return ctx.enter_context(nc.sbuf_tensor(f"prepare_{name}", shape, dt))

        def sem(name):
            return ctx.enter_context(nc.semaphore(f"prepare_{name}"))

        gu_in = [sb(f"gu_in{u}", [P, WCH, C]) for u in range(2)]
        dn_in = [sb(f"dn_in{u}", [P, CH, WCH, I]) for u in range(2)]
        fs_in = sb("fs_in", [P, 2, C])
        sd_in = sb("sd_in", [P, CH, I])
        filler = sb("filler", [P, ROW])
        stats = sb("stats", [P, T, 6])
        sel32 = sb("sel32", [64, 32])
        rs_tmp = sb("rs_tmp", [P, 3, T])
        ps_gu = [ctx.enter_context(nc.psum_tensor(f"prepare_ps_gu{u}", [P, 2, CH, P], F32)) for u in range(2)]
        ps_dn = [ctx.enter_context(nc.psum_tensor(f"prepare_ps_dn{u}", [I, 2, C], F32)) for u in range(2)]
        ps_fs = ctx.enter_context(nc.psum_tensor("prepare_ps_fs", [P, 2, FS], F32))
        ps_sd = ctx.enter_context(nc.psum_tensor("prepare_ps_sd", [I, C], F32))

        x_in = [sem(f"x_in{q}") for q in range(4)]
        fs_loaded = sem("fs_loaded")
        gu_loaded = [sem(f"gu_loaded{u}") for u in range(2)]
        filled = sem("filled")
        passed = sem("passed")
        const = sem("const")
        filler_made = sem("filler_made")
        const_chain = sem("const_chain")
        stats_done = sem("stats_done")
        dve_rs = Steps(sem("dve_rs"), *RSQRT)
        pe_chunk = Steps(sem("pe_chunk"), "gu0", "dn0", "gu1", "dn1")
        act_chunk = Steps(sem("act_chunk"), "gu0", "gu1")
        dve_chunk = Steps(sem("dve_chunk"), "dn0", "dn1")
        pe_fs = sem("pe_fs")
        dve_fs = sem("dve_fs")
        block = ctx.enter_context(nc.Block())
        gu_dram = gate_up.rearrange("(n e) f c -> n f e c", e=WCH)
        dn_dram = down.rearrange("(n e) (k p) i -> n k p e i", e=WCH, p=P)

        @block.sync
        def _(sp):
            sp.dma_start(fs_in[0:E, 0, :], router_w).then_inc(fs_loaded, 16)
            sp.dma_start(fs_in[E:P, 0, :], sh_gate).then_inc(fs_loaded, 16)
            sp.dma_start(fs_in[0:I, 1, :], sh_up).then_inc(fs_loaded, 16)
            sp.dma_start(fs_in[I:I + 1, 1, :], sh_weight).then_inc(fs_loaded, 16)
            sp.dma_start(sd_in[:, :, :], sh_down.rearrange("(k p) i -> p k i", p=P)).then_inc(fs_loaded, 16)

            def step(s, u):
                if later(s, 2):
                    pe_chunk.wait(sp, s - 2, "dn1")
                    hold(sp, passed)
                sp.dma_start(gu_in[u][:, :, :], gu_dram[at(s)].rearrange("n f e c -> (n f) e c")
                             ).then_inc(gu_loaded[u], 16)
                for h in range(CH):
                    sp.dma_start(dn_in[u][:, h, :, :],
                                 dn_dram[at(s), h].rearrange("n p e i -> (n p) e i")).then_inc(gu_loaded[u], 16)

            pipelined(sp, step, chunks, 0, 2, 2)
            sp.wait_ge(filler_made, 2)
            sp.dma_start(lists.rearrange("(e r) c -> r e c", r=CAP)[0:P],
                         filler[:, :].rearrange("p (o c) -> p o c", o=1).broadcast_to([P, E, ROW])
                         ).then_inc(filled, 16)
            sp.wait_ge(filled, 16)

        @block.scalar
        def _(act):
            for q in range(4):
                n = T // 4
                act.dma_start(acc[:, q * n:(q + 1) * n, :], x_tiles[:, q * n:(q + 1) * n, :]).then_inc(x_in[q], 16)

            def step(s, u):
                for h in range(2):
                    pe_chunk.wait(act, s, f"gu{h}")
                    act_chunk.mark(nc.scalar.copy(w_gu[:, bass.ds(s * WCH + 2 * h, 2), :, :], ps_gu[h][:, :, :, :]),
                                   f"gu{h}")

            pipelined(act, step, chunks, 0, 2, 2)

        @block.tensor
        def _(pe):
            pe.wait_ge(const, 1)
            pe.wait_ge(fs_loaded, 80)
            for c in range(CH):
                cols = slice(c * P, (c + 1) * P)
                pe.transpose(ps_fs[:, c, 0:P], fs_in[:, 0, cols], ident[:, :])
                pe.transpose(ps_fs[:, c, P:FS], fs_in[0:I + 1, 1, cols], ident[0:I + 1, 0:I + 1])
                mm = pe.transpose(ps_sd[:, cols], sd_in[:, c, :], ident[:, :])
            mm.then_inc(pe_fs, 1)

            def step(s, u):
                pe.wait_ge(gu_loaded[u], 16 * (1 + CH) * ((s - u) // 2 + 1) if isinstance(s, int)
                           else (s - u) * (8 * (1 + CH)) + 16 * (1 + CH))
                for h in range(2):
                    if later(s, 1):
                        act_chunk.wait(pe, s - 1, f"gu{h}")
                    for e in range(2):
                        for c in range(CH):
                            mm = pe.transpose(ps_gu[h][:, e, c, :], gu_in[u][:, 2 * h + e, c * P:(c + 1) * P],
                                              ident[:, :])
                    pe_chunk.mark(mm, f"gu{h}")
                    if later(s, 1):
                        dve_chunk.wait(pe, s - 1, f"dn{h}")
                        hold(pe, passed)
                    for e in range(2):
                        for c in range(CH):
                            mm = pe.transpose(ps_dn[h][:, e, c * P:(c + 1) * P], dn_in[u][:, c, 2 * h + e, :],
                                              ident[:, :])
                    pe_chunk.mark(mm, f"dn{h}")

            pipelined(pe, step, chunks, 0, 2, 2)

        @block.vector
        def _(dve):
            dve.wait_ge(const, 2)
            dve.tensor_copy(pick[:, :, :], sel32[:, :].rearrange("p (c o) -> p c o", o=1).broadcast_to([64, 32, 64]))
            dve.wait_ge(pe_fs, 1)
            dve.tensor_copy(w_fs[:, :, :], ps_fs[:, :, :])
            dve.tensor_copy(w_sd[:, :], ps_sd[:, :]).then_inc(dve_fs, 1)

            def step(s, u):
                for h in range(2):
                    pe_chunk.wait(dve, s, f"dn{h}")
                    dve_chunk.mark(dve.tensor_copy(w_dn[:, bass.ds(s * WCH + 2 * h, 2), :], ps_dn[h][:, :, :]),
                                   f"dn{h}")

            for t in range(T):
                if t % (T // 4) == 0:
                    dve.wait_ge(x_in[t // (T // 4)], 16)
                dve.bn_stats(stats[:, t, :], acc[:, t, :]).then_inc(stats_done, 1)
            dve.wait_ge(stats_done, T)
            for t in range(T):
                dve.bn_aggr(mean[:, t, :], stats[:, t, :]).then_inc(stats_done, 1)
            dve.wait_ge(stats_done, 2 * T)
            rsqrt(dve, dve_rs, 0, rstd[:, :], mean[:, :, 1], rs_tmp[:, 0, :], rs_tmp[:, 1, :], rs_tmp[:, 2, :])
            pipelined(dve, step, chunks, 0, 2, 2)

        @block.gpsimd
        def _(pool):
            made = [0]

            def link(ins):
                made[0] += 1
                ins.then_inc(const_chain, 1)
                pool.wait_ge(const_chain, made[0])

            link(pool.memset(ident[:, :], 0.0))
            pool.affine_select(out=ident[:, :], in_=ident[:, :], compare_op=ALU.not_equal, fill=1.0, base=0,
                               pattern=[[-1, P]], channel_multiplier=1).then_inc(const, 1)
            link(pool.memset(sel32[:, :], 0.0))
            link(pool.affine_select(out=sel32[:, :], in_=sel32[:, :], compare_op=ALU.not_equal, fill=1.0, base=0,
                                    pattern=[[-1, 32]], channel_multiplier=1))
            pool.affine_select(out=sel32[:, :], in_=sel32[:, :], compare_op=ALU.not_equal, fill=1.0, base=-32,
                               pattern=[[-1, 32]], channel_multiplier=1).then_inc(const, 1)
            link(pool.memset(filler[:, :], 0.0))
            pool.memset(filler[:, C:C + TOPK], -1.0).then_inc(filler_made, 2)
            link(pool.memset(kvmask[:, :], 1.0))
            for h in range(2):
                m = kvmask[h * 64:(h + 1) * 64, :]
                link(pool.affine_select(out=m, in_=m, compare_op=ALU.is_ge, fill=0.0, base=0,
                                        pattern=[[-D, KV]], channel_multiplier=1))
                link(pool.affine_select(out=m, in_=m, compare_op=ALU.is_ge, fill=0.0, base=D - 1,
                                        pattern=[[D, KV]], channel_multiplier=-1))
            pool.memset(ones[:, :], 1.0)
            link(pool.memset(before[:, :], 1.0))
            pool.affine_select(out=before[:, :], in_=before[:, :], compare_op=ALU.is_ge, fill=0.0, base=-1,
                               pattern=[[1, P]], channel_multiplier=-1)
            pool.iota(iota_e[:, :], [[1, E]], base=0, channel_multiplier=0, allow_small_or_imprecise_dtypes=True)
            pool.iota(list_base[:, :], [[CAP, E]], base=P, channel_multiplier=0, allow_small_or_imprecise_dtypes=True)
            pool.iota(dest[:, :, :], [[P * TOPK, T], [1, TOPK]], base=-int(BIG), channel_multiplier=TOPK,
                      allow_small_or_imprecise_dtypes=True)
            pool.memset(k["chosen"][:, 0, :], 0.0)


def route(nc, k, lists, ctx_):
    acc, w_fs, w_sd, mean, rstd, ident = k["acc"], k["w_fs"], k["w_sd"], k["mean"], k["rstd"], k["ident"]
    kvmask, pick, before, ones = k["kvmask"], k["pick"], k["before"], k["ones"]
    iota_e, list_base, dest, weights, chosen = k["iota_e"], k["list_base"], k["dest"], k["weights"], k["chosen"]
    with ExitStack() as ctx:
        def sb(name, shape, dt=F32):
            return ctx.enter_context(nc.sbuf_tensor(f"route_{name}", shape, dt))

        def sem(name):
            return ctx.enter_context(nc.semaphore(f"route_{name}"))

        def psum(name, shape):
            return ctx.enter_context(nc.psum_tensor(f"route_{name}", shape, F32))

        key_in = [sb(f"key_in{u}", [P, KD]) for u in range(2)]
        val_in = [sb(f"val_in{u}", [P, 2, KD]) for u in range(2)]
        key_hl = sb("key_hl", [P, 2, KD], F32R)
        keys = [sb(f"keys{u}", [P, 2, KV, KS], F32R) for u in range(2)]
        vals = [sb(f"vals{u}", [P, 2, KV, D + 1]) for u in range(2)]
        q_tok = sb("q_tok", [P, G, 2, KD])
        q_hi = [sb(f"q_hi{u}", [P, 2, G, S], F32R) for u in range(2)]
        q_lo = [sb(f"q_lo{u}", [P, 2, G, S], F32R) for u in range(2)]
        negmax = sb("negmax", [P, 2, 4, KV])
        negmax_t = sb("negmax_t", [64, P], F32R)
        probs = [sb(f"probs{b}", [P, 4, G * S]) for b in range(2)]
        rden = sb("rden", [P, 4, KV])
        attn = sb("attn", [P, C])
        st = sb("st", [P, 6])
        mv = sb("mv", [P, 2])
        rs2 = sb("rs2", [P, 1])
        rs_tmp = sb("rs_tmp", [P, 3])
        row = [sb(f"row{u}", [P, ROW]) for u in range(2)]
        h_t = sb("h_t", [P, CH, P])
        lg = sb("lg", [P, FS])
        top = sb("top", [P, TOPK])
        nlmax = sb("nlmax", [P, 1])
        ex = sb("ex", [P, E])
        esum = sb("esum", [P, 1])
        eg = sb("eg", [P, I + 1])
        den = sb("den", [P, I + 1])
        sig = sb("sig", [P, I + 1])
        silu = sb("silu", [P, I])
        hid = sb("hid", [P, I])
        hid_t = sb("hid_t", [I, P])
        top_e = sb("top_e", [P, TOPK])
        idx = sb("idx", [P, TOPK], U32)
        marked = sb("marked", [P, E])
        picked = sb("picked", [P, E], BF16)
        rsum = sb("rsum", [P, 1])
        top_p = sb("top_p", [P, TOPK])
        psumk = sb("psumk", [P, 1])
        rpk = sb("rpk", [P, 1])
        slot = sb("slot", [P, E])
        junk = sb("junk", [P, TOPK, E])
        posf = sb("posf", [P, TOPK])
        pos = [sb(f"pos{u}", [P, TOPK], I32) for u in range(2)]

        ps_q = psum("ps_q", [P, G, P])
        ps_qb = ps_q[:, :, :].rearrange("p g (b s) -> p b g s", b=2)
        ps_s = [psum(f"ps_s{u}", [P, KV, KS]) for u in range(2)]
        ps_t = psum("ps_t", [P, 4, G * S])
        ps_v = psum("ps_v", [P, 512])
        ps_h = psum("ps_h", [P, 512])
        ps_l = psum("ps_l", [P, 512])
        ps_pv = ps_v[:, 0:4 * KV * (D + 1)].rearrange("p (a v d) -> p a v d", a=4, v=KV)
        ps_rank = ps_v[:, 288:288 + E]
        ps_max = ps_v[0:64, 352:352 + P]
        ps_key = ps_h[:, 0:P]
        ps_ht = ps_h[:, P:P + C].rearrange("p (c t) -> p c t", c=CH)
        ps_hid = ps_h[0:I, 384:384 + P]
        ps_lg = ps_l[:, 0:FS]
        ps_sh = ps_l[:, 256:256 + C]

        shift = sb("shift", [P, T])
        passed = sem("passed")
        shift_made = sem("shift_made")
        zeroed = sem("zeroed")
        kv_loaded = [sem(f"kv_loaded{u}") for u in range(2)]
        scattered = [sem(f"scattered{u}") for u in range(2)]
        act_q = Steps(sem("act_q"), "tokens", "high")
        dve_q = Steps(sem("dve_q"), "key_high", "key_low", "low", "keys")
        act_v = Steps(sem("act_v"), "vals")
        pe_q = Steps(sem("pe_q"), "key", "q")
        pe_s = Steps(sem("pe_s"), "s0", "s1", "s2", "s3")
        dve_s = Steps(sem("dve_s"), "s0", "s1", "s2", "s3", "copy", "high", "low")
        pe_m = Steps(sem("pe_m"), "max")
        pe_t = Steps(sem("pe_t"), "t0", "t1")
        act_t = Steps(sem("act_t"), "t0a", "t0b", "t1a", "t1b")
        pe_v = Steps(sem("pe_v"), "v0", "v1")
        dve_v = Steps(sem("dve_v"), "recip", "attn", "sum", "stats", "mean", "row")
        dve_rs = Steps(sem("dve_rs"), *RSQRT)
        pe_h = Steps(sem("pe_h"), "h_t", "logits")
        act_h = Steps(sem("act_h"), "h_t", "logits", "gates", "gate", "exp")
        dve_g = Steps(sem("dve_g"), "den", "sig", "silu", "hid", "top", "nlmax")
        dve_r = Steps(sem("dve_r"), "top_e", "index", "idx", "dest", "marked", "picked", "chosen", "rsum", "p",
                      "psum", "rpk", "w")
        pe_hid = Steps(sem("pe_hid"), "hid", "rank", "shared")
        act_hid = Steps(sem("act_hid"), "hid")
        dve_sh = Steps(sem("dve_sh"), "shared")
        dve_p = Steps(sem("dve_p"), "slot", "posf", "pos")
        block = ctx.enter_context(nc.Block())
        ctx_keys = ctx_.rearrange("(n b) t d -> n (b t) d", b=2)
        ctx_vals = ctx_.rearrange("(n b) t d -> n t b d", b=2)

        @block.sync
        def _(sp):
            def step(s, u):
                if later(s, 2):
                    dve_q.wait(sp, s - 2, "key_low")
                    hold(sp, passed)
                    act_v.wait(sp, s - 2, "vals")
                    hold(sp, passed)
                sp.dma_start(key_in[u][:, :], ctx_keys[at(s)].rearrange("n p d -> (n p) d")).then_inc(kv_loaded[u], 16)
                for c in range(2):
                    sp.dma_start(val_in[u][c * KS:(c + 1) * KS, :, :],
                                 ctx_vals[at(s)].rearrange("n t b d -> (n t) b d")).then_inc(kv_loaded[u], 16)

            pipelined(sp, step, T, 0, 2, 2)

        def kv_wait(eng, s, u):
            eng.wait_ge(kv_loaded[u], (s - u) * 24 + 48)


        @block.scalar
        def _(act):
            act.wait_ge(shift_made, 1)
            act.wait_ge(zeroed, 3)

            def prep(s, u):
                if later(s, 1):
                    pe_q.wait(act, s - 1, "q")
                x_t = acc[:, at(s), :].rearrange("p o (v g d) -> p g (o v) d", g=G, d=D)
                for c in range(2):
                    ins = nc.scalar.activation(q_tok[:, :, c, :].rearrange("p g (v d) -> p g v d", d=D), x_t,
                                               ACT.Identity, bias=shift[:, at(s)], scale=rstd[:, at(s)])
                act_q.mark(ins, "tokens")
                kv_wait(act, s, u)
                if later(s, 2):
                    pe_v.wait(act, s - 2, "v1")
                for c in range(2):
                    rows = slice(c * KS, (c + 1) * KS)
                    src = val_in[u][rows, :, :].rearrange("p b (v c d) -> p b v c d", c=2, d=D)[:, :, :, c, :]
                    ins = nc.scalar.copy(vals[u][rows, :, c:KV:2, 0:D], src)
                act_v.mark(ins, "vals")
                pe_q.wait(act, s, "q")
                if later(s, 2):
                    pe_t.wait(act, s - 2, "t1")
                act_q.mark(nc.scalar.copy(q_hi[u][:, :, :, :], ps_qb), "high")

            def attend(s):
                for b in range(2):
                    pe_t.wait(act, s, f"t{b}")
                    if later(s, 1):
                        pe_v.wait(act, s - 1, f"v{b}")
                    for h in range(2):
                        act_t.mark(nc.scalar.activation(probs[b][:, 2 * h:2 * h + 2, :], ps_t[:, 2 * h:2 * h + 2, :],
                                                        ACT.Exp, scale=SCALE), f"t{b}{'ab'[h]}")

            def router_a(s):
                pe_h.wait(act, s, "h_t")
                act_h.mark(nc.scalar.copy(h_t[:, :, :], ps_ht), "h_t")
                pe_h.wait(act, s, "logits")
                if later(s, 1):
                    dve_r.wait(act, s - 1, "w")
                act_h.mark(nc.scalar.copy(lg[:, :], ps_lg), "logits")
                act_h.wait(act, s, "logits")
                act_h.mark(nc.scalar.activation(eg[:, 0:I], lg[:, E:E + I], ACT.Exp, scale=-1.0), "gates")
                act_h.mark(nc.scalar.activation(eg[:, I:I + 1], lg[:, FS - 1:FS], ACT.Exp, scale=-1.0), "gate")
                dve_g.wait(act, s, "nlmax")
                act_h.mark(nc.scalar.activation(ex[:, :], lg[:, 0:E], ACT.Exp, bias=nlmax[:, 0:1],
                                                accum_out=esum[:, 0:1]), "exp")

            def router_b(s):
                pe_hid.wait(act, s, "hid")
                act_hid.mark(nc.scalar.copy(hid_t[:, :], ps_hid), "hid")

            def step(s, u):
                if live(s, 2, T):
                    router_a(s - 2)
                if live(s, 0, T):
                    prep(s, u)
                if live(s, 2, T):
                    router_b(s - 2)
                if live(s, 1, T):
                    attend(s - 1)

            pipelined(act, step, T, 2, 2, 4)

        @block.tensor
        def _(pe):
            def scores(s, u):
                act_q.wait(pe, s, "high")
                dve_q.wait(pe, s, "keys")
                for i in range(4):
                    b, g2 = i // 2, i % 2
                    if i >= 2:
                        dve_s.wait(pe, s, f"s{i - 2}")
                    elif later(s, 1):
                        dve_s.wait(pe, s - 1, f"s{i + 2}")
                    for part, q in ((0, q_hi[u]), (1, q_lo[u])):
                        mm = pe.matmul(ps_s[i % 2][:, :, :], q[:, b, 2 * g2:2 * g2 + 2, :],
                                       keys[u][:, b, :, :], start=part == 0, stop=part == 1)
                    pe_s.mark(mm, f"s{i}")

            def attend(s, u):
                dve_s.wait(pe, s, "copy")
                if later(s, 1):
                    dve_v.wait(pe, s - 1, "attn")
                    dve_p.wait(pe, s - 1, "slot")
                hold(pe, passed)
                pe_m.mark(pe.transpose(ps_max, negmax[:, :, :, :], ident[:, :]), "max")
                dve_s.wait(pe, s, "low")
                for b in range(2):
                    if b == 1:
                        act_t.wait(pe, s, "t0b")
                    elif later(s, 1):
                        act_t.wait(pe, s - 1, "t1b")
                    for j in range(4):
                        kj = keys[u][:, b, 2 * j:2 * j + 2, :]
                        o = ps_t[:, j, :]
                        pe.matmul(o, kj, q_hi[u][:, b, :, :], start=True, stop=False)
                        pe.matmul(o, kj, q_lo[u][:, b, :, :], start=False, stop=False)
                        for g2 in range(2):
                            c = (2 * b + g2) * KV + 2 * j
                            mm = pe.matmul(o[:, g2 * P:(g2 + 1) * P], pick[:, c:c + 2, :], negmax_t[:, :],
                                           start=False, stop=g2 == 1)
                    pe_t.mark(mm, f"t{b}")
                act_v.wait(pe, s, "vals")
                for b in range(2):
                    act_t.wait(pe, s, f"t{b}b")
                    for g2 in range(2):
                        for j in range(4):
                            mm = pe.matmul(ps_pv[:, 2 * b + g2, 2 * j:2 * j + 2, :],
                                           probs[b][:, j, g2 * P:(g2 + 1) * P], vals[u][:, b, 2 * j:2 * j + 2, :],
                                           start=True, stop=True)
                    pe_v.mark(mm, f"v{b}")

            def router_a(s, u):
                dve_v.wait(pe, s, "row")
                if later(s, 1):
                    act_hid.wait(pe, s - 1, "hid")
                    dve_sh.wait(pe, s - 1, "shared")
                for c in range(CH):
                    mm = pe.transpose(ps_ht[:, c, :], row[u][:, c * P:(c + 1) * P], ident[:, :])
                pe_h.mark(mm, "h_t")
                act_h.wait(pe, s, "h_t")
                for c in range(CH):
                    mm = pe.matmul(ps_lg, h_t[:, c, :], w_fs[:, c, :], start=c == 0, stop=c == CH - 1)
                pe_h.mark(mm, "logits")

            def router_b(s, u, last):
                dve_g.wait(pe, s, "hid")
                if not last:
                    dve_q.wait(pe, s + 2, "keys")
                hold(pe, passed)
                pe_hid.mark(pe.transpose(ps_hid, hid[:, :], ident[:, :]), "hid")
                dve_r.wait(pe, s, "picked")
                pe.matmul(ps_rank, before[:, :], picked[:, :], start=True, stop=False)
                pe_hid.mark(pe.matmul(ps_rank, ones[:, :], chosen[:, u, :], start=False, stop=True), "rank")
                act_hid.wait(pe, s, "hid")
                pe_hid.mark(pe.matmul(ps_sh, hid_t[:, :], w_sd[:, :], start=True, stop=True), "shared")

            def step(s, u):
                if live(s, 2, T):
                    router_a(s - 2, u)
                if live(s, 1, T):
                    scores(s - 1, 1 - u)
                if live(s, 0, T):
                    pe_q.mark(prep_key(s), "key")
                    prep_q(s)
                if live(s, 2, T):
                    router_b(s - 2, u, not live(s, 0, T))
                if live(s, 1, T):
                    attend(s - 1, 1 - u)

            def prep_key(s):
                if later(s, 1):
                    dve_q.wait(pe, s - 1, "keys")
                if later(s, 2):
                    act_h.wait(pe, s - 2, "h_t")
                dve_q.wait(pe, s, "key_low")
                return pe.transpose(ps_key, key_hl[:, :, :].bitcast(F32), ident[:, :])

            def prep_q(s):
                if later(s, 1):
                    dve_q.wait(pe, s - 1, "low")
                act_q.wait(pe, s, "tokens")
                for g in range(G):
                    mm = pe.transpose(ps_q[:, g, :], q_tok[:, g, :, :], ident[:, :])
                pe_q.mark(mm, "q")

            pipelined(pe, step, T, 2, 2, 4)

        @block.vector
        def _(dve):
            nc.vector.scalar_tensor_tensor(out=shift[:, :], in0=mean[:, :, 0], scalar=-1.0, in1=rstd[:, :],
                                           op0=ALU.mult, op1=ALU.mult).then_inc(shift_made, 1)

            def prep(s, u):
                kv_wait(dve, s, u)
                if later(s, 1):
                    pe_q.wait(dve, s - 1, "key")
                dve_q.mark(dve.tensor_copy(key_hl[:, 0, :], key_in[u][:, :]), "key_high")
                dve_q.wait(dve, s, "key_high")
                dve_q.mark(dve.tensor_tensor(key_hl[:, 1, :], key_in[u][:, :], key_hl[:, 0, :].bitcast(F32),
                                             ALU.subtract), "key_low")

            def prep_b(s, u):
                if later(s, 2):
                    pe_t.wait(dve, s - 2, "t1")
                act_q.wait(dve, s, "high")
                dve_q.mark(dve.tensor_tensor(q_lo[u][:, :, :, :], ps_qb, q_hi[u][:, :, :, :].bitcast(F32),
                                             ALU.subtract), "low")
                pe_q.wait(dve, s, "key")
                src = ps_key.rearrange("p (b o t) -> p b o t", b=2, o=1).broadcast_to([P, 2, KV, KS])
                msk = kvmask[:, :].rearrange("p (a v o) -> p a v o", a=1, o=1).broadcast_to([P, 2, KV, KS])
                dve_q.mark(dve.tensor_tensor(keys[u][:, :, :, :], src, msk, ALU.mult), "keys")

            def maxima(s):
                for i in range(4):
                    pe_s.wait(dve, s, f"s{i}")
                    if i == 0 and later(s, 1):
                        pe_m.wait(dve, s - 1, "max")
                    dve_s.mark(dve.tensor_reduce(negmax[:, 0, i, :], ps_s[i % 2][:, :, :], AX, ALU.max, negate=True),
                               f"s{i}")
                dve_s.wait(dve, s, "s3")
                dve_s.mark(dve.tensor_copy(negmax[:, 1, :, :], negmax[:, 0, :, :]), "copy")

            def spread_maxima(s):
                pe_m.wait(dve, s, "max")
                if later(s, 1):
                    pe_t.wait(dve, s - 1, "t1")
                dve_s.mark(dve.tensor_copy(negmax_t[:, :], ps_max), "high")
                dve_s.wait(dve, s, "high")
                dve_s.mark(dve.tensor_tensor(negmax_t[32:64, :], ps_max[32:64, :], negmax_t[32:64, :].bitcast(F32),
                                             ALU.subtract), "low")

            def attend(s, u):
                pe_v.wait(dve, s, "v1")
                dve_v.mark(dve.reciprocal(rden[:, :, :], ps_pv[:, :, :, D]), "recip")
                dve_v.wait(dve, s, "recip")
                for b in range(2):
                    for g in range(2):
                        rows = slice(g * S, (g + 1) * S)
                        o = attn[b * S:(b + 1) * S, :].rearrange("p (v h g d) -> p h v g d", h=2, g=2, d=D)[:, :, :, g, :]
                        r = rden[rows, 2 * b:2 * b + 2, :].rearrange("p h (v o) -> p h v o", o=1)
                        ins = dve.tensor_tensor(o, ps_pv[rows, 2 * b:2 * b + 2, :, 0:D],
                                                r.broadcast_to([S, 2, KV, D]), ALU.mult)
                dve_v.mark(ins, "attn")
                dve_v.wait(dve, s, "attn")
                x_t = acc[:, at(s), :].rearrange("p o c -> p (o c)")
                act_q.wait(dve, s, "tokens")
                dve_v.mark(dve.tensor_tensor(x_t, x_t, attn[:, :], ALU.add), "sum")
                dve_v.wait(dve, s, "sum")
                hold(dve, passed)
                dve_v.mark(dve.bn_stats(st[:, :], x_t), "stats")
                dve_v.wait(dve, s, "stats")
                hold(dve, passed)
                dve_v.mark(dve.bn_aggr(mv[:, :], st[:, :]), "mean")
                if later(s, 2):
                    dve.wait_ge(scattered[u], (s - u) * (8 * TOPK))
                dve_v.wait(dve, s, "mean")
                rsqrt(dve, dve_rs, s, rs2[:, :], mv[:, 1:2], rs_tmp[:, 0:1], rs_tmp[:, 1:2], rs_tmp[:, 2:3])
                dve_v.mark(dve.tensor_scalar(row[u][:, 0:C], x_t, mv[:, 0:1], rs2[:, 0:1], ALU.subtract, ALU.mult),
                           "row")

            def gates(s):
                act_h.wait(dve, s, "logits")
                act_h.wait(dve, s, "gate")
                dve_g.mark(dve.tensor_scalar(den[:, :], eg[:, :], 1.0, None, ALU.add), "den")
                dve_g.wait(dve, s, "den")
                dve_g.mark(dve.reciprocal(sig[:, :], den[:, :]), "sig")
                dve_g.wait(dve, s, "sig")
                dve_g.mark(dve.tensor_tensor(silu[:, :], lg[:, E:E + I], sig[:, 0:I], ALU.mult), "silu")
                dve_g.wait(dve, s, "silu")
                dve_g.mark(dve.tensor_tensor(hid[:, :], silu[:, :], lg[:, E + I:E + 2 * I], ALU.mult), "hid")
                dve_g.mark(dve.max(top[:, :], lg[:, 0:E]), "top")
                dve_g.wait(dve, s, "top")
                dve_g.mark(dve.tensor_scalar(nlmax[:, :], top[:, 0:1], -1.0, None, ALU.mult), "nlmax")

            def choose(s, u):
                act_h.wait(dve, s, "exp")
                hold(dve, passed)
                dve_r.mark(dve.max(top_e[:, :], ex[:, :]), "top_e")
                dve_r.wait(dve, s, "top_e")
                hold(dve, passed)
                dve_r.mark(dve.max_index(idx[:, :], top_e[:, :], ex[:, :]), "index")
                dve_r.wait(dve, s, "index")
                dve_r.mark(dve.tensor_copy(row[u][:, C:C + TOPK], idx[:, :]), "idx")
                dve_r.mark(dve.tensor_copy(row[u][:, C + TOPK:ROW], dest[:, at(s), :].rearrange("p o k -> p (o k)")),
                           "dest")
                dve_r.mark(dve.match_replace(marked[:, :], top_e[:, :], ex[:, :], -1.0), "marked")
                dve_r.wait(dve, s, "marked")
                if later(s, 1):
                    pe_hid.wait(dve, s - 1, "rank")
                dve_r.mark(dve.tensor_scalar(picked[:, :], marked[:, :], 0.0, None, ALU.is_lt), "picked")
                dve_r.wait(dve, s, "picked")
                dve_r.mark(dve.tensor_tensor(chosen[:, 1 - u, :], chosen[:, u, :], picked[:, :], ALU.add), "chosen")
                dve_r.mark(dve.reciprocal(rsum[:, :], esum[:, :]), "rsum")
                dve_r.wait(dve, s, "rsum")
                dve_r.mark(dve.tensor_scalar(top_p[:, :], top_e[:, :], rsum[:, 0:1], None, ALU.mult), "p")
                dve_r.wait(dve, s, "p")
                dve_r.mark(dve.tensor_reduce(psumk[:, :], top_p[:, :], AX, ALU.add), "psum")
                dve_r.wait(dve, s, "psum")
                dve_r.mark(dve.reciprocal(rpk[:, :], psumk[:, :]), "rpk")
                dve_r.wait(dve, s, "rpk")
                dve_r.mark(dve.tensor_scalar(weights[:, at(s), :].rearrange("p o k -> p (o k)"), top_p[:, :],
                                             rpk[:, 0:1], None, ALU.mult), "w")

            def places(s, u):
                pe_hid.wait(dve, s, "rank")
                dve_p.mark(dve.tensor_tensor(slot[:, :], ps_rank, list_base[:, :], ALU.add), "slot")
                dve_p.wait(dve, s, "slot")
                for j in range(TOPK):
                    ins = dve.scalar_tensor_tensor(out=junk[:, j, :], in0=iota_e[:, :],
                                                   scalar=row[u][:, C + j:C + j + 1], in1=slot[:, :],
                                                   op0=ALU.is_equal, op1=ALU.mult, accum_out=posf[:, j:j + 1])
                dve_p.mark(ins, "posf")
                dve_p.wait(dve, s, "posf")
                dve_p.mark(dve.tensor_copy(pos[u][:, :], posf[:, :]), "pos")

            def shared(s):
                pe_hid.wait(dve, s, "shared")
                x_t = acc[:, at(s), :].rearrange("p o c -> p (o c)")
                dve_sh.mark(dve.scalar_tensor_tensor(out=x_t, in0=ps_sh, scalar=sig[:, I:I + 1], in1=x_t,
                                                     op0=ALU.mult, op1=ALU.add), "shared")

            def step(s, u):
                if live(s, 0, T):
                    prep(s, u)
                if live(s, 2, T):
                    gates(s - 2)
                if live(s, 1, T):
                    maxima(s - 1)
                if live(s, 2, T):
                    choose(s - 2, u)
                if live(s, 0, T):
                    prep_b(s, u)
                if live(s, 2, T):
                    places(s - 2, u)
                if live(s, 1, T):
                    spread_maxima(s - 1)
                if live(s, 2, T):
                    shared(s - 2)
                if live(s, 1, T):
                    attend(s - 1, 1 - u)

            pipelined(dve, step, T, 2, 2, 4)

        @block.gpsimd
        def _(pool):
            for u in range(2):
                pool.memset(vals[u][:, :, :, :], 0.0).then_inc(zeroed, 1)
            pool.wait_ge(zeroed, 2)
            for u in range(2):
                for c in range(2):
                    ins = pool.memset(vals[u][c * KS:(c + 1) * KS, :, c:KV:2, D:D + 1], 1.0)
            ins.then_inc(zeroed, 1)

            def scatter(s, u):
                dve_p.wait(pool, s, "pos")
                hold(pool, passed)
                for j in range(TOPK):
                    pool.indirect_dma_start(
                        out=lists, out_offset=bass.IndirectOffsetOnAxis(ap=pos[u][:, j:j + 1], axis=0),
                        in_=row[u][:, :], in_offset=None).then_inc(scattered[u], 16)

            def step(s, u):
                scatter(s, u)

            pipelined(pool, step, T, 0, 2, 2)
            for u in range(2):
                pool.wait_ge(scattered[u], T // 2 * TOPK * 16)


def experts(nc, k, lists, results):
    w_gu, w_dn, ident, ones, chosen = k["w_gu"], k["w_dn"], k["ident"], k["ones"], k["chosen"]
    with ExitStack() as ctx:
        def sb(name, shape, dt=F32):
            return ctx.enter_context(nc.sbuf_tensor(f"experts_{name}", shape, dt))

        def sem(name):
            return ctx.enter_context(nc.semaphore(f"experts_{name}"))

        def psum(name, shape):
            return ctx.enter_context(nc.psum_tensor(f"experts_{name}", shape, F32))

        U = 4
        rows = [sb(f"rows{u}", [P, ROW]) for u in range(U)]
        rows_t = [sb(f"rows_t{u}", [P, CH, P]) for u in range(2)]
        silu = [sb(f"silu{u}", [P, I]) for u in range(2)]
        hid = [sb(f"hid{u}", [P, I]) for u in range(2)]
        hid_t = [sb(f"hid_t{u}", [I, P]) for u in range(2)]
        made = [sb(f"made{u}", [P, C]) for u in range(U)]
        junk = sb("junk", [P, U, TOPK])
        goes_f = sb("goes_f", [P, U])
        goes = [sb(f"goes{u}", [P, 1], I32) for u in range(U)]
        ps_t = [psum(f"ps_t{u}", [P, CH, P]) for u in range(2)]
        ps_gu = [psum(f"ps_gu{u}", [P, 2 * I]) for u in range(2)]
        ps_h = [psum(f"ps_h{u}", [I, P]) for u in range(2)]
        ps_o = [psum(f"ps_o{u}", [P, C]) for u in range(2)]

        tile_row = sb("tile_row", [1, TILES], I32)
        tile_exp = sb("tile_exp", [1, TILES], I32)
        tile_exp_f = sb("tile_exp_f", [P, TILES])
        steps16 = sb("steps16", [E, T])
        upto = sb("upto", [E, E], BF16)
        iota_j = sb("iota_j", [E, TILES])
        iota_j128 = sb("iota_j128", [1, TILES])
        list_start = sb("list_start", [E, 1])
        exp_id = sb("exp_id", [E, P])
        onesf = sb("onesf", [E, P])
        cnt = sb("cnt", [E, 1])
        fits = sb("fits", [E, T])
        tiles = sb("tiles", [E, 1])
        tiles_b = sb("tiles_b", [E, 1], BF16)
        ends = sb("ends", [E, 1])
        begins = sb("begins", [E, 1])
        ended = sb("ended", [E, TILES])
        own = sb("own", [E, TILES])
        where = sb("where", [E, 1])
        where2 = sb("where2", [E, 1])
        where_r = sb("where_r", [E, P])
        trow = sb("trow", [1, TILES])

        passed = sem("passed")
        const = sem("const")
        const_chain = sem("const_chain")
        pe_tab = Steps(sem("pe_tab"), "count", "ends", "row", "expert")
        dve_tab = Steps(sem("dve_tab"), "count", "fits", "tiles", "tiles_b", "ends", "begins", "ended", "own",
                        "where", "where2", "where_r", "exp_f", "exp", "trow", "row")
        loaded = [sem(f"loaded{u}") for u in range(U)]
        stored = [sem(f"stored{u}") for u in range(U)]
        pe_t = Steps(sem("pe_t"), "t")
        act_t = Steps(sem("act_t"), "t")
        pe_gu = Steps(sem("pe_gu"), "gu")
        act_s = Steps(sem("act_s"), "silu")
        dve_h = Steps(sem("dve_h"), "hid")
        pe_h = Steps(sem("pe_h"), "h")
        dve_t = Steps(sem("dve_t"), "h")
        pe_o = Steps(sem("pe_o"), "o")
        act_o = Steps(sem("act_o"), "o")
        dve_to = Steps(sem("dve_to"), "sum", "goes")
        block = ctx.enter_context(nc.Block())
        LAG = 3

        @block.gpsimd
        def _(pool):
            pool.iota(steps16[:, :], [[P, T]], base=0, channel_multiplier=0, allow_small_or_imprecise_dtypes=True)
            pool.iota(iota_j[:, :], [[1, TILES]], base=0, channel_multiplier=0, allow_small_or_imprecise_dtypes=True)
            pool.iota(iota_j128[:, :], [[P, TILES]], base=0, channel_multiplier=0,
                      allow_small_or_imprecise_dtypes=True)
            pool.iota(list_start[:, :], [[0, 1]], base=0, channel_multiplier=CAP, allow_small_or_imprecise_dtypes=True)
            pool.iota(exp_id[:, :], [[0, P]], base=0, channel_multiplier=1, allow_small_or_imprecise_dtypes=True)
            pool.memset(onesf[:, :], 1.0)
            pool.memset(upto[:, :], 1.0).then_inc(const_chain, 1)
            pool.wait_ge(const_chain, 1)
            pool.affine_select(out=upto[:, :], in_=upto[:, :], compare_op=ALU.is_ge, fill=0.0, base=0,
                               pattern=[[1, E]], channel_multiplier=-1).then_inc(const, 1)

            def step(s, u):
                dve_to.wait(pool, s, "goes")
                act_o.wait(pool, s, "o")
                hold(pool, passed)
                pool.indirect_dma_start(
                    out=results, out_offset=bass.IndirectOffsetOnAxis(ap=goes[u][:, 0:1], axis=0),
                    in_=made[u][:, :], in_offset=None, bounds_check=N * TOPK - 1, oob_is_err=False
                ).then_inc(stored[u], 16)

            pipelined(pool, step, TILES, 0, U, U)
            for u in range(U):
                pool.wait_ge(stored[u], TILES // U * 16)

        @block.sync
        def _(sp):
            dve_tab.wait(sp, 0, "row")

            def step(s, u):
                if later(s, U):
                    pe_t.wait(sp, s - U, "t")
                    hold(sp, passed)
                    dve_to.wait(sp, s - U, "sum")
                    hold(sp, passed)
                r = sp.value_load(tile_row[0:1, at(s)], min_val=0, max_val=E * CAP - P)
                sp.dma_start(rows[u][:, :], lists[bass.ds(r, P), :]).then_inc(loaded[u], 16)

            pipelined(sp, step, TILES, 0, U, U)

        @block.tensor
        def _(pe):
            pe_tab.mark(pe.matmul(ps_o[0][0:E, 0:1], chosen[:, 0, :], ones[:, 0:1], start=True, stop=True), "count")
            dve_tab.wait(pe, 0, "tiles_b")
            pe_tab.mark(pe.matmul(ps_o[0][0:E, 0:1], upto[:, :], tiles_b[:, :], start=True, stop=True), "ends")
            dve_tab.wait(pe, 0, "where_r")
            pe_tab.mark(pe.matmul(ps_o[0][:, 0:TILES], where_r[:, :], own[:, :], start=True, stop=True), "row")
            pe_tab.mark(pe.matmul(ps_o[1][:, 0:TILES], exp_id[:, :], own[:, :], start=True, stop=True), "expert")
            dve_tab.wait(pe, 0, "row")

            def step(s, u):
                if live(s, 0, TILES):
                    b = u % 2
                    pe.wait_ge(loaded[u], (s - u) * (16 // U) + 16)
                    if later(s, 2):
                        act_t.wait(pe, s - 2, "t")
                    for c in range(CH):
                        mm = pe.transpose(ps_t[b][:, c, :], rows[u][:, c * P:(c + 1) * P], ident[:, :])
                    pe_t.mark(mm, "t")
                if live(s, 1, TILES):
                    b = (u - 1) % 2
                    e = pe.value_load(tile_exp[0:1, at(s - 1)], min_val=0, max_val=E - 1)
                    act_t.wait(pe, s - 1, "t")
                    if later(s, 3):
                        dve_h.wait(pe, s - 3, "hid")
                    for c in range(CH):
                        mm = pe.matmul(ps_gu[b][:, :], rows_t[b][:, c, :],
                                       w_gu[:, bass.ds(e, 1), c, :].rearrange("p o f -> p (o f)"),
                                       start=c == 0, stop=c == CH - 1)
                    pe_gu.mark(mm, "gu")
                if live(s, 2, TILES):
                    b = u % 2
                    dve_h.wait(pe, s - 2, "hid")
                    if later(s, 4):
                        dve_t.wait(pe, s - 4, "h")
                    hold(pe, passed)
                    pe_h.mark(pe.transpose(ps_h[b][:, :], hid[b][:, :], ident[:, :]), "h")
                if live(s, 3, TILES):
                    b = (u - 1) % 2
                    e = pe.value_load(tile_exp[0:1, at(s - 3)], min_val=0, max_val=E - 1)
                    dve_t.wait(pe, s - 3, "h")
                    if later(s, 5):
                        act_o.wait(pe, s - 5, "o")
                    pe_o.mark(pe.matmul(ps_o[b][:, :], hid_t[b][:, :],
                                        w_dn[:, bass.ds(e, 1), :].rearrange("p o c -> p (o c)"),
                                        start=True, stop=True), "o")

            pipelined(pe, step, TILES, LAG, U, 2 * U)

        @block.scalar
        def _(act):
            def step(s, u):
                if live(s, 0, TILES):
                    b = u % 2
                    pe_t.wait(act, s, "t")
                    if later(s, 2):
                        pe_gu.wait(act, s - 2, "gu")
                    act_t.mark(nc.scalar.copy(rows_t[b][:, :, :], ps_t[b][:, :, :]), "t")
                if live(s, 1, TILES):
                    b = (u - 1) % 2
                    pe_gu.wait(act, s - 1, "gu")
                    if later(s, 3):
                        dve_h.wait(act, s - 3, "hid")
                    act_s.mark(nc.scalar.activation(silu[b][:, :], ps_gu[b][:, 0:I], ACT.Silu), "silu")
                if live(s, 3, TILES):
                    b, v = (u - 1) % 2, (u - 3) % U
                    pe_o.wait(act, s - 3, "o")
                    if later(s, 3 + U):
                        act.wait_ge(stored[v], (s - 3 - v) * (16 // U))
                    act_o.mark(nc.scalar.copy(made[v][:, :], ps_o[b][:, :]), "o")

            pipelined(act, step, TILES, LAG, U, 2 * U)

        @block.vector
        def _(dve):
            def mk(ins, name):
                dve_tab.mark(ins, name)
                dve_tab.wait(dve, 0, name)

            pe_tab.wait(dve, 0, "count")
            mk(dve.tensor_copy(cnt[:, :], ps_o[0][0:E, 0:1]), "count")
            dve.wait_ge(const, 1)
            mk(dve.tensor_scalar(fits[:, :], steps16[:, :], cnt[:, 0:1], None, ALU.is_lt), "fits")
            mk(dve.tensor_reduce(tiles[:, :], fits[:, :], AX, ALU.add), "tiles")
            mk(dve.tensor_copy(tiles_b[:, :], tiles[:, :]), "tiles_b")
            pe_tab.wait(dve, 0, "ends")
            mk(dve.tensor_copy(ends[:, :], ps_o[0][0:E, 0:1]), "ends")
            mk(dve.tensor_tensor(begins[:, :], ends[:, :], tiles[:, :], ALU.subtract), "begins")
            mk(dve.tensor_scalar(ended[:, :], iota_j[:, :], ends[:, 0:1], None, ALU.is_ge), "ended")
            mk(dve.scalar_tensor_tensor(out=own[:, :], in0=iota_j[:, :], scalar=begins[:, 0:1], in1=ended[:, :],
                                        op0=ALU.is_ge, op1=ALU.subtract), "own")
            mk(dve.tensor_tensor(where[:, :], list_start[:, :], cnt[:, :], ALU.add), "where")
            mk(dve.scalar_tensor_tensor(out=where2[:, :], in0=begins[:, :], scalar=float(P), in1=where[:, :],
                                        op0=ALU.mult, op1=ALU.add), "where2")
            mk(dve.tensor_scalar(where_r[:, :], onesf[:, :], where2[:, 0:1], None, ALU.mult), "where_r")
            pe_tab.wait(dve, 0, "expert")
            mk(dve.tensor_copy(tile_exp_f[:, :], ps_o[1][:, 0:TILES]), "exp_f")
            mk(dve.tensor_copy(tile_exp[:, :], tile_exp_f[0:1, :]), "exp")
            mk(dve.tensor_tensor(trow[:, :], ps_o[0][0:1, 0:TILES], iota_j128[:, :], ALU.subtract), "trow")
            mk(dve.tensor_scalar(tile_row[:, :], trow[:, :], 0.0, None, ALU.max), "row")

            def step(s, u):
                if live(s, 0, TILES):
                    dve.wait_ge(loaded[u], (s - u) * (16 // U) + 16)
                    dve_to.mark(dve.scalar_tensor_tensor(
                        out=junk[:, u, :], in0=rows[u][:, C:C + TOPK], scalar=tile_exp_f[:, at(s)],
                        in1=rows[u][:, C + TOPK:ROW], op0=ALU.is_equal, op1=ALU.mult,
                        accum_out=goes_f[:, u:u + 1]), "sum")
                    dve_to.wait(dve, s, "sum")
                    if later(s, U):
                        dve.wait_ge(stored[u], (s - u) * (16 // U))
                    dve_to.mark(dve.tensor_scalar(goes[u][:, :], goes_f[:, u:u + 1], BIG, None, ALU.add), "goes")
                if live(s, 1, TILES):
                    b = (u - 1) % 2
                    act_s.wait(dve, s - 1, "silu")
                    if later(s, 3):
                        pe_h.wait(dve, s - 3, "h")
                    dve_h.mark(dve.tensor_tensor(hid[b][:, :], silu[b][:, :], ps_gu[b][:, I:2 * I], ALU.mult), "hid")
                if live(s, 2, TILES):
                    b = u % 2
                    pe_h.wait(dve, s - 2, "h")
                    if later(s, 4):
                        pe_o.wait(dve, s - 4, "o")
                    dve_t.mark(dve.tensor_copy(hid_t[b][:, :], ps_h[b][:, :]), "h")

            pipelined(dve, step, TILES, LAG, U, 2 * U)


def combine(nc, k, results, out_tiles):
    acc, weights = k["acc"], k["weights"]
    with ExitStack() as ctx:
        def sem(name):
            return ctx.enter_context(nc.semaphore(f"combine_{name}"))

        U = 2
        got = [ctx.enter_context(nc.sbuf_tensor(f"got{u}", [P, TOPK, C], F32)) for u in range(U)]
        loaded = [sem(f"loaded{u}") for u in range(U)]
        passed = sem("passed")
        summed = Steps(sem("summed"), *[f"k{j}" for j in range(TOPK)])
        stored = sem("stored")
        block = ctx.enter_context(nc.Block())
        by_tile = results.rearrange("(n p k) c -> n p k c", p=P, k=TOPK)

        @block.sync
        def _(sp):
            def step(s, u):
                if later(s, U):
                    summed.wait(sp, s - U, f"k{TOPK - 1}")
                    hold(sp, passed)
                sp.dma_start(got[u][:, :, :], by_tile[at(s)].rearrange("n p k c -> (n p) k c")).then_inc(loaded[u], 16)

            pipelined(sp, step, T, 0, U, U)

        @block.vector
        def _(dve):
            def step(s, u):
                dve.wait_ge(loaded[u], (s - u) * (16 // U) + 16)
                x_t = acc[:, at(s), :].rearrange("p o c -> p (o c)")
                for j in range(TOPK):
                    summed.mark(dve.scalar_tensor_tensor(
                        out=x_t, in0=got[u][:, j, :], scalar=weights[:, at(s), j:j + 1].rearrange("p o k -> p (o k)"),
                        in1=x_t, op0=ALU.mult, op1=ALU.add), f"k{j}")
                    if j < TOPK - 1:
                        summed.wait(dve, s, f"k{j}")

            pipelined(dve, step, T, 0, U, U)

        @block.scalar
        def _(act):
            def step(s, u):
                summed.wait(act, s, f"k{TOPK - 1}")
                hold(act, passed)
                act.dma_start(out_tiles[:, at(s), :], acc[:, at(s), :]).then_inc(stored, 16)

            pipelined(act, step, T, 0, U, U)
            act.wait_ge(stored, T * 16)


_INS = ["x", "ctx_512", "L0_ffn_router_w", "L0_ffn_gate_up_proj", "L0_ffn_down_proj", "L0_ffn_shared_gate_w",
        "L0_ffn_shared_up_w", "L0_ffn_shared_down_w", "L0_ffn_shared_expert_gate_w"]


def kernel(**inputs):
    import numpy as np
    import concourse.bacc as bacc
    from concourse.bass_utils import run_bass_kernel_spmd

    nc = bacc.Bacc("TRN2", target_bir_lowering=False, num_devices=1)
    arrays, args = {}, []
    for name in _INS:
        a = np.ascontiguousarray(inputs[name])
        arrays[f"in_{name}"] = a
        args.append(nc.dram_tensor(f"in_{name}", a.shape, mybir.dt.from_np(a.dtype), kind="ExternalInput").ap())
    out = nc.dram_tensor("out", (B, S, C), F32, kind="ExternalOutput").ap()
    moe_block(nc, *args, out)
    done = run_bass_kernel_spmd(nc, [arrays], core_ids=[0])
    return done.results[0]["out"]
```

```python
from contextlib import ExitStack

import concourse.bass as bass
from concourse import mybir

F32 = mybir.dt.float32
F32R = mybir.dt.float32r
BF16 = mybir.dt.bfloat16
I32 = mybir.dt.int32
U32 = mybir.dt.uint32
ALU = mybir.AluOpType
ACT = mybir.ActivationFunctionType
AX = mybir.AxisListType.X

P = 128
B, S, C = 32, 64, 256
KS, KD = 64, 64
KV, G, D = 8, 4, 8
T = B * S // P
CH = C // P
E, I, TOPK = 64, 64, 8
N = B * S
EPS = 1e-5
SCALE = float(D) ** -0.5
CAP = P + N
ROW = C + 2 * TOPK
FS = 3 * I + 1
TILES = -(-((N * TOPK + E * (P - 1)) // P) // 8) * 8
BIG = float(1 << 20)
WCH = 4


class Steps:

    def __init__(self, sem, *names):
        self.sem, self.names = sem, names

    def up(self, name):
        assert name in self.names
        return self.sem, 1

    def past(self, rnd, name):
        return self.sem, rnd * len(self.names) + (self.names.index(name) + 1)


def pipelined(eng, step, rounds, lag, unroll, first, begin=None):
    assert first % unroll == 0 and (rounds - first) % unroll == 0

    def steps(s, count):
        if begin:
            begin(s)
        for u in range(count):
            step(s + u if u else s, u)

    for s in range(0, first, unroll):
        steps(s, unroll)
    with eng.Fori(first // unroll, rounds // unroll) as i:
        steps(i * unroll, unroll)
    for s in range(rounds, rounds + lag, unroll):
        steps(s, min(unroll, rounds + lag - s))


def hold(eng, passed):
    eng.sem_inc(passed, 1)


def live(s, lag, rounds):
    return not isinstance(s, int) or 0 <= s - lag < rounds


def later(s, n):
    return not isinstance(s, int) or s >= n


RSQRT = ["v", "guess"] + [f"n{i}{c}" for i in range(3) for c in "abc"]


def rsqrt(dve, steps, rnd, out, var, v, a, b):
    def do(ins, name):
        ins.then_inc(*steps.up(name))
        dve.wait_ge(*steps.past(rnd, name))

    do(dve.tensor_scalar(v, var, EPS, None, ALU.add), "v")
    do(dve.tensor_scalar(out.bitcast(I32), v.bitcast(I32), -0.5, float(0x5f3759df), ALU.mult, ALU.add), "guess")
    for i in range(3):
        do(dve.tensor_tensor(a, out, out, ALU.mult), f"n{i}a")
        do(dve.scalar_tensor_tensor(out=b, in0=a, scalar=-0.5, in1=v, op0=ALU.mult, op1=ALU.mult), f"n{i}b")
        do(dve.scalar_tensor_tensor(out=out, in0=b, scalar=1.5, in1=out, op0=ALU.add, op1=ALU.mult), f"n{i}c")


def at(i):
    return bass.ds(i, 1)


def moe_block(nc, x, ctx_, router_w, gate_up, down, sh_gate, sh_up, sh_down, sh_weight, out):
    lists = nc.dram_tensor("lists", [E * CAP, ROW], F32).ap()
    results = nc.dram_tensor("results", [N * TOPK, C], F32).ap()
    x_tiles = x.rearrange("(n b) s c -> (b s) n c", b=2)
    out_tiles = out.rearrange("(n b) s c -> (b s) n c", b=2)
    with ExitStack() as ctx:
        def sb(name, shape, dt=F32):
            return ctx.enter_context(nc.sbuf_tensor(name, shape, dt))

        keep = dict(
            w_gu=sb("w_gu", [P, E, CH, P]),
            w_dn=sb("w_dn", [I, E, C]),
            acc=sb("acc", [P, T, C]),
            w_fs=sb("w_fs", [P, CH, FS]),
            w_sd=sb("w_sd", [I, C]),
            mean=sb("mean", [P, T, 2]),
            rstd=sb("rstd", [P, T]),
            ident=sb("ident", [P, P]),
            kvmask=sb("kvmask", [P, KV]),
            pick=sb("pick", [64, 32, 64], F32R),
            before=sb("before", [P, P], BF16),
            ones=sb("ones", [P, P], BF16),
            iota_e=sb("iota_e", [P, E]),
            list_base=sb("list_base", [P, E]),
            dest=sb("dest", [P, T, TOPK]),
            weights=sb("weights", [P, T, TOPK]),
            esum=sb("esum", [P, T]),
            chosen=sb("chosen", [P, 2, E], BF16),
            filler=sb("filler", [P, ROW]),
        )
        prepare(nc, keep, lists, x_tiles, router_w, gate_up, down, sh_gate, sh_up, sh_down, sh_weight)
        route(nc, keep, lists, ctx_)
        experts(nc, keep, lists, results)
        combine(nc, keep, results, out_tiles)


def prepare(nc, k, lists, x_tiles, router_w, gate_up, down, sh_gate, sh_up, sh_down, sh_weight):
    w_gu, w_dn, acc, w_fs, w_sd = k["w_gu"], k["w_dn"], k["acc"], k["w_fs"], k["w_sd"]
    mean, rstd, ident, kvmask, pick = k["mean"], k["rstd"], k["ident"], k["kvmask"], k["pick"]
    before, ones, iota_e, list_base, dest = k["before"], k["ones"], k["iota_e"], k["list_base"], k["dest"]
    chunks = E // WCH
    with ExitStack() as ctx:
        def sb(name, shape, dt=F32):
            return ctx.enter_context(nc.sbuf_tensor(f"prepare_{name}", shape, dt))

        def sem(name):
            return ctx.enter_context(nc.semaphore(f"prepare_{name}"))

        U = 4
        gu_in = [sb(f"gu_in{u}", [P, WCH, C]) for u in range(U)]
        dn_in = [sb(f"dn_in{u}", [P, CH, WCH, I]) for u in range(U)]
        fs_in = sb("fs_in", [P, 2, C])
        sd_in = sb("sd_in", [P, CH, I])
        filler = k["filler"]
        stats = sb("stats", [P, T, 6])
        sel32 = sb("sel32", [64, 32])
        rs_tmp = sb("rs_tmp", [P, 3, T])
        ps_gu = [ctx.enter_context(nc.psum_tensor(f"prepare_ps_gu{u}", [P, 2, CH, P], F32)) for u in range(2)]
        ps_dn = [ctx.enter_context(nc.psum_tensor(f"prepare_ps_dn{u}", [I, 2, C], F32)) for u in range(2)]
        ps_fs = ctx.enter_context(nc.psum_tensor("prepare_ps_fs", [P, 2, FS], F32))
        ps_sd = ctx.enter_context(nc.psum_tensor("prepare_ps_sd", [I, C], F32))

        x_in = [sem(f"x_in{q}") for q in range(4)]
        fs_loaded = sem("fs_loaded")
        gu_loaded = [sem(f"gu_loaded{u}") for u in range(U)]
        passed = sem("passed")
        const = sem("const")
        const_chain = sem("const_chain")
        stats_done = sem("stats_done")
        dve_rs = Steps(sem("dve_rs"), *RSQRT)
        pe_chunk = Steps(sem("pe_chunk"), "gu0", "dn0", "gu1", "dn1")
        act_chunk = Steps(sem("act_chunk"), "gu0", "gu1")
        dve_chunk = Steps(sem("dve_chunk"), "dn0", "dn1")
        pe_fs = sem("pe_fs")
        dve_fs = sem("dve_fs")
        block = ctx.enter_context(nc.Block())
        gu_dram = gate_up.rearrange("(n e) f c -> n f e c", e=WCH)
        dn_dram = down.rearrange("(n e) (k p) i -> n k p e i", e=WCH, p=P)

        @block.sync
        def _(sp):
            sp.dma_start(fs_in[0:E, 0, :], router_w).then_inc(fs_loaded, 16)
            sp.dma_start(fs_in[E:P, 0, :], sh_gate).then_inc(fs_loaded, 16)
            sp.dma_start(fs_in[0:I, 1, :], sh_up).then_inc(fs_loaded, 16)
            sp.dma_start(fs_in[I:I + 1, 1, :], sh_weight).then_inc(fs_loaded, 16)
            sp.dma_start(sd_in[:, :, :], sh_down.rearrange("(k p) i -> p k i", p=P)).then_inc(fs_loaded, 16)

            def step(s, u):
                if later(s, U):
                    sp.wait_ge(*pe_chunk.past(s - U, "dn1"))
                    hold(sp, passed)
                sp.dma_start(gu_in[u][:, :, :], gu_dram[at(s)].rearrange("n f e c -> (n f) e c")
                             ).then_inc(gu_loaded[u], 16)
                for h in range(CH):
                    sp.dma_start(dn_in[u][:, h, :, :],
                                 dn_dram[at(s), h].rearrange("n p e i -> (n p) e i")).then_inc(gu_loaded[u], 16)

            pipelined(sp, step, chunks, 0, U, U)

        @block.scalar
        def _(act):
            for q in range(4):
                n = T // 4
                act.dma_start(acc[:, q * n:(q + 1) * n, :], x_tiles[:, q * n:(q + 1) * n, :]).then_inc(x_in[q], 16)

            def step(s, u):
                for h in range(2):
                    act.wait_ge(*pe_chunk.past(s, f"gu{h}"))
                    nc.scalar.copy(w_gu[:, bass.ds(s * WCH + 2 * h, 2), :, :], ps_gu[h][:, :, :, :]).then_inc(*act_chunk.up(f"gu{h}"))

            pipelined(act, step, chunks, 0, U, U)

        @block.tensor
        def _(pe):
            pe.wait_ge(const, 1)
            pe.wait_ge(fs_loaded, 80)
            for c in range(CH):
                cols = slice(c * P, (c + 1) * P)
                pe.transpose(ps_fs[:, c, 0:P], fs_in[:, 0, cols], ident[:, :])
                pe.transpose(ps_fs[:, c, P:FS], fs_in[0:I + 1, 1, cols], ident[0:I + 1, 0:I + 1])
                mm = pe.transpose(ps_sd[:, cols], sd_in[:, c, :], ident[:, :])
            mm.then_inc(pe_fs, 1)

            def step(s, u):
                pe.wait_ge(gu_loaded[u], (s - u) * (16 // U * (1 + CH)) + 16 * (1 + CH))
                for h in range(2):
                    if later(s, 1):
                        pe.wait_ge(*act_chunk.past(s - 1, f"gu{h}"))
                    for e in range(2):
                        for c in range(CH):
                            mm = pe.transpose(ps_gu[h][:, e, c, :], gu_in[u][:, 2 * h + e, c * P:(c + 1) * P],
                                              ident[:, :])
                    mm.then_inc(*pe_chunk.up(f"gu{h}"))
                    if later(s, 1):
                        pe.wait_ge(*dve_chunk.past(s - 1, f"dn{h}"))
                        hold(pe, passed)
                    for e in range(2):
                        for c in range(CH):
                            mm = pe.transpose(ps_dn[h][:, e, c * P:(c + 1) * P], dn_in[u][:, c, 2 * h + e, :],
                                              ident[:, :])
                    mm.then_inc(*pe_chunk.up(f"dn{h}"))

            pipelined(pe, step, chunks, 0, U, U)

        @block.vector
        def _(dve):
            dve.wait_ge(const, 2)
            dve.tensor_copy(pick[:, :, :], sel32[:, :].rearrange("p (c o) -> p c o", o=1).broadcast_to([64, 32, 64]))
            dve.wait_ge(pe_fs, 1)
            dve.tensor_copy(w_fs[:, :, :], ps_fs[:, :, :])
            dve.tensor_copy(w_sd[:, :], ps_sd[:, :]).then_inc(dve_fs, 1)

            def step(s, u):
                for h in range(2):
                    dve.wait_ge(*pe_chunk.past(s, f"dn{h}"))
                    dve.tensor_copy(w_dn[:, bass.ds(s * WCH + 2 * h, 2), :], ps_dn[h][:, :, :]).then_inc(*dve_chunk.up(f"dn{h}"))

            for t in range(T):
                if t % (T // 4) == 0:
                    dve.wait_ge(x_in[t // (T // 4)], 16)
                dve.bn_stats(stats[:, t, :], acc[:, t, :]).then_inc(stats_done, 1)
            dve.wait_ge(stats_done, T)
            for t in range(T):
                dve.bn_aggr(mean[:, t, :], stats[:, t, :]).then_inc(stats_done, 1)
            dve.wait_ge(stats_done, 2 * T)
            rsqrt(dve, dve_rs, 0, rstd[:, :], mean[:, :, 1], rs_tmp[:, 0, :], rs_tmp[:, 1, :], rs_tmp[:, 2, :])
            pipelined(dve, step, chunks, 0, U, U)

        @block.gpsimd
        def _(pool):
            made = [0]

            def link(ins):
                made[0] += 1
                ins.then_inc(const_chain, 1)
                pool.wait_ge(const_chain, made[0])

            link(pool.memset(ident[:, :], 0.0))
            pool.affine_select(out=ident[:, :], in_=ident[:, :], compare_op=ALU.not_equal, fill=1.0, base=0,
                               pattern=[[-1, P]], channel_multiplier=1).then_inc(const, 1)
            link(pool.memset(sel32[:, :], 0.0))
            link(pool.affine_select(out=sel32[:, :], in_=sel32[:, :], compare_op=ALU.not_equal, fill=1.0, base=0,
                                    pattern=[[-1, 32]], channel_multiplier=1))
            pool.affine_select(out=sel32[:, :], in_=sel32[:, :], compare_op=ALU.not_equal, fill=1.0, base=-32,
                               pattern=[[-1, 32]], channel_multiplier=1).then_inc(const, 1)
            link(pool.memset(filler[:, :], 0.0))
            pool.memset(filler[:, C:C + TOPK], -1.0)
            link(pool.memset(kvmask[:, :], 1.0))
            for h in range(2):
                m = kvmask[h * 64:(h + 1) * 64, :]
                link(pool.affine_select(out=m, in_=m, compare_op=ALU.is_ge, fill=0.0, base=0,
                                        pattern=[[-D, KV]], channel_multiplier=1))
                link(pool.affine_select(out=m, in_=m, compare_op=ALU.is_ge, fill=0.0, base=D - 1,
                                        pattern=[[D, KV]], channel_multiplier=-1))
            pool.memset(ones[:, :], 1.0)
            link(pool.memset(before[:, :], 1.0))
            pool.affine_select(out=before[:, :], in_=before[:, :], compare_op=ALU.is_ge, fill=0.0, base=-1,
                               pattern=[[1, P]], channel_multiplier=-1)
            pool.iota(iota_e[:, :], [[1, E]], base=0, channel_multiplier=0, allow_small_or_imprecise_dtypes=True)
            pool.iota(list_base[:, :], [[CAP, E]], base=P, channel_multiplier=0, allow_small_or_imprecise_dtypes=True)
            pool.iota(dest[:, :, :], [[P * TOPK, T], [1, TOPK]], base=-int(BIG), channel_multiplier=TOPK,
                      allow_small_or_imprecise_dtypes=True)
            pool.memset(k["chosen"][:, 0, :], 0.0)


def route(nc, k, lists, ctx_):
    acc, w_fs, w_sd, mean, rstd, ident = k["acc"], k["w_fs"], k["w_sd"], k["mean"], k["rstd"], k["ident"]
    kvmask, pick, before, ones = k["kvmask"], k["pick"], k["before"], k["ones"]
    iota_e, list_base, dest, weights, chosen = k["iota_e"], k["list_base"], k["dest"], k["weights"], k["chosen"]
    esum = k["esum"]
    with ExitStack() as ctx:
        def sb(name, shape, dt=F32):
            return ctx.enter_context(nc.sbuf_tensor(f"route_{name}", shape, dt))

        def sem(name):
            return ctx.enter_context(nc.semaphore(f"route_{name}"))

        def psum(name, shape):
            return ctx.enter_context(nc.psum_tensor(f"route_{name}", shape, F32))

        key_in = [sb(f"key_in{u}", [P, KD]) for u in range(2)]
        val_in = [sb(f"val_in{u}", [P, 2, KD]) for u in range(2)]
        key_hl = sb("key_hl", [P, 2, KD], F32R)
        key_t = [sb(f"key_t{u}", [P, P]) for u in range(2)]
        keys = [sb(f"keys{u}", [P, 2, KV, KS], F32R) for u in range(2)]
        vals = [sb(f"vals{u}", [P, 2, KV, D + 1]) for u in range(2)]
        q_tok = sb("q_tok", [P, G, 2, KD])
        q_hi = [sb(f"q_hi{u}", [P, 2, G, S], F32R) for u in range(2)]
        q_lo = [sb(f"q_lo{u}", [P, 2, G, S], F32R) for u in range(2)]
        negmax = sb("negmax", [P, 2, 4, KV])
        negmax_t = sb("negmax_t", [64, P], F32R)
        probs = [sb(f"probs{b}", [P, 4, G * S]) for b in range(2)]
        rden = sb("rden", [P, 4, KV])
        attn = sb("attn", [P, C])
        st = sb("st", [P, 6])
        mv = sb("mv", [P, 2])
        ln_v = sb("ln_v", [P, 1])
        rs2 = sb("rs2", [P, 1])
        newton = sb("newton", [P, 2])
        rs_new = sb("rs_new", [P, 1])
        shift2 = sb("shift2", [P, 1])
        eps = sb("eps", [P, 1])
        row = [sb(f"row{u}", [P, ROW]) for u in range(2)]
        h_t = sb("h_t", [P, CH, P])
        lg = sb("lg", [P, FS])
        nlmax = sb("nlmax", [P, 1])
        ex = sb("ex", [P, E])
        eg = sb("eg", [P, I + 1])
        den = sb("den", [P, I + 1])
        sig = sb("sig", [P, I + 1])
        silu = sb("silu", [P, I])
        hid = sb("hid", [P, I])
        hid_t = sb("hid_t", [I, P])
        top_e = sb("top_e", [P, TOPK])
        idx = sb("idx", [P, TOPK], U32)
        marked = sb("marked", [P, E])
        picked = sb("picked", [P, E], BF16)
        slot = sb("slot", [P, E])
        placed = sb("placed", [P, E])
        posf = sb("posf", [P, TOPK])
        pos = [sb(f"pos{u}", [P, TOPK], I32) for u in range(2)]

        ps_q = psum("ps_q", [P, G, P])
        ps_qb = ps_q[:, :, :].rearrange("p g (b s) -> p b g s", b=2)
        ps_s = [psum(f"ps_s{u}", [P, KV, KS]) for u in range(2)]
        ps_t = psum("ps_t", [P, 4, G * S])
        ps_v = psum("ps_v", [P, 512])
        ps_h = psum("ps_h", [P, 512])
        ps_l = psum("ps_l", [P, 512])
        ps_pv = ps_v[:, 0:4 * KV * (D + 1)].rearrange("p (a v d) -> p a v d", a=4, v=KV)
        ps_max = ps_v[0:64, 384:384 + P]
        ps_key = ps_h[:, 384:384 + P]
        ps_ht = ps_h[:, 0:C].rearrange("p (c t) -> p c t", c=CH)
        ps_hid = ps_h[0:I, C:C + P]
        ps_lg = ps_l[:, 0:FS]
        ps_rank = ps_l[:, 0:E]
        ps_sh = ps_l[:, 256:256 + C]

        shift = sb("shift", [P, T])
        passed = sem("passed")
        shift_made = sem("shift_made")
        zeroed = sem("zeroed")
        filled = sem("filled")
        kv_loaded = [sem(f"kv_loaded{u}") for u in range(2)]
        scattered = [sem(f"scattered{u}") for u in range(2)]
        act_l = Steps(sem("act_l"), "tokens")
        dve_l = Steps(sem("dve_l"), "high", "low")
        pe_q = Steps(sem("pe_q"), "key", "q")
        act_q = Steps(sem("act_q"), "key", "high")
        dve_q = Steps(sem("dve_q"), "low", "keys")
        act_v = Steps(sem("act_v"), "vals")
        pe_s = Steps(sem("pe_s"), "s0", "s1", "s2", "s3")
        dve_s = Steps(sem("dve_s"), "s0", "s1", "s2", "s3", "copy")
        pe_m = Steps(sem("pe_m"), "max")
        dve_m = Steps(sem("dve_m"), "high", "low")
        pe_t = Steps(sem("pe_t"), "t0", "t1")
        act_t = Steps(sem("act_t"), "t0a", "t0b", "t1a", "t1b")
        pe_v = Steps(sem("pe_v"), "v0", "v1")
        dve_v = Steps(sem("dve_v"), "recip", "attn", "sum", "stats", "mean")
        act_n = Steps(sem("act_n"), "ln", "rstd", "row")
        dve_n = Steps(sem("dve_n"), "a", "b", "rstd", "shift")
        pe_h = Steps(sem("pe_h"), "h_t", "logits")
        act_h = Steps(sem("act_h"), "h_t", "logits", "e_gates", "e_weight", "ln", "sig", "exp")
        dve_g = Steps(sem("dve_g"), "nlmax", "silu", "hid")
        dve_r = Steps(sem("dve_r"), "top_e", "marked", "index", "picked", "weights", "idx", "dest", "chosen")
        pe_hid = Steps(sem("pe_hid"), "hid", "rank", "shared")
        act_hid = Steps(sem("act_hid"), "hid")
        dve_sh = Steps(sem("dve_sh"), "shared")
        dve_p = Steps(sem("dve_p"), "slot", "placed", "posf", "pos")
        block = ctx.enter_context(nc.Block())
        ctx_keys = ctx_.rearrange("(n b) t d -> n (b t) d", b=2)
        ctx_vals = ctx_.rearrange("(n b) t d -> n t b d", b=2)

        @block.sync
        def _(sp):
            parts = lists.rearrange("(n e r) c -> n r e c", n=8, r=CAP)

            def step(s, u):
                if later(s, 2):
                    sp.wait_ge(*dve_l.past(s - 2, "low"))
                    hold(sp, passed)
                    sp.wait_ge(*act_v.past(s - 2, "vals"))
                    hold(sp, passed)
                sp.dma_start(key_in[u][:, :], ctx_keys[at(s)].rearrange("n p d -> (n p) d")).then_inc(kv_loaded[u], 16)
                for c in range(2):
                    sp.dma_start(val_in[u][c * KS:(c + 1) * KS, :, :],
                                 ctx_vals[at(s)].rearrange("n t b d -> (n t) b d")).then_inc(kv_loaded[u], 16)
                if isinstance(s, int):
                    sp.dma_start(parts[s, 0:P],
                                 k["filler"][:, :].rearrange("p (o c) -> p o c", o=1).broadcast_to([P, E // 8, ROW])
                                 ).then_inc(filled, 16)

            pipelined(sp, step, T, 0, 2, 8)
            sp.wait_ge(filled, 8 * 16)

        def kv_wait(eng, s, u):
            eng.wait_ge(kv_loaded[u], (s - u) * 24 + 48)

        LAG = 6

        @block.scalar
        def _(act):
            act.preload_act_table_set("natural_log_exp_and_others")
            act.wait_ge(shift_made, 2)
            act.wait_ge(zeroed, 3)

            def router_a(s):
                act.wait_ge(*pe_h.past(s, "h_t"))
                nc.scalar.copy(h_t[:, :, :], ps_ht).then_inc(*act_h.up("h_t"))
                act.wait_ge(*pe_h.past(s, "logits"))
                if later(s, 1):
                    act.wait_ge(*dve_r.past(s - 1, "chosen"))
                    act.wait_ge(*dve_sh.past(s - 1, "shared"))
                nc.scalar.copy(lg[:, :], ps_lg).then_inc(*act_h.up("logits"))
                act.wait_ge(*act_h.past(s, "logits"))
                nc.scalar.activation(eg[:, 0:I], lg[:, E:E + I], ACT.Exp, scale=-1.0).then_inc(*act_h.up("e_gates"))
                nc.scalar.activation(eg[:, I:I + 1], lg[:, FS - 1:FS], ACT.Exp, scale=-1.0).then_inc(*act_h.up("e_weight"))
                act.wait_ge(*act_h.past(s, "e_weight"))
                nc.scalar.activation(den[:, :], eg[:, :], ACT.Ln, bias=1.0).then_inc(*act_h.up("ln"))
                act.wait_ge(*act_h.past(s, "ln"))
                nc.scalar.activation(sig[:, :], den[:, :], ACT.Exp, scale=-1.0).then_inc(*act_h.up("sig"))

            def exps(s, b):
                act.wait_ge(*pe_t.past(s, f"t{b}"))
                if later(s, 1):
                    act.wait_ge(*pe_v.past(s - 1, f"v{b}"))
                for h in range(2):
                    nc.scalar.activation(probs[b][:, 2 * h:2 * h + 2, :], ps_t[:, 2 * h:2 * h + 2, :],
                                                    ACT.Exp, scale=SCALE).then_inc(*act_t.up(f"t{b}{'ab'[h]}"))

            def router_b(s, v):
                act.wait_ge(*dve_g.past(s, "nlmax"))
                nc.scalar.activation(ex[:, :], lg[:, 0:E], ACT.Exp, bias=nlmax[:, 0:1],
                                                accum_out=esum[:, at(s)]).then_inc(*act_h.up("exp"))

            def router_c(s):
                act.wait_ge(*pe_hid.past(s, "hid"))
                nc.scalar.copy(hid_t[:, :], ps_hid).then_inc(*act_hid.up("hid"))

            def prep_key(s, u):
                act.wait_ge(*pe_q.past(s, "key"))
                if later(s, 2):
                    act.wait_ge(*dve_q.past(s - 2, "keys"))
                nc.scalar.copy(key_t[u][:, :], ps_key).then_inc(*act_q.up("key"))

            def prep(s, u):
                act.wait_ge(*pe_q.past(s, "q"))
                if later(s, 2):
                    act.wait_ge(*pe_t.past(s - 2, "t1"))
                nc.scalar.copy(q_hi[u][:, :, :, :], ps_qb).then_inc(*act_q.up("high"))

            def norm(s, u):
                act.wait_ge(*dve_v.past(s, "mean"))
                nc.scalar.activation(ln_v[:, :], mv[:, 1:2], ACT.Ln, bias=eps[:, 0:1]).then_inc(*act_n.up("ln"))
                act.wait_ge(*act_n.past(s, "ln"))
                if later(s, 1):
                    act.wait_ge(*dve_n.past(s - 1, "shift"))
                nc.scalar.activation(rs2[:, :], ln_v[:, :], ACT.Exp, scale=-0.5).then_inc(*act_n.up("rstd"))
                act.wait_ge(*dve_n.past(s, "shift"))
                if later(s, 2):
                    act.wait_ge(scattered[u], (s - u) * (8 * TOPK))
                nc.scalar.activation(row[u][:, 0:C], acc[:, at(s), :].rearrange("p o c -> p (o c)"),
                                                ACT.Identity, bias=shift2[:, 0:1], scale=rs_new[:, 0:1]).then_inc(*act_n.up("row"))

            def load(s):
                if later(s, 1):
                    act.wait_ge(*pe_q.past(s - 1, "q"))
                x_t = acc[:, at(s), :].rearrange("p o (v g d) -> p g (o v) d", g=G, d=D)
                for c in range(2):
                    ins = nc.scalar.activation(q_tok[:, :, c, :].rearrange("p g (v d) -> p g v d", d=D), x_t,
                                               ACT.Identity, bias=shift[:, at(s)], scale=rstd[:, at(s)])
                ins.then_inc(*act_l.up("tokens"))

            def values(s, u):
                kv_wait(act, s, u)
                if later(s, 2):
                    act.wait_ge(*pe_v.past(s - 2, "v1"))
                for c in range(2):
                    rows = slice(c * KS, (c + 1) * KS)
                    src = val_in[u][rows, :, :].rearrange("p b (v c d) -> p b v c d", c=2, d=D)[:, :, :, c, :]
                    ins = nc.scalar.copy(vals[u][rows, :, c:KV:2, 0:D], src)
                ins.then_inc(*act_v.up("vals"))

            def step(s, u):
                v = 1 - u
                if live(s, 1, T):
                    prep_key(s - 1, v)
                if live(s, 5, T):
                    router_a(s - 5)
                if live(s, 3, T):
                    exps(s - 3, 0)
                if live(s, 5, T):
                    router_b(s - 5, v)
                if live(s, 3, T):
                    exps(s - 3, 1)
                if live(s, 5, T):
                    router_c(s - 5)
                if live(s, 1, T):
                    prep(s - 1, v)
                if live(s, 4, T):
                    norm(s - 4, u)
                if live(s, 0, T):
                    load(s)
                if live(s, 1, T):
                    values(s - 1, v)

            pipelined(act, step, T, LAG, 2, 8)

        @block.tensor
        def _(pe):
            def prep_key(s):
                if later(s, 5):
                    pe.wait_ge(*act_hid.past(s - 5, "hid"))
                elif later(s, 1):
                    pe.wait_ge(*act_q.past(s - 1, "key"))
                pe.wait_ge(*dve_l.past(s, "low"))
                pe.transpose(ps_key, key_hl[:, :, :].bitcast(F32), ident[:, :]).then_inc(*pe_q.up("key"))

            def maxima(s):
                pe.wait_ge(*dve_s.past(s, "copy"))
                if later(s, 1):
                    pe.wait_ge(*dve_v.past(s - 1, "attn"))
                hold(pe, passed)
                pe.transpose(ps_max, negmax[:, :, :, :], ident[:, :]).then_inc(*pe_m.up("max"))

            def prep_q(s):
                if later(s, 1):
                    pe.wait_ge(*dve_q.past(s - 1, "low"))
                pe.wait_ge(*act_l.past(s, "tokens"))
                for g in range(G):
                    mm = pe.transpose(ps_q[:, g, :], q_tok[:, g, :, :], ident[:, :])
                mm.then_inc(*pe_q.up("q"))

            def scores(s, u, i):
                if i == 0:
                    pe.wait_ge(*act_q.past(s, "high"))
                    pe.wait_ge(*dve_q.past(s, "keys"))
                b, g2 = i // 2, i % 2
                if i >= 2:
                    pe.wait_ge(*dve_s.past(s, f"s{i - 2}"))
                elif later(s, 1):
                    pe.wait_ge(*dve_s.past(s - 1, f"s{i + 2}"))
                for part, q in ((0, q_hi[u]), (1, q_lo[u])):
                    mm = pe.matmul(ps_s[i % 2][:, :, :], q[:, b, 2 * g2:2 * g2 + 2, :],
                                   keys[u][:, b, :, :], start=part == 0, stop=part == 1)
                mm.then_inc(*pe_s.up(f"s{i}"))

            def attend(s, u, b):
                if b == 0:
                    pe.wait_ge(*dve_m.past(s, "low"))
                if b == 1:
                    pe.wait_ge(*act_t.past(s, "t0b"))
                elif later(s, 1):
                    pe.wait_ge(*act_t.past(s - 1, "t1b"))
                for j in range(4):
                    kj = keys[u][:, b, 2 * j:2 * j + 2, :]
                    o = ps_t[:, j, :]
                    pe.matmul(o, kj, q_hi[u][:, b, :, :], start=True, stop=False)
                    pe.matmul(o, kj, q_lo[u][:, b, :, :], start=False, stop=False)
                    for g2 in range(2):
                        c = (2 * b + g2) * KV + 2 * j
                        mm = pe.matmul(o[:, g2 * P:(g2 + 1) * P], pick[:, c:c + 2, :], negmax_t[:, :],
                                       start=False, stop=g2 == 1)
                mm.then_inc(*pe_t.up(f"t{b}"))

            def weigh(s, u, b):
                if b == 0:
                    pe.wait_ge(*act_v.past(s, "vals"))
                pe.wait_ge(*act_t.past(s, f"t{b}b"))
                for g2 in range(2):
                    for j in range(4):
                        mm = pe.matmul(ps_pv[:, 2 * b + g2, 2 * j:2 * j + 2, :],
                                       probs[b][:, j, g2 * P:(g2 + 1) * P], vals[u][:, b, 2 * j:2 * j + 2, :],
                                       start=True, stop=True)
                mm.then_inc(*pe_v.up(f"v{b}"))

            def router_a(s, u):
                pe.wait_ge(*act_n.past(s, "row"))
                if later(s, 1):
                    pe.wait_ge(*act_hid.past(s - 1, "hid"))
                if live(s, -4, T):
                    pe.wait_ge(*act_q.past(s + 4, "key"))
                for c in range(CH):
                    mm = pe.transpose(ps_ht[:, c, :], row[u][:, c * P:(c + 1) * P], ident[:, :])
                mm.then_inc(*pe_h.up("h_t"))

            def router_b(s, u):
                pe.wait_ge(*act_h.past(s, "h_t"))
                if later(s, 1):
                    pe.wait_ge(*dve_p.past(s - 1, "slot"))
                    pe.wait_ge(*dve_sh.past(s - 1, "shared"))
                for c in range(CH):
                    mm = pe.matmul(ps_lg, h_t[:, c, :], w_fs[:, c, :], start=c == 0, stop=c == CH - 1)
                mm.then_inc(*pe_h.up("logits"))

            def router_c(s):
                pe.wait_ge(*dve_g.past(s, "hid"))
                hold(pe, passed)
                pe.transpose(ps_hid, hid[:, :], ident[:, :]).then_inc(*pe_hid.up("hid"))

            def router_d(s, u):
                pe.wait_ge(*dve_r.past(s, "picked"))
                pe.wait_ge(*act_h.past(s, "logits"))
                pe.matmul(ps_rank, before[:, :], picked[:, :], start=True, stop=False)
                pe.matmul(ps_rank, ones[:, :], chosen[:, u, :], start=False, stop=True).then_inc(*pe_hid.up("rank"))
                pe.wait_ge(*act_hid.past(s, "hid"))
                pe.matmul(ps_sh, hid_t[:, :], w_sd[:, :], start=True, stop=True).then_inc(*pe_hid.up("shared"))

            def step(s, u):
                v = 1 - u
                if live(s, 1, T):
                    prep_key(s - 1)
                    prep_q(s - 1)
                if live(s, 2, T):
                    scores(s - 2, u, 0)
                if live(s, 3, T):
                    maxima(s - 3)
                if live(s, 5, T):
                    router_a(s - 5, v)
                if live(s, 2, T):
                    scores(s - 2, u, 1)
                if live(s, 5, T):
                    router_b(s - 5, v)
                if live(s, 3, T):
                    attend(s - 3, v, 0)
                if live(s, 2, T):
                    scores(s - 2, u, 2)
                if live(s, 3, T):
                    attend(s - 3, v, 1)
                if live(s, 2, T):
                    scores(s - 2, u, 3)
                if live(s, 5, T):
                    router_c(s - 5)
                if live(s, 3, T):
                    weigh(s - 3, v, 0)
                    weigh(s - 3, v, 1)
                if live(s, 5, T):
                    router_d(s - 5, v)

            pipelined(pe, step, T, LAG, 2, 8)

        @block.vector
        def _(dve):
            dve.memset(eps[:, :], EPS).then_inc(shift_made, 1)
            nc.vector.scalar_tensor_tensor(out=shift[:, :], in0=mean[:, :, 0], scalar=-1.0, in1=rstd[:, :],
                                           op0=ALU.mult, op1=ALU.mult).then_inc(shift_made, 1)

            def load(s, u):
                kv_wait(dve, s, u)
                if later(s, 1):
                    dve.wait_ge(*pe_q.past(s - 1, "key"))
                dve.tensor_copy(key_hl[:, 0, :], key_in[u][:, :]).then_inc(*dve_l.up("high"))
                dve.wait_ge(*dve_l.past(s, "high"))
                dve.tensor_tensor(key_hl[:, 1, :], key_in[u][:, :], key_hl[:, 0, :].bitcast(F32),
                                             ALU.subtract).then_inc(*dve_l.up("low"))

            def prep(s, u):
                if later(s, 2):
                    dve.wait_ge(*pe_t.past(s - 2, "t1"))
                dve.wait_ge(*act_q.past(s, "high"))
                dve.tensor_tensor(q_lo[u][:, :, :, :], ps_qb, q_hi[u][:, :, :, :].bitcast(F32),
                                             ALU.subtract).then_inc(*dve_q.up("low"))
                dve.wait_ge(*act_q.past(s, "key"))
                src = key_t[u][:, :].rearrange("p (b o t) -> p b o t", b=2, o=1).broadcast_to([P, 2, KV, KS])
                msk = kvmask[:, :].rearrange("p (a v o) -> p a v o", a=1, o=1).broadcast_to([P, 2, KV, KS])
                dve.tensor_tensor(keys[u][:, :, :, :], src, msk, ALU.mult).then_inc(*dve_q.up("keys"))

            def maximum(s, i):
                dve.wait_ge(*pe_s.past(s, f"s{i}"))
                if i == 0 and later(s, 1):
                    dve.wait_ge(*pe_m.past(s - 1, "max"))
                dve.tensor_reduce(negmax[:, 0, i, :], ps_s[i % 2][:, :, :], AX, ALU.max, negate=True).then_inc(*dve_s.up(f"s{i}"))

            def maxima_copy(s):
                dve.wait_ge(*dve_s.past(s, "s3"))
                dve.tensor_copy(negmax[:, 1, :, :], negmax[:, 0, :, :]).then_inc(*dve_s.up("copy"))

            def maxima_split(s):
                dve.wait_ge(*pe_m.past(s, "max"))
                if later(s, 1):
                    dve.wait_ge(*pe_t.past(s - 1, "t1"))
                dve.tensor_copy(negmax_t[:, :], ps_max).then_inc(*dve_m.up("high"))
                dve.wait_ge(*dve_m.past(s, "high"))
                dve.tensor_tensor(negmax_t[32:64, :], ps_max[32:64, :], negmax_t[32:64, :].bitcast(F32),
                                             ALU.subtract).then_inc(*dve_m.up("low"))

            def divide(s):
                dve.wait_ge(*pe_v.past(s, "v1"))
                dve.reciprocal(rden[:, :, :], ps_pv[:, :, :, D]).then_inc(*dve_v.up("recip"))
                dve.wait_ge(*dve_v.past(s, "recip"))
                for b in range(2):
                    for g in range(2):
                        rows = slice(g * S, (g + 1) * S)
                        o = attn[b * S:(b + 1) * S, :].rearrange("p (v h g d) -> p h v g d", h=2, g=2, d=D)[:, :, :, g, :]
                        r = rden[rows, 2 * b:2 * b + 2, :].rearrange("p h (v o) -> p h v o", o=1)
                        ins = dve.tensor_tensor(o, ps_pv[rows, 2 * b:2 * b + 2, :, 0:D],
                                                r.broadcast_to([S, 2, KV, D]), ALU.mult)
                ins.then_inc(*dve_v.up("attn"))

            def residual(s):
                x_t = acc[:, at(s), :].rearrange("p o c -> p (o c)")
                dve.wait_ge(*act_l.past(s, "tokens"))
                dve.wait_ge(*dve_v.past(s, "attn"))
                dve.tensor_tensor(x_t, x_t, attn[:, :], ALU.add).then_inc(*dve_v.up("sum"))

            def norm(s, part):
                x_t = acc[:, at(s), :].rearrange("p o c -> p (o c)")
                if part == 0:
                    dve.wait_ge(*dve_v.past(s, "sum"))
                    hold(dve, passed)
                    dve.bn_stats(st[:, :], x_t).then_inc(*dve_v.up("stats"))
                elif part == 1:
                    dve.wait_ge(*dve_v.past(s, "stats"))
                    if later(s, 1):
                        dve.wait_ge(*act_n.past(s - 1, "rstd"))
                    hold(dve, passed)
                    dve.bn_aggr(mv[:, :], st[:, :]).then_inc(*dve_v.up("mean"))
                else:
                    dve.wait_ge(*act_n.past(s, "rstd"))
                    if later(s, 1):
                        dve.wait_ge(*act_n.past(s - 1, "row"))
                    na, nb = newton[:, 0:1], newton[:, 1:2]
                    dve.scalar_tensor_tensor(out=na, in0=mv[:, 1:2], scalar=EPS, in1=rs2[:, :],
                                                        op0=ALU.add, op1=ALU.mult).then_inc(*dve_n.up("a"))
                    dve.wait_ge(*dve_n.past(s, "a"))
                    dve.scalar_tensor_tensor(out=nb, in0=na, scalar=-0.5, in1=rs2[:, :],
                                                        op0=ALU.mult, op1=ALU.mult).then_inc(*dve_n.up("b"))
                    dve.wait_ge(*dve_n.past(s, "b"))
                    dve.scalar_tensor_tensor(out=rs_new[:, :], in0=nb, scalar=1.5, in1=rs2[:, :],
                                                        op0=ALU.add, op1=ALU.mult).then_inc(*dve_n.up("rstd"))
                    dve.wait_ge(*dve_n.past(s, "rstd"))
                    dve.scalar_tensor_tensor(out=shift2[:, :], in0=mv[:, 0:1], scalar=-1.0, in1=rs_new[:, :],
                                                        op0=ALU.mult, op1=ALU.mult).then_inc(*dve_n.up("shift"))

            def gates(s):
                dve.wait_ge(*act_h.past(s, "logits"))
                dve.tensor_reduce(nlmax[:, :], lg[:, 0:E], AX, ALU.max, negate=True).then_inc(*dve_g.up("nlmax"))
                dve.wait_ge(*act_h.past(s, "sig"))
                dve.tensor_tensor(silu[:, :], lg[:, E:E + I], sig[:, 0:I], ALU.mult).then_inc(*dve_g.up("silu"))

            def hidden(s):
                dve.wait_ge(*dve_g.past(s, "silu"))
                dve.tensor_tensor(hid[:, :], silu[:, :], lg[:, E + I:E + 2 * I], ALU.mult).then_inc(*dve_g.up("hid"))

            def choose(s, u):
                dve.wait_ge(*act_h.past(s, "exp"))
                hold(dve, passed)
                dve.max(top_e[:, :], ex[:, :]).then_inc(*dve_r.up("top_e"))
                dve.wait_ge(*dve_r.past(s, "top_e"))
                hold(dve, passed)
                dve.match_replace(marked[:, :], top_e[:, :], ex[:, :], -1.0).then_inc(*dve_r.up("marked"))
                dve.max_index(idx[:, :], top_e[:, :], ex[:, :]).then_inc(*dve_r.up("index"))
                dve.wait_ge(*dve_r.past(s, "marked"))
                if later(s, 1):
                    dve.wait_ge(*pe_hid.past(s - 1, "rank"))
                dve.tensor_scalar(picked[:, :], marked[:, :], 0.0, None, ALU.is_lt).then_inc(*dve_r.up("picked"))
                dve.tensor_copy(weights[:, at(s), :].rearrange("p o k -> p (o k)"), top_e[:, :]).then_inc(*dve_r.up("weights"))
                dve.wait_ge(*dve_r.past(s, "index"))
                dve.tensor_copy(row[u][:, C:C + TOPK], idx[:, :]).then_inc(*dve_r.up("idx"))
                dve.tensor_copy(row[u][:, C + TOPK:ROW], dest[:, at(s), :].rearrange("p o k -> p (o k)")).then_inc(*dve_r.up("dest"))
                dve.wait_ge(*dve_r.past(s, "picked"))
                dve.tensor_tensor(chosen[:, 1 - u, :], chosen[:, u, :], picked[:, :], ALU.add).then_inc(*dve_r.up("chosen"))

            def places(s, u):
                dve.wait_ge(*pe_hid.past(s, "shared"))
                dve.tensor_tensor(slot[:, :], ps_rank, list_base[:, :], ALU.add).then_inc(*dve_p.up("slot"))
                dve.wait_ge(*dve_p.past(s, "slot"))
                dve.tensor_tensor(placed[:, :], slot[:, :], picked[:, :], ALU.mult).then_inc(*dve_p.up("placed"))
                dve.wait_ge(*dve_p.past(s, "placed"))
                hold(dve, passed)
                dve.max(posf[:, :], placed[:, :]).then_inc(*dve_p.up("posf"))
                dve.wait_ge(*dve_p.past(s, "posf"))
                if later(s, 2):
                    dve.wait_ge(scattered[u], (s - u) * (8 * TOPK))
                dve.tensor_copy(pos[u][:, :], posf[:, :]).then_inc(*dve_p.up("pos"))

            def shared(s):
                dve.wait_ge(*pe_hid.past(s, "shared"))
                x_t = acc[:, at(s), :].rearrange("p o c -> p (o c)")
                dve.scalar_tensor_tensor(out=x_t, in0=ps_sh, scalar=sig[:, I:I + 1], in1=x_t,
                                                     op0=ALU.mult, op1=ALU.add).then_inc(*dve_sh.up("shared"))

            def step(s, u):
                v = 1 - u
                if live(s, 6, T):
                    shared(s - 6)
                if live(s, 4, T):
                    divide(s - 4)
                if live(s, 3, T):
                    maxima_split(s - 3)
                if live(s, 2, T):
                    maximum(s - 2, 0)
                if live(s, 4, T):
                    residual(s - 4)
                if live(s, 2, T):
                    maximum(s - 2, 1)
                if live(s, 4, T):
                    norm(s - 4, 0)
                if live(s, 5, T):
                    gates(s - 5)
                if live(s, 2, T):
                    maximum(s - 2, 2)
                if live(s, 4, T):
                    norm(s - 4, 1)
                if live(s, 5, T):
                    hidden(s - 5)
                if live(s, 2, T):
                    maximum(s - 2, 3)
                if live(s, 5, T):
                    choose(s - 5, v)
                if live(s, 2, T):
                    maxima_copy(s - 2)
                if live(s, 1, T):
                    prep(s - 1, v)
                if live(s, 4, T):
                    norm(s - 4, 2)
                if live(s, 5, T):
                    places(s - 5, v)
                if live(s, 0, T):
                    load(s, u)

            pipelined(dve, step, T, LAG, 2, 8)

        @block.gpsimd
        def _(pool):
            for u in range(2):
                pool.memset(vals[u][:, :, :, :], 0.0).then_inc(zeroed, 1)
            pool.wait_ge(zeroed, 2)
            for u in range(2):
                for c in range(2):
                    ins = pool.memset(vals[u][c * KS:(c + 1) * KS, :, c:KV:2, D:D + 1], 1.0)
            ins.then_inc(zeroed, 1)

            def step(s, u):
                pool.wait_ge(*dve_p.past(s, "pos"))
                hold(pool, passed)
                for j in range(TOPK):
                    pool.indirect_dma_start(
                        out=lists, out_offset=bass.IndirectOffsetOnAxis(ap=pos[u][:, j:j + 1], axis=0),
                        in_=row[u][:, :], in_offset=None).then_inc(scattered[u], 16)

            pipelined(pool, step, T, 0, 2, 2)
            for u in range(2):
                pool.wait_ge(scattered[u], T // 2 * TOPK * 16)


def experts(nc, k, lists, results):
    w_gu, w_dn, ident, ones, chosen = k["w_gu"], k["w_dn"], k["ident"], k["ones"], k["chosen"]
    with ExitStack() as ctx:
        def sb(name, shape, dt=F32):
            return ctx.enter_context(nc.sbuf_tensor(f"experts_{name}", shape, dt))

        def sem(name):
            return ctx.enter_context(nc.semaphore(f"experts_{name}"))

        def psum(name, shape):
            return ctx.enter_context(nc.psum_tensor(f"experts_{name}", shape, F32))

        U = 8
        LAG = 4
        rows = [sb(f"rows{u}", [P, ROW]) for u in range(U)]
        rows_t = [sb(f"rows_t{u}", [P, CH, P]) for u in range(2)]
        silu = [sb(f"silu{u}", [P, I]) for u in range(2)]
        hid = [sb(f"hid{u}", [P, I]) for u in range(2)]
        hid_t = [sb(f"hid_t{u}", [I, P]) for u in range(2)]
        made = [sb(f"made{u}", [P, C]) for u in range(U)]
        junk = sb("junk", [P, U, TOPK])
        goes_f = sb("goes_f", [P, U])
        goes = [sb(f"goes{u}", [P, 1], I32) for u in range(U)]
        ps_t = [psum(f"ps_t{u}", [P, CH, P]) for u in range(2)]
        ps_gu = [psum(f"ps_gu{u}", [P, 2 * I]) for u in range(2)]
        ps_h = [psum(f"ps_h{u}", [I, P]) for u in range(2)]
        ps_o = [psum(f"ps_o{u}", [P, C]) for u in range(2)]

        tile_row = sb("tile_row", [1, TILES], I32)
        tile_exp = sb("tile_exp", [1, TILES + 2 * U], I32)
        tile_exp_f = sb("tile_exp_f", [P, TILES])
        steps16 = sb("steps16", [E, T])
        upto = sb("upto", [E, E], BF16)
        iota_j = sb("iota_j", [E, TILES])
        iota_j128 = sb("iota_j128", [1, TILES])
        list_start = sb("list_start", [E, 1])
        exp_id = sb("exp_id", [E, P])
        onesf = sb("onesf", [E, P])
        cnt = sb("cnt", [E, 1])
        fits = sb("fits", [E, T])
        tiles = sb("tiles", [E, 1])
        tiles_b = sb("tiles_b", [E, 1], BF16)
        ends = sb("ends", [E, 1])
        begins = sb("begins", [E, 1])
        ended = sb("ended", [E, TILES])
        own = sb("own", [E, TILES])
        where = sb("where", [E, 1])
        where2 = sb("where2", [E, 1])
        where_r = sb("where_r", [E, P])
        trow = sb("trow", [1, TILES])

        passed = sem("passed")
        const = sem("const")
        const_chain = sem("const_chain")
        pe_tab = Steps(sem("pe_tab"), "count", "ends", "row", "expert")
        dve_tab = Steps(sem("dve_tab"), "count", "fits", "tiles", "tiles_b", "ends", "begins", "ended", "own",
                        "where", "where2", "where_r", "exp_f", "exp", "trow", "row", "recip", "probs", "total",
                        "recip2", "weights")
        loaded = [sem(f"loaded{u}") for u in range(U)]
        stored = [sem(f"stored{u}") for u in range(U)]
        pe_t = Steps(sem("pe_t"), "t")
        act_t = Steps(sem("act_t"), "t")
        pe_gu = Steps(sem("pe_gu"), "gu")
        act_s = Steps(sem("act_s"), "silu")
        dve_h = Steps(sem("dve_h"), "hid")
        pe_h = Steps(sem("pe_h"), "h")
        dve_t = Steps(sem("dve_t"), "h")
        pe_o = Steps(sem("pe_o"), "o")
        act_o = Steps(sem("act_o"), "o")
        dve_to = Steps(sem("dve_to"), "sum", "goes")
        block = ctx.enter_context(nc.Block())

        @block.gpsimd
        def _(pool):
            pool.iota(steps16[:, :], [[P, T]], base=0, channel_multiplier=0, allow_small_or_imprecise_dtypes=True)
            pool.iota(iota_j[:, :], [[1, TILES]], base=0, channel_multiplier=0, allow_small_or_imprecise_dtypes=True)
            pool.iota(iota_j128[:, :], [[P, TILES]], base=0, channel_multiplier=0,
                      allow_small_or_imprecise_dtypes=True)
            pool.iota(list_start[:, :], [[0, 1]], base=0, channel_multiplier=CAP, allow_small_or_imprecise_dtypes=True)
            pool.iota(exp_id[:, :], [[0, P]], base=0, channel_multiplier=1, allow_small_or_imprecise_dtypes=True)
            pool.memset(onesf[:, :], 1.0)
            pool.memset(tile_exp[:, :], 0)
            pool.memset(upto[:, :], 1.0).then_inc(const_chain, 1)
            pool.wait_ge(const_chain, 1)
            pool.affine_select(out=upto[:, :], in_=upto[:, :], compare_op=ALU.is_ge, fill=0.0, base=0,
                               pattern=[[1, E]], channel_multiplier=-1).then_inc(const, 1)

            def step(s, u):
                pool.wait_ge(*dve_to.past(s, "goes"))
                pool.wait_ge(*act_o.past(s, "o"))
                hold(pool, passed)
                pool.indirect_dma_start(
                    out=results, out_offset=bass.IndirectOffsetOnAxis(ap=goes[u][:, 0:1], axis=0),
                    in_=made[u][:, :], in_offset=None, bounds_check=N * TOPK - 1, oob_is_err=False
                ).then_inc(stored[u], 16)

            pipelined(pool, step, TILES, 0, U, U)
            for u in range(U):
                pool.wait_ge(stored[u], TILES // U * 16)

        @block.sync
        def _(sp):
            sp.wait_ge(*dve_tab.past(0, "row"))

            def step(s, u):
                if later(s, U):
                    sp.wait_ge(*pe_t.past(s - U, "t"))
                    hold(sp, passed)
                    sp.wait_ge(*dve_to.past(s - U, "sum"))
                    hold(sp, passed)
                r = sp.snap(row_regs[u], min_val=0, max_val=E * CAP - P)
                sp.dma_start(rows[u][:, :], lists[bass.ds(r, P), :]).then_inc(loaded[u], 16)

            row_regs = [sp.alloc_register(f"row_reg{u}") for u in range(U)]

            def begin(s):
                sp.load(row_regs, tile_row[0:1, bass.ds(s, U)])

            pipelined(sp, step, TILES, 0, U, U, begin)

        @block.tensor
        def _(pe):
            pe.matmul(ps_o[0][0:E, 0:1], chosen[:, 0, :], ones[:, 0:1], start=True, stop=True).then_inc(*pe_tab.up("count"))
            pe.wait_ge(*dve_tab.past(0, "tiles_b"))
            pe.matmul(ps_o[0][0:E, 0:1], upto[:, :], tiles_b[:, :], start=True, stop=True).then_inc(*pe_tab.up("ends"))
            pe.wait_ge(*dve_tab.past(0, "where_r"))
            pe.matmul(ps_o[0][:, 0:TILES], where_r[:, :], own[:, :], start=True, stop=True).then_inc(*pe_tab.up("row"))
            pe.matmul(ps_o[1][:, 0:TILES], exp_id[:, :], own[:, :], start=True, stop=True).then_inc(*pe_tab.up("expert"))
            pe.wait_ge(*dve_tab.past(0, "row"))

            exp_regs = [pe.alloc_register(f"exp_reg{u}") for u in range(LAG + U - 1)]

            def begin(s):
                pe.load(exp_regs, tile_exp[0:1, bass.ds(s, LAG + U - 1)])

            def expert(u, lag):
                return pe.snap(exp_regs[u + LAG - lag], min_val=0, max_val=E - 1)

            def step(s, u):
                b = u % 2
                if live(s, 3, TILES):
                    pe.wait_ge(*dve_h.past(s - 3, "hid"))
                    if later(s, 5):
                        pe.wait_ge(*dve_t.past(s - 5, "h"))
                    hold(pe, passed)
                    pe.transpose(ps_h[1 - b][:, :], hid[1 - b][:, :], ident[:, :]).then_inc(*pe_h.up("h"))
                if live(s, 0, TILES):
                    pe.wait_ge(loaded[u], (s - u) * (16 // U) + 16)
                    if later(s, 2):
                        pe.wait_ge(*act_t.past(s - 2, "t"))
                    for c in range(CH):
                        mm = pe.transpose(ps_t[b][:, c, :], rows[u][:, c * P:(c + 1) * P], ident[:, :])
                    mm.then_inc(*pe_t.up("t"))
                if live(s, 1, TILES):
                    e = expert(u, 1)
                    pe.wait_ge(*act_t.past(s - 1, "t"))
                    if later(s, 3):
                        pe.wait_ge(*dve_h.past(s - 3, "hid"))
                    for c in range(CH):
                        mm = pe.matmul(ps_gu[1 - b][:, :], rows_t[1 - b][:, c, :],
                                       w_gu[:, bass.ds(e, 1), c, :].rearrange("p o f -> p (o f)"),
                                       start=c == 0, stop=c == CH - 1)
                    mm.then_inc(*pe_gu.up("gu"))
                if live(s, 4, TILES):
                    pe.wait_ge(*dve_t.past(s - 4, "h"))
                    if later(s, 6):
                        pe.wait_ge(*act_o.past(s - 6, "o"))
                    pe.matmul(ps_o[b][:, :], hid_t[b][:, :],
                                        w_dn[:, bass.ds(expert(u, 4), 1), :].rearrange("p o c -> p (o c)"),
                                        start=True, stop=True).then_inc(*pe_o.up("o"))

            pipelined(pe, step, TILES, LAG, U, 2 * U, begin)

        @block.scalar
        def _(act):
            def step(s, u):
                b = u % 2
                if live(s, 0, TILES):
                    act.wait_ge(*pe_t.past(s, "t"))
                    if later(s, 2):
                        act.wait_ge(*pe_gu.past(s - 2, "gu"))
                    nc.scalar.copy(rows_t[b][:, :, :], ps_t[b][:, :, :]).then_inc(*act_t.up("t"))
                if live(s, 1, TILES):
                    act.wait_ge(*pe_gu.past(s - 1, "gu"))
                    if later(s, 3):
                        act.wait_ge(*dve_h.past(s - 3, "hid"))
                    nc.scalar.activation(silu[1 - b][:, :], ps_gu[1 - b][:, 0:I], ACT.Silu).then_inc(*act_s.up("silu"))
                if live(s, 4, TILES):
                    v = (u - 4) % U
                    act.wait_ge(*pe_o.past(s - 4, "o"))
                    if later(s, 4 + U):
                        act.wait_ge(stored[v], (s - 4 - v) * (16 // U))
                    nc.scalar.copy(made[v][:, :], ps_o[b][:, :]).then_inc(*act_o.up("o"))

            pipelined(act, step, TILES, LAG, U, 2 * U)

        @block.vector
        def _(dve):
            def mk(ins, name):
                ins.then_inc(*dve_tab.up(name))
                dve.wait_ge(*dve_tab.past(0, name))

            dve.wait_ge(*pe_tab.past(0, "count"))
            mk(dve.tensor_copy(cnt[:, :], ps_o[0][0:E, 0:1]), "count")
            dve.wait_ge(const, 1)
            mk(dve.tensor_scalar(fits[:, :], steps16[:, :], cnt[:, 0:1], None, ALU.is_lt), "fits")
            mk(dve.tensor_reduce(tiles[:, :], fits[:, :], AX, ALU.add), "tiles")
            mk(dve.tensor_copy(tiles_b[:, :], tiles[:, :]), "tiles_b")
            dve.wait_ge(*pe_tab.past(0, "ends"))
            mk(dve.tensor_copy(ends[:, :], ps_o[0][0:E, 0:1]), "ends")
            mk(dve.tensor_tensor(begins[:, :], ends[:, :], tiles[:, :], ALU.subtract), "begins")
            mk(dve.tensor_scalar(ended[:, :], iota_j[:, :], ends[:, 0:1], None, ALU.is_ge), "ended")
            mk(dve.scalar_tensor_tensor(out=own[:, :], in0=iota_j[:, :], scalar=begins[:, 0:1], in1=ended[:, :],
                                        op0=ALU.is_ge, op1=ALU.subtract), "own")
            mk(dve.tensor_tensor(where[:, :], list_start[:, :], cnt[:, :], ALU.add), "where")
            mk(dve.scalar_tensor_tensor(out=where2[:, :], in0=begins[:, :], scalar=float(P), in1=where[:, :],
                                        op0=ALU.mult, op1=ALU.add), "where2")
            mk(dve.tensor_scalar(where_r[:, :], onesf[:, :], where2[:, 0:1], None, ALU.mult), "where_r")
            dve.wait_ge(*pe_tab.past(0, "expert"))
            mk(dve.tensor_copy(tile_exp_f[:, :], ps_o[1][:, 0:TILES]), "exp_f")
            mk(dve.tensor_copy(tile_exp[:, LAG:LAG + TILES], tile_exp_f[0:1, :]), "exp")
            mk(dve.tensor_tensor(trow[:, :], ps_o[0][0:1, 0:TILES], iota_j128[:, :], ALU.subtract), "trow")
            mk(dve.tensor_scalar(tile_row[:, :], trow[:, :], 0.0, None, ALU.max), "row")

            def step(s, u):
                b = u % 2
                if live(s, 3, TILES):
                    dve.wait_ge(*pe_h.past(s - 3, "h"))
                    if later(s, 5):
                        dve.wait_ge(*pe_o.past(s - 5, "o"))
                    dve.tensor_copy(hid_t[1 - b][:, :], ps_h[1 - b][:, :]).then_inc(*dve_t.up("h"))
                if live(s, 0, TILES):
                    dve.wait_ge(loaded[u], (s - u) * (16 // U) + 16)
                    dve.scalar_tensor_tensor(
                        out=junk[:, u, :], in0=rows[u][:, C:C + TOPK], scalar=tile_exp_f[:, at(s)],
                        in1=rows[u][:, C + TOPK:ROW], op0=ALU.is_equal, op1=ALU.mult,
                        accum_out=goes_f[:, u:u + 1]).then_inc(*dve_to.up("sum"))
                if live(s, 1, TILES):
                    dve.wait_ge(*act_s.past(s - 1, "silu"))
                    if later(s, 3):
                        dve.wait_ge(*pe_h.past(s - 3, "h"))
                    dve.tensor_tensor(hid[1 - b][:, :], silu[1 - b][:, :], ps_gu[1 - b][:, I:2 * I],
                                                 ALU.mult).then_inc(*dve_h.up("hid"))
                if live(s, 0, TILES):
                    dve.wait_ge(*dve_to.past(s, "sum"))
                    if later(s, U):
                        dve.wait_ge(stored[u], (s - u) * (16 // U))
                    dve.tensor_scalar(goes[u][:, :], goes_f[:, u:u + 1], BIG, None, ALU.add).then_inc(*dve_to.up("goes"))

            weights, total = k["weights"], k["esum"]

            def over(v):
                return v[:, :].rearrange("p (t o) -> p t o", o=1).broadcast_to([P, T, TOPK])

            mk(dve.reciprocal(total[:, :], total[:, :]), "recip")
            mk(dve.tensor_tensor(weights[:, :, :], weights[:, :, :], over(total), ALU.mult), "probs")
            mk(dve.tensor_reduce(total[:, :], weights[:, :, :], AX, ALU.add), "total")
            mk(dve.reciprocal(total[:, :], total[:, :]), "recip2")
            mk(dve.tensor_tensor(weights[:, :, :], weights[:, :, :], over(total), ALU.mult), "weights")
            pipelined(dve, step, TILES, LAG, U, 2 * U)


def combine(nc, k, results, out_tiles):
    acc, weights = k["acc"], k["weights"]
    with ExitStack() as ctx:
        def sem(name):
            return ctx.enter_context(nc.semaphore(f"combine_{name}"))

        U = 4
        got = [ctx.enter_context(nc.sbuf_tensor(f"got{u}", [P, TOPK, C], F32)) for u in range(U)]
        loaded = [sem(f"loaded{u}") for u in range(U)]
        passed = sem("passed")
        summed = Steps(sem("summed"), *[f"k{j}" for j in range(TOPK)], "both")
        stored = sem("stored")
        block = ctx.enter_context(nc.Block())
        by_tile = results.rearrange("(n p k) c -> n p k c", p=P, k=TOPK)

        @block.sync
        def _(sp):
            def step(s, u):
                if later(s, U):
                    sp.wait_ge(*summed.past(s - U, "both"))
                    hold(sp, passed)
                sp.dma_start(got[u][:, :, :], by_tile[at(s)].rearrange("n p k c -> (n p) k c")).then_inc(loaded[u], 16)

            pipelined(sp, step, T, 0, U, U)

        @block.vector
        def _(dve):
            def step(s, u):
                dve.wait_ge(loaded[u], (s - u) * (16 // U) + 16)
                x_t = acc[:, at(s), :].rearrange("p o c -> p (o c)")
                odd = got[u][:, 1, :]
                for j in range(TOPK):
                    w = weights[:, at(s), j:j + 1].rearrange("p o k -> p (o k)")
                    if j >= 2:
                        dve.wait_ge(*summed.past(s, f"k{j - 2}"))
                    if j == 1:
                        ins = dve.tensor_scalar(odd, odd, w, None, ALU.mult)
                    else:
                        to = odd if j % 2 else x_t
                        ins = dve.scalar_tensor_tensor(out=to, in0=got[u][:, j, :], scalar=w, in1=to,
                                                       op0=ALU.mult, op1=ALU.add)
                    ins.then_inc(*summed.up(f"k{j}"))
                dve.wait_ge(*summed.past(s, f"k{TOPK - 1}"))
                dve.tensor_tensor(x_t, x_t, odd, ALU.add).then_inc(*summed.up("both"))

            pipelined(dve, step, T, 0, U, U)

        @block.scalar
        def _(act):
            def step(s, u):
                act.wait_ge(*summed.past(s, "both"))
                hold(act, passed)
                act.dma_start(out_tiles[:, at(s), :], acc[:, at(s), :]).then_inc(stored, 16)

            pipelined(act, step, T, 0, U, U)
            act.wait_ge(stored, T * 16)


_INS = ["x", "ctx_512", "L0_ffn_router_w", "L0_ffn_gate_up_proj", "L0_ffn_down_proj", "L0_ffn_shared_gate_w",
        "L0_ffn_shared_up_w", "L0_ffn_shared_down_w", "L0_ffn_shared_expert_gate_w"]


def kernel(**inputs):
    import numpy as np
    import concourse.bacc as bacc
    from concourse.bass_utils import run_bass_kernel_spmd

    nc = bacc.Bacc("TRN2", target_bir_lowering=False, num_devices=1)
    arrays, args = {}, []
    for name in _INS:
        a = np.ascontiguousarray(inputs[name])
        arrays[f"in_{name}"] = a
        args.append(nc.dram_tensor(f"in_{name}", a.shape, mybir.dt.from_np(a.dtype), kind="ExternalInput").ap())
    out = nc.dram_tensor("out", (B, S, C), F32, kind="ExternalOutput").ap()
    moe_block(nc, *args, out)
    done = run_bass_kernel_spmd(nc, [arrays], core_ids=[0])
    return done.results[0]["out"]
```

```python
from contextlib import ExitStack

import concourse.bass as bass
from concourse import mybir

F32 = mybir.dt.float32
F32R = mybir.dt.float32r
BF16 = mybir.dt.bfloat16
I32 = mybir.dt.int32
U32 = mybir.dt.uint32
ALU = mybir.AluOpType
ACT = mybir.ActivationFunctionType
AX = mybir.AxisListType.X

P = 128
B, S, C = 32, 64, 256
KS, KD = 64, 64
KV, G, D = 8, 4, 8
T = B * S // P
CH = C // P
E, I, TOPK = 64, 64, 8
N = B * S
EPS = 1e-5
SCALE = float(D) ** -0.5
CAP = P + N
ROW = C + 2 * TOPK
FS = 3 * I + 1
FETCH = 24
TILES = -(-((N * TOPK + E * (P - 1)) // P) // FETCH) * FETCH
BEHIND = 4
BIG = float(1 << 20)
WCH = 4


class Steps:

    def __init__(self, sem, *names):
        self.sem, self.names = sem, names

    def up(self, name):
        assert name in self.names
        return self.sem, 1

    def past(self, rnd, name):
        return self.sem, rnd * len(self.names) + (self.names.index(name) + 1)


def pipelined(eng, step, rounds, lag, unroll, first, begin=None):
    assert first % unroll == 0 and (rounds - first) % unroll == 0

    def steps(s, count):
        if begin:
            begin(s)
        for u in range(count):
            step(s + u if u else s, u)

    for s in range(0, first, unroll):
        steps(s, unroll)
    with eng.Fori(first // unroll, rounds // unroll) as i:
        steps(i * unroll, unroll)
    for s in range(rounds, rounds + lag, unroll):
        steps(s, min(unroll, rounds + lag - s))


def hold(eng, passed):
    eng.sem_inc(passed, 1)


def live(s, lag, rounds):
    return not isinstance(s, int) or 0 <= s - lag < rounds


def later(s, n):
    return not isinstance(s, int) or s >= n


RSQRT = ["v", "guess"] + [f"n{i}{c}" for i in range(3) for c in "abc"]


def rsqrt(dve, steps, rnd, out, var, v, a, b):
    def do(ins, name):
        ins.then_inc(*steps.up(name))
        dve.wait_ge(*steps.past(rnd, name))

    do(dve.tensor_scalar(v, var, EPS, None, ALU.add), "v")
    do(dve.tensor_scalar(out.bitcast(I32), v.bitcast(I32), -0.5, float(0x5f3759df), ALU.mult, ALU.add), "guess")
    for i in range(3):
        do(dve.tensor_tensor(a, out, out, ALU.mult), f"n{i}a")
        do(dve.scalar_tensor_tensor(out=b, in0=a, scalar=-0.5, in1=v, op0=ALU.mult, op1=ALU.mult), f"n{i}b")
        do(dve.scalar_tensor_tensor(out=out, in0=b, scalar=1.5, in1=out, op0=ALU.add, op1=ALU.mult), f"n{i}c")


def at(i):
    return bass.ds(i, 1)


def moe_block(nc, x, ctx_, router_w, gate_up, down, sh_gate, sh_up, sh_down, sh_weight, out):
    lists = nc.dram_tensor("lists", [E * CAP, ROW], F32).ap()
    results = nc.dram_tensor("results", [N * TOPK, C], F32).ap()
    x_tiles = x.rearrange("(n b) s c -> (b s) n c", b=2)
    out_tiles = out.rearrange("(n b) s c -> (b s) n c", b=2)
    with ExitStack() as ctx:
        def sb(name, shape, dt=F32):
            return ctx.enter_context(nc.sbuf_tensor(name, shape, dt))

        keep = dict(
            w_gu=sb("w_gu", [P, E, CH, P]),
            w_dn=sb("w_dn", [P, E, C], F32R),
            acc=sb("acc", [P, T, C]),
            w_fs=sb("w_fs", [P, CH, FS]),
            w_sd=sb("w_sd", [I, C]),
            mean=sb("mean", [P, T, 2]),
            rstd=sb("rstd", [P, T]),
            ident=sb("ident", [P, P]),
            kvmask=sb("kvmask", [P, KV]),
            pick=sb("pick", [64, 32, 64], F32R),
            before=sb("before", [P, P], BF16),
            ones=sb("ones", [P, P], BF16),
            list_base=sb("list_base", [P, E]),
            dest=sb("dest", [P, T, TOPK]),
            weights=sb("weights", [P, T, TOPK]),
            esum=sb("esum", [P, T]),
            chosen=sb("chosen", [P, 2, E], BF16),
            filler=sb("filler", [P, ROW]),
            shift=sb("shift", [P, T]),
            tile_row=sb("tile_row", [1, TILES], I32),
            tile_exp=sb("tile_exp", [1, TILES + 2 * FETCH], I32),
            tile_exp_f=sb("tile_exp_f", [P, TILES]),
            eps=sb("eps", [P, 1]),
        )
        prepare(nc, keep, lists, x_tiles, router_w, gate_up, down, sh_gate, sh_up, sh_down, sh_weight)
        route(nc, keep, lists, ctx_)
        experts(nc, keep, lists, results)
        combine(nc, keep, results, out_tiles)


def prepare(nc, k, lists, x_tiles, router_w, gate_up, down, sh_gate, sh_up, sh_down, sh_weight):
    w_gu, w_dn, acc, w_fs, w_sd = k["w_gu"], k["w_dn"], k["acc"], k["w_fs"], k["w_sd"]
    mean, rstd, ident, kvmask, pick = k["mean"], k["rstd"], k["ident"], k["kvmask"], k["pick"]
    before, ones, list_base, dest = k["before"], k["ones"], k["list_base"], k["dest"]
    chunks = E // WCH
    with ExitStack() as ctx:
        def sb(name, shape, dt=F32):
            return ctx.enter_context(nc.sbuf_tensor(f"prepare_{name}", shape, dt))

        def sem(name):
            return ctx.enter_context(nc.semaphore(f"prepare_{name}"))

        U = 4
        gu_in = [sb(f"gu_in{u}", [P, WCH, C]) for u in range(U)]
        dn_in = [sb(f"dn_in{u}", [P, CH, WCH, I]) for u in range(U)]
        fs_in = sb("fs_in", [P, 2, C])
        sd_in = sb("sd_in", [P, CH, I])
        filler = k["filler"]
        stats = sb("stats", [P, T, 6])
        sel32 = sb("sel32", [64, 32])
        rs_tmp = sb("rs_tmp", [P, 3, T])
        ps_gu = [ctx.enter_context(nc.psum_tensor(f"prepare_ps_gu{u}", [P, 2, CH, P], F32)) for u in range(2)]
        ps_dn = [ctx.enter_context(nc.psum_tensor(f"prepare_ps_dn{u}", [I, 2, C], F32)) for u in range(2)]
        ps_fs = ctx.enter_context(nc.psum_tensor("prepare_ps_fs", [P, 2, FS], F32))
        ps_sd = ctx.enter_context(nc.psum_tensor("prepare_ps_sd", [I, C], F32))

        x_in = [sem(f"x_in{q}") for q in range(U)]
        fs_loaded = sem("fs_loaded")
        gu_loaded = [sem(f"gu_loaded{u}") for u in range(U)]
        passed = sem("passed")
        const = sem("const")
        const_chain = sem("const_chain")
        dve_rs = Steps(sem("dve_rs"), *RSQRT)
        pe_chunk = Steps(sem("pe_chunk"), "gu0", "dn0", "gu1", "dn1")
        act_chunk = Steps(sem("act_chunk"), "gu0", "gu1")
        dve_chunk = Steps(sem("dve_chunk"), "dn0", "dn1")
        act_dn = Steps(sem("act_dn"), "dn0", "dn1")
        stats_done = sem("stats_done")
        pe_fs = sem("pe_fs")
        dve_fs = sem("dve_fs")
        block = ctx.enter_context(nc.Block())
        gu_dram = gate_up.rearrange("(n e) f c -> n f e c", e=WCH)
        dn_dram = down.rearrange("(n e) (k p) i -> n k p e i", e=WCH, p=P)

        @block.sync
        def _(sp):
            sp.dma_start(fs_in[0:E, 0, :], router_w).then_inc(fs_loaded, 16)
            sp.dma_start(fs_in[E:P, 0, :], sh_gate).then_inc(fs_loaded, 16)
            sp.dma_start(fs_in[0:I, 1, :], sh_up).then_inc(fs_loaded, 16)
            sp.dma_start(fs_in[I:I + 1, 1, :], sh_weight).then_inc(fs_loaded, 16)
            sp.dma_start(sd_in[:, :, :], sh_down.rearrange("(k p) i -> p k i", p=P)).then_inc(fs_loaded, 16)

            def step(s, u):
                if later(s, U):
                    sp.wait_ge(*pe_chunk.past(s - U, "dn1"))
                    hold(sp, passed)
                sp.dma_start(gu_in[u][:, :, :], gu_dram[at(s)].rearrange("n f e c -> (n f) e c")
                             ).then_inc(gu_loaded[u], 16)
                for h in range(CH):
                    sp.dma_start(dn_in[u][:, h, :, :],
                                 dn_dram[at(s), h].rearrange("n p e i -> (n p) e i")).then_inc(gu_loaded[u], 16)

            pipelined(sp, step, chunks, 0, U, U)

        @block.scalar
        def _(act):
            act.preload_act_table_set("natural_log_exp_and_others")
            for q in range(U):
                n = T // U
                act.dma_start(acc[:, q * n:(q + 1) * n, :], x_tiles[:, q * n:(q + 1) * n, :]).then_inc(x_in[q], 16)

            def step(s, u):
                for h in range(2):
                    e = bass.ds(s * WCH + 2 * h, 2)
                    act.wait_ge(*pe_chunk.past(s, f"gu{h}"))
                    nc.scalar.copy(w_gu[:, e, :, :], ps_gu[h][:, :, :, :]).then_inc(*act_chunk.up(f"gu{h}"))
                    act.wait_ge(*pe_chunk.past(s, f"dn{h}"))
                    nc.scalar.copy(w_dn[0:I, e, :], ps_dn[h][:, :, :]).then_inc(*act_dn.up(f"dn{h}"))

            pipelined(act, step, chunks, 0, U, U)

        @block.tensor
        def _(pe):
            pe.wait_ge(const, 1)
            pe.wait_ge(fs_loaded, 80)
            for c in range(CH):
                cols = slice(c * P, (c + 1) * P)
                pe.transpose(ps_fs[:, c, 0:P], fs_in[:, 0, cols], ident[:, :])
                pe.transpose(ps_fs[:, c, P:FS], fs_in[0:I + 1, 1, cols], ident[0:I + 1, 0:I + 1])
                mm = pe.transpose(ps_sd[:, cols], sd_in[:, c, :], ident[:, :])
            mm.then_inc(pe_fs, 1)

            def step(s, u):
                pe.wait_ge(gu_loaded[u], (s - u) * (16 // U * (1 + CH)) + 16 * (1 + CH))
                for h in range(2):
                    if later(s, 1):
                        pe.wait_ge(*act_chunk.past(s - 1, f"gu{h}"))
                    for e in range(2):
                        for c in range(CH):
                            mm = pe.transpose(ps_gu[h][:, e, c, :], gu_in[u][:, 2 * h + e, c * P:(c + 1) * P],
                                              ident[:, :])
                    mm.then_inc(*pe_chunk.up(f"gu{h}"))
                    if later(s, 1):
                        pe.wait_ge(*dve_chunk.past(s - 1, f"dn{h}"))
                        hold(pe, passed)
                    for e in range(2):
                        for c in range(CH):
                            mm = pe.transpose(ps_dn[h][:, e, c * P:(c + 1) * P], dn_in[u][:, c, 2 * h + e, :],
                                              ident[:, :])
                    mm.then_inc(*pe_chunk.up(f"dn{h}"))

            pipelined(pe, step, chunks, 0, U, U)

        @block.vector
        def _(dve):
            dve.wait_ge(const, 2)
            dve.tensor_copy(pick[:, :, :], sel32[:, :].rearrange("p (c o) -> p c o", o=1).broadcast_to([64, 32, 64]))
            dve.wait_ge(pe_fs, 1)
            dve.tensor_copy(w_fs[:, :, :], ps_fs[:, :, :])
            dve.tensor_copy(w_sd[:, :], ps_sd[:, :]).then_inc(dve_fs, 1)

            def first_norm():
                dve.wait_ge(stats_done, T)
                for t in range(T):
                    dve.bn_aggr(mean[:, t, :], stats[:, t, :]).then_inc(stats_done, 1)
                dve.wait_ge(stats_done, 2 * T)
                rsqrt(dve, dve_rs, 0, rstd[:, :], mean[:, :, 1], rs_tmp[:, 0, :], rs_tmp[:, 1, :], rs_tmp[:, 2, :])
                dve.scalar_tensor_tensor(out=k["shift"][:, :], in0=mean[:, :, 0], scalar=-1.0, in1=rstd[:, :],
                                         op0=ALU.mult, op1=ALU.mult)

            def step(s, u):
                if isinstance(s, int):
                    dve.wait_ge(x_in[s], 16)
                    for t in range(s * T // U, (s + 1) * T // U):
                        dve.bn_stats(stats[:, t, :], acc[:, t, :]).then_inc(stats_done, 1)
                for h in range(2):
                    dve.wait_ge(*act_dn.past(s, f"dn{h}"))
                    e = bass.ds(s * WCH + 2 * h, 2)
                    dve.tensor_tensor(w_dn[I:P, e, :], ps_dn[h][:, :, :], w_dn[0:I, e, :].bitcast(F32),
                                      ALU.subtract).then_inc(*dve_chunk.up(f"dn{h}"))
                if isinstance(s, int) and s == U - 1:
                    first_norm()

            pipelined(dve, step, chunks, 0, U, U)

        @block.gpsimd
        def _(pool):
            made = [0]

            def link(ins):
                made[0] += 1
                ins.then_inc(const_chain, 1)
                pool.wait_ge(const_chain, made[0])

            link(pool.memset(ident[:, :], 0.0))
            pool.affine_select(out=ident[:, :], in_=ident[:, :], compare_op=ALU.not_equal, fill=1.0, base=0,
                               pattern=[[-1, P]], channel_multiplier=1).then_inc(const, 1)
            link(pool.memset(sel32[:, :], 0.0))
            link(pool.affine_select(out=sel32[:, :], in_=sel32[:, :], compare_op=ALU.not_equal, fill=1.0, base=0,
                                    pattern=[[-1, 32]], channel_multiplier=1))
            pool.affine_select(out=sel32[:, :], in_=sel32[:, :], compare_op=ALU.not_equal, fill=1.0, base=-32,
                               pattern=[[-1, 32]], channel_multiplier=1).then_inc(const, 1)
            link(pool.memset(filler[:, :], 0.0))
            pool.memset(filler[:, C:C + TOPK], -1.0)
            link(pool.memset(kvmask[:, :], 1.0))
            for h in range(2):
                m = kvmask[h * 64:(h + 1) * 64, :]
                link(pool.affine_select(out=m, in_=m, compare_op=ALU.is_ge, fill=0.0, base=0,
                                        pattern=[[-D, KV]], channel_multiplier=1))
                link(pool.affine_select(out=m, in_=m, compare_op=ALU.is_ge, fill=0.0, base=D - 1,
                                        pattern=[[D, KV]], channel_multiplier=-1))
            pool.memset(ones[:, :], 1.0)
            link(pool.memset(before[:, :], 1.0))
            pool.affine_select(out=before[:, :], in_=before[:, :], compare_op=ALU.is_ge, fill=0.0, base=-1,
                               pattern=[[1, P]], channel_multiplier=-1)
            pool.iota(list_base[:, :], [[CAP, E]], base=P, channel_multiplier=0, allow_small_or_imprecise_dtypes=True)
            pool.iota(dest[:, :, :], [[P * TOPK, T], [1, TOPK]], base=-int(BIG), channel_multiplier=TOPK,
                      allow_small_or_imprecise_dtypes=True)
            pool.memset(k["chosen"][:, 0, :], 0.0)
            pool.memset(k["eps"][:, :], EPS)


def route(nc, k, lists, ctx_):
    acc, w_fs, w_sd, mean, rstd, ident = k["acc"], k["w_fs"], k["w_sd"], k["mean"], k["rstd"], k["ident"]
    kvmask, pick, before, ones = k["kvmask"], k["pick"], k["before"], k["ones"]
    list_base, dest, weights, chosen = k["list_base"], k["dest"], k["weights"], k["chosen"]
    esum, shift, eps = k["esum"], k["shift"], k["eps"]
    tile_row, tile_exp, tile_exp_f = k["tile_row"], k["tile_exp"], k["tile_exp_f"]
    with ExitStack() as ctx:
        def sb(name, shape, dt=F32):
            return ctx.enter_context(nc.sbuf_tensor(f"route_{name}", shape, dt))

        def sem(name):
            return ctx.enter_context(nc.semaphore(f"route_{name}"))

        def psum(name, shape):
            return ctx.enter_context(nc.psum_tensor(f"route_{name}", shape, F32))

        UR = 4
        key_in = [sb(f"key_in{u}", [P, KD]) for u in range(UR)]
        val_in = [sb(f"val_in{u}", [P, 2, KD]) for u in range(UR)]
        key_hl = sb("key_hl", [P, 2, KD], F32R)
        key_t = [sb(f"key_t{u}", [P, P]) for u in range(2)]
        keys = [sb(f"keys{u}", [P, 2, KV, KS], F32R) for u in range(2)]
        vals = [sb(f"vals{u}", [P, 2, KV, D + 1]) for u in range(2)]
        q_tok = sb("q_tok", [P, G, 2, KD])
        q_hi = [sb(f"q_hi{u}", [P, 2, G, S], F32R) for u in range(2)]
        q_lo = [sb(f"q_lo{u}", [P, 2, G, S], F32R) for u in range(2)]
        negmax = sb("negmax", [P, 2, 4, KV])
        negmax_t = sb("negmax_t", [64, P], F32R)
        probs = [sb(f"probs{b}", [P, 4, G * S]) for b in range(2)]
        rden = sb("rden", [P, 4, KV])
        attn = sb("attn", [P, C])
        st = sb("st", [P, 6])
        mv = sb("mv", [P, 2])
        ln_v = sb("ln_v", [P, 1])
        rs2 = sb("rs2", [P, 1])
        newton = sb("newton", [P, 2])
        rs_new = sb("rs_new", [P, 1])
        shift2 = sb("shift2", [P, 1])
        row = [sb(f"row{u}", [P, ROW]) for u in range(UR)]
        h_t = sb("h_t", [P, CH, P])
        lg = sb("lg", [P, FS])
        nlmax = sb("nlmax", [P, 1])
        ex = sb("ex", [P, E])
        eg = sb("eg", [P, I + 1])
        den = sb("den", [P, I + 1])
        sig = [sb(f"sig{u}", [P, I + 1]) for u in range(2)]
        silu = sb("silu", [P, I])
        hid = sb("hid", [P, I])
        hid_t = sb("hid_t", [I, P])
        top_e = sb("top_e", [P, TOPK])
        idx = sb("idx", [P, TOPK], U32)
        marked = sb("marked", [P, E])
        picked = [sb(f"picked{u}", [P, E], BF16) for u in range(2)]
        slot = sb("slot", [P, E])
        placed = sb("placed", [P, E])
        posf = sb("posf", [P, TOPK])
        pos = [sb(f"pos{u}", [P, TOPK], I32) for u in range(UR)]

        ps_q = psum("ps_q", [P, G, P])
        ps_qb = ps_q[:, :, :].rearrange("p g (b s) -> p b g s", b=2)
        ps_s = [psum(f"ps_s{u}", [P, KV, KS]) for u in range(2)]
        ps_t = psum("ps_t", [P, 4, G * S])
        ps_v = psum("ps_v", [P, 512])
        ps_h = psum("ps_h", [P, 512])
        ps_l = psum("ps_l", [P, 512])
        ps_pv = ps_v[:, 0:4 * KV * (D + 1)].rearrange("p (a v d) -> p a v d", a=4, v=KV)
        ps_max = ps_v[0:64, 384:384 + P]
        ps_key = ps_h[:, 384:384 + P]
        ps_ht = ps_h[:, 0:C].rearrange("p (c t) -> p c t", c=CH)
        ps_hid = ps_h[0:I, C:C + P]
        ps_lg = ps_l[:, 0:FS]
        ps_rank = ps_l[:, 0:E]
        ps_sh = ps_l[:, 256:256 + C]

        steps16 = sb("steps16", [E, T])
        upto = sb("upto", [E, E], BF16)
        iota_j = sb("iota_j", [E, TILES])
        iota_j128 = sb("iota_j128", [1, TILES])
        list_start = sb("list_start", [E, 1])
        exp_id = sb("exp_id", [E, P])
        cnt = sb("cnt", [E, 1])
        fits = sb("fits", [E, T])
        tiles = sb("tiles", [E, 1])
        tiles_b = sb("tiles_b", [E, 1], BF16)
        ends = sb("ends", [E, 1])
        begins = sb("begins", [E, 1])
        where = sb("where", [E, 1])
        where2 = sb("where2", [E, 1])
        scratch = probs[0][:, :, :].rearrange("p a q -> p (a q)")
        ended, own = scratch[0:E, 0:TILES], scratch[0:E, TILES:2 * TILES]
        trow, where_r = scratch[0:1, 2 * TILES:3 * TILES], scratch[0:E, 3 * TILES:3 * TILES + P]
        ps_tab = ps_q[:, :, :].rearrange("p g t -> p (g t)")

        passed = sem("passed")
        zeroed = sem("zeroed")
        filled = sem("filled")
        key_loaded = [sem(f"key_loaded{u}") for u in range(UR)]
        val_loaded = [sem(f"val_loaded{u}") for u in range(UR)]
        scattered = [sem(f"scattered{u}") for u in range(UR)]
        table_const = sem("table_const")
        table_chain = sem("table_chain")
        pe_tab = Steps(sem("pe_tab"), "count", "ends", "row", "expert")
        dve_tab = Steps(sem("dve_tab"), "count", "fits", "tiles", "tiles_b", "ends", "begins", "ended", "own",
                        "where", "where2", "where_r", "exp_f", "exp", "trow", "row")
        act_load = Steps(sem("act_load"), "tokens")
        dve_load = Steps(sem("dve_load"), "high", "low")
        pe_key = Steps(sem("pe_key"), "t")
        pe_q = Steps(sem("pe_q"), "t")
        act_key = Steps(sem("act_key"), "copy")
        act_q = Steps(sem("act_q"), "high")
        dve_q = Steps(sem("dve_q"), "low")
        dve_keys = Steps(sem("dve_keys"), "spread")
        act_keys = Steps(sem("act_keys"), "spread")
        act_v = Steps(sem("act_v"), "vals")
        pe_s = Steps(sem("pe_s"), "s0", "s1", "s2", "s3")
        dve_s = Steps(sem("dve_s"), "s0", "s1", "s2", "s3", "copy")
        pe_m = Steps(sem("pe_m"), "max")
        dve_m = Steps(sem("dve_m"), "high", "low")
        pe_t = Steps(sem("pe_t"), "t00", "t01", "t10", "t11")
        act_t = Steps(sem("act_t"), "t00", "t01", "t10", "t11")
        pe_v = Steps(sem("pe_v"), "v00", "v01", "v10", "v11")
        dve_v = Steps(sem("dve_v"), "recip", "attn")
        dve_x = Steps(sem("dve_x"), "sum")
        dve_st = Steps(sem("dve_st"), "stats")
        dve_mv = Steps(sem("dve_mv"), "mean")
        act_n = Steps(sem("act_n"), "ln", "rstd")
        dve_n = Steps(sem("dve_n"), "a", "b", "rstd", "shift")
        act_row = Steps(sem("act_row"), "row")
        pe_h = Steps(sem("pe_h"), "h_t")
        act_h = Steps(sem("act_h"), "h_t")
        pe_l = Steps(sem("pe_l"), "logits")
        act_l = Steps(sem("act_l"), "logits")
        dve_lmax = Steps(sem("dve_lmax"), "nlmax")
        act_e = Steps(sem("act_e"), "exp")
        act_g = Steps(sem("act_g"), "e_gates", "e_weight")
        dve_g = Steps(sem("dve_g"), "den", "sig", "silu", "hid")
        dve_r = Steps(sem("dve_r"), "top_e", "marked", "index", "picked", "weights", "idx", "dest", "chosen")
        pe_hid = Steps(sem("pe_hid"), "hid")
        act_hid = Steps(sem("act_hid"), "hid")
        pe_r = Steps(sem("pe_r"), "rank")
        pe_sh = Steps(sem("pe_sh"), "shared")
        dve_sh = Steps(sem("dve_sh"), "shared")
        dve_p = Steps(sem("dve_p"), "slot", "placed", "posf", "pos")
        block = ctx.enter_context(nc.Block())
        ctx_keys = ctx_.rearrange("(n b) t d -> n (b t) d", b=2)
        ctx_vals = ctx_.rearrange("(n b) t d -> n t b d", b=2)

        @block.sync
        def _(sp):
            parts = lists.rearrange("(n e r) c -> n r e c", n=8, r=CAP)

            def step(s, u):
                if later(s, UR):
                    sp.wait_ge(*dve_load.past(s - UR, "low"))
                    hold(sp, passed)
                    sp.wait_ge(*act_v.past(s - UR, "vals"))
                    hold(sp, passed)
                sp.dma_start(key_in[u][:, :], ctx_keys[at(s)].rearrange("n p d -> (n p) d")).then_inc(key_loaded[u], 16)
                for c in range(2):
                    sp.dma_start(val_in[u][c * KS:(c + 1) * KS, :, :],
                                 ctx_vals[at(s)].rearrange("n t b d -> (n t) b d")).then_inc(val_loaded[u], 16)
                if isinstance(s, int):
                    sp.dma_start(parts[s, 0:P],
                                 k["filler"][:, :].rearrange("p (o c) -> p o c", o=1).broadcast_to([P, E // 8, ROW])
                                 ).then_inc(filled, 16)

            pipelined(sp, step, T, 0, UR, 8)
            sp.wait_ge(filled, 8 * 16)

        LAG = 6

        @block.scalar
        def _(act):
            act.wait_ge(zeroed, 3)

            def load(s, u):
                if later(s, 1):
                    act.wait_ge(*pe_q.past(s - 1, "t"))
                x_t = acc[:, at(s), :].rearrange("p o (v g d) -> p g (o v) d", g=G, d=D)
                for c in range(2):
                    ins = nc.scalar.activation(q_tok[:, :, c, :].rearrange("p g (v d) -> p g v d", d=D), x_t,
                                               ACT.Identity, bias=shift[:, at(s)], scale=rstd[:, at(s)])
                ins.then_inc(*act_load.up("tokens"))

            def key_copy(s, u):
                act.wait_ge(*pe_key.past(s, "t"))
                if later(s, 2):
                    act.wait_ge(*dve_keys.past(s - 2, "spread"))
                    act.wait_ge(*act_keys.past(s - 2, "spread"))
                nc.scalar.copy(key_t[u % 2][:, :], ps_key).then_inc(*act_key.up("copy"))

            def spread(s, u):
                if later(s, 2):
                    act.wait_ge(*pe_t.past(s - 2, "t11"))
                    act.wait_ge(*pe_s.past(s - 2, "s3"))
                act.wait_ge(*act_key.past(s, "copy"))
                for h in range(KV // 2, KV):
                    ins = nc.scalar.activation(keys[u % 2][:, :, h, :],
                                               key_t[u % 2][:, :].rearrange("p (b t) -> p b t", b=2),
                                               ACT.Copy, scale=kvmask[:, h:h + 1])
                ins.then_inc(*act_keys.up("spread"))

            def q_high(s, u):
                act.wait_ge(*pe_q.past(s, "t"))
                if later(s, 2):
                    act.wait_ge(*pe_t.past(s - 2, "t11"))
                    act.wait_ge(*pe_s.past(s - 2, "s3"))
                nc.scalar.copy(q_hi[u % 2][:, :, :, :], ps_qb).then_inc(*act_q.up("high"))

            def values(s, u):
                act.wait_ge(val_loaded[u], (s - u) * (32 // UR) + 32)
                if later(s, 2):
                    act.wait_ge(*pe_v.past(s - 2, "v11"))
                for c in range(2):
                    rows = slice(c * KS, (c + 1) * KS)
                    src = val_in[u][rows, :, :].rearrange("p b (v c d) -> p b v c d", c=2, d=D)[:, :, :, c, :]
                    ins = nc.scalar.copy(vals[u % 2][rows, :, c:KV:2, 0:D], src)
                ins.then_inc(*act_v.up("vals"))

            def exps(s, b, h):
                act.wait_ge(*pe_t.past(s, f"t{b}{h}"))
                if later(s, 1):
                    act.wait_ge(*pe_v.past(s - 1, f"v{b}{h}"))
                nc.scalar.activation(probs[b][:, 2 * h:2 * h + 2, :], ps_t[:, 2 * h:2 * h + 2, :],
                                     ACT.Exp, scale=SCALE).then_inc(*act_t.up(f"t{b}{h}"))

            def norm(s, u):
                act.wait_ge(*dve_mv.past(s, "mean"))
                nc.scalar.activation(ln_v[:, :], mv[:, 1:2], ACT.Ln, bias=eps[:, 0:1]).then_inc(*act_n.up("ln"))
                act.wait_ge(*act_n.past(s, "ln"))
                if later(s, 1):
                    act.wait_ge(*dve_n.past(s - 1, "shift"))
                nc.scalar.activation(rs2[:, :], ln_v[:, :], ACT.Exp, scale=-0.5).then_inc(*act_n.up("rstd"))

            def norm_row(s, u):
                act.wait_ge(*dve_n.past(s, "shift"))
                if later(s, UR):
                    act.wait_ge(scattered[u], (s - u) * (16 * TOPK // UR))
                nc.scalar.activation(row[u][:, 0:C], acc[:, at(s), :].rearrange("p o c -> p (o c)"),
                                     ACT.Identity, bias=shift2[:, 0:1], scale=rs_new[:, 0:1]
                                     ).then_inc(*act_row.up("row"))

            def h_copy(s, u):
                act.wait_ge(*pe_h.past(s, "h_t"))
                if later(s, 1):
                    act.wait_ge(*pe_l.past(s - 1, "logits"))
                nc.scalar.copy(h_t[:, :, :], ps_ht).then_inc(*act_h.up("h_t"))

            def logits(s, u):
                act.wait_ge(*pe_l.past(s, "logits"))
                if later(s, 1):
                    act.wait_ge(*dve_g.past(s - 1, "hid"))
                    act.wait_ge(*dve_lmax.past(s - 1, "nlmax"))
                nc.scalar.copy(lg[:, :], ps_lg).then_inc(*act_l.up("logits"))

            def gates(s, u):
                act.wait_ge(*act_l.past(s, "logits"))
                if later(s, 1):
                    act.wait_ge(*dve_g.past(s - 1, "hid"))
                nc.scalar.activation(eg[:, 0:I], lg[:, E:E + I], ACT.Exp, scale=-1.0).then_inc(*act_g.up("e_gates"))
                nc.scalar.activation(eg[:, I:I + 1], lg[:, FS - 1:FS], ACT.Exp, scale=-1.0
                                     ).then_inc(*act_g.up("e_weight"))

            def choices(s, u):
                act.wait_ge(*dve_lmax.past(s, "nlmax"))
                if later(s, 1):
                    act.wait_ge(*dve_r.past(s - 1, "index"))
                nc.scalar.activation(ex[:, :], lg[:, 0:E], ACT.Exp, bias=nlmax[:, 0:1],
                                     accum_out=esum[:, at(s)]).then_inc(*act_e.up("exp"))

            def hid_copy(s, u):
                act.wait_ge(*pe_hid.past(s, "hid"))
                if later(s, 1):
                    act.wait_ge(*pe_sh.past(s - 1, "shared"))
                nc.scalar.copy(hid_t[:, :], ps_hid).then_inc(*act_hid.up("hid"))

            def step(s, u):
                if live(s, 4, T):
                    exps(s - 4, 1, 0)
                if live(s, 2, T):
                    q_high(s - 2, (u - 2) % UR)
                if live(s, 4, T):
                    exps(s - 4, 1, 1)
                if live(s, 2, T):
                    spread(s - 2, (u - 2) % UR)
                if live(s, 6, T):
                    hid_copy(s - 6, (u - 6) % UR)
                if live(s, 5, T):
                    norm_row(s - 5, (u - 5) % UR)
                if live(s, 1, T):
                    key_copy(s - 1, (u - 1) % UR)
                if live(s, 3, T):
                    values(s - 3, (u - 3) % UR)
                if live(s, 5, T):
                    h_copy(s - 5, (u - 5) % UR)
                    logits(s - 5, (u - 5) % UR)
                if live(s, 3, T):
                    exps(s - 3, 0, 0)
                if live(s, 5, T):
                    gates(s - 5, (u - 5) % UR)
                    choices(s - 5, (u - 5) % UR)
                if live(s, 3, T):
                    exps(s - 3, 0, 1)
                if live(s, 4, T):
                    norm(s - 4, (u - 4) % UR)
                if live(s, 0, T):
                    load(s, u)

            pipelined(act, step, T, LAG, UR, 8)
            act.preload_act_table(ACT.Silu)

        @block.tensor
        def _(pe):
            def keys_turned(s, u):
                if later(s, 5):
                    pe.wait_ge(*act_hid.past(s - 5, "hid"))
                elif later(s, 1):
                    pe.wait_ge(*act_key.past(s - 1, "copy"))
                pe.wait_ge(*dve_load.past(s, "low"))
                pe.transpose(ps_key, key_hl[:, :, :].bitcast(F32), ident[:, :]).then_inc(*pe_key.up("t"))

            def q_t(s, u):
                if later(s, 1):
                    pe.wait_ge(*dve_q.past(s - 1, "low"))
                pe.wait_ge(*act_load.past(s, "tokens"))
                for g in range(G):
                    mm = pe.transpose(ps_q[:, g, :], q_tok[:, g, :, :], ident[:, :])
                mm.then_inc(*pe_q.up("t"))

            def scores(s, u, i):
                if i == 0:
                    pe.wait_ge(*dve_q.past(s, "low"))
                    pe.wait_ge(*dve_keys.past(s, "spread"))
                    pe.wait_ge(*act_keys.past(s, "spread"))
                b, g2 = i // 2, i % 2
                if i >= 2:
                    pe.wait_ge(*dve_s.past(s, f"s{i - 2}"))
                elif later(s, 1):
                    pe.wait_ge(*dve_s.past(s - 1, f"s{i + 2}"))
                for part, q in ((0, q_hi[u % 2]), (1, q_lo[u % 2])):
                    mm = pe.matmul(ps_s[i % 2][:, :, :], q[:, b, 2 * g2:2 * g2 + 2, :],
                                   keys[u % 2][:, b, :, :], start=part == 0, stop=part == 1)
                mm.then_inc(*pe_s.up(f"s{i}"))

            def maxima_t(s, u):
                pe.wait_ge(*dve_s.past(s, "copy"))
                if later(s, 1):
                    pe.wait_ge(*dve_v.past(s - 1, "attn"))
                hold(pe, passed)
                pe.transpose(ps_max, negmax[:, :, :, :], ident[:, :]).then_inc(*pe_m.up("max"))

            def attend(s, u, b, h):
                if b == 0:
                    pe.wait_ge(*dve_m.past(s, "low"))
                if b == 1:
                    pe.wait_ge(*act_t.past(s, f"t0{h}"))
                elif later(s, 1):
                    pe.wait_ge(*act_t.past(s - 1, f"t1{h}"))
                for j in (2 * h, 2 * h + 1):
                    kj = keys[u % 2][:, b, 2 * j:2 * j + 2, :]
                    o = ps_t[:, j, :]
                    pe.matmul(o, kj, q_hi[u % 2][:, b, :, :], start=True, stop=False)
                    pe.matmul(o, kj, q_lo[u % 2][:, b, :, :], start=False, stop=False)
                    for g2 in range(2):
                        c = (2 * b + g2) * KV + 2 * j
                        mm = pe.matmul(o[:, g2 * P:(g2 + 1) * P], pick[:, c:c + 2, :], negmax_t[:, :],
                                       start=False, stop=g2 == 1)
                mm.then_inc(*pe_t.up(f"t{b}{h}"))

            def weigh(s, u, b, h):
                if b == 0:
                    pe.wait_ge(*act_v.past(s, "vals"))
                    pe.wait_ge(*dve_m.past(s, "low"))
                pe.wait_ge(*act_t.past(s, f"t{b}{h}"))
                for j in (2 * h, 2 * h + 1):
                    for g2 in range(2):
                        mm = pe.matmul(ps_pv[:, 2 * b + g2, 2 * j:2 * j + 2, :],
                                       probs[b][:, j, g2 * P:(g2 + 1) * P], vals[u % 2][:, b, 2 * j:2 * j + 2, :],
                                       start=True, stop=True)
                mm.then_inc(*pe_v.up(f"v{b}{h}"))

            def rows_turned(s, u):
                pe.wait_ge(*act_row.past(s, "row"))
                if later(s, 1):
                    pe.wait_ge(*act_hid.past(s - 1, "hid"))
                if live(s, -4, T):
                    pe.wait_ge(*act_key.past(s + 4, "copy"))
                for c in range(CH):
                    mm = pe.transpose(ps_ht[:, c, :], row[u][:, c * P:(c + 1) * P], ident[:, :])
                mm.then_inc(*pe_h.up("h_t"))

            def logits(s, u):
                pe.wait_ge(*act_h.past(s, "h_t"))
                if later(s, 1):
                    pe.wait_ge(*dve_p.past(s - 1, "slot"))
                    pe.wait_ge(*dve_sh.past(s - 1, "shared"))
                for c in range(CH):
                    mm = pe.matmul(ps_lg, h_t[:, c, :], w_fs[:, c, :], start=c == 0, stop=c == CH - 1)
                mm.then_inc(*pe_l.up("logits"))

            def hidden_t(s, u):
                pe.wait_ge(*dve_g.past(s, "hid"))
                hold(pe, passed)
                pe.transpose(ps_hid, hid[:, :], ident[:, :]).then_inc(*pe_hid.up("hid"))

            def ranks(s, u):
                pe.wait_ge(*dve_r.past(s, "picked"))
                pe.wait_ge(*act_l.past(s, "logits"))
                pe.matmul(ps_rank, before[:, :], picked[u % 2][:, :], start=True, stop=False)
                pe.matmul(ps_rank, ones[:, :], chosen[:, u % 2, :], start=False, stop=True).then_inc(*pe_r.up("rank"))

            def shared(s, u):
                pe.wait_ge(*act_hid.past(s, "hid"))
                pe.matmul(ps_sh, hid_t[:, :], w_sd[:, :], start=True, stop=True).then_inc(*pe_sh.up("shared"))

            def step(s, u):
                if live(s, 3, T):
                    scores(s - 3, (u - 3) % UR, 3)
                if live(s, 4, T):
                    weigh(s - 4, (u - 4) % UR, 1, 1)
                if live(s, 1, T):
                    keys_turned(s - 1, (u - 1) % UR)
                if live(s, 2, T):
                    scores(s - 2, (u - 2) % UR, 0)
                if live(s, 6, T):
                    ranks(s - 6, (u - 6) % UR)
                    shared(s - 6, (u - 6) % UR)
                if live(s, 5, T):
                    rows_turned(s - 5, (u - 5) % UR)
                if live(s, 2, T):
                    scores(s - 2, (u - 2) % UR, 1)
                if live(s, 3, T):
                    maxima_t(s - 3, (u - 3) % UR)
                if live(s, 1, T):
                    q_t(s - 1, (u - 1) % UR)
                if live(s, 5, T):
                    logits(s - 5, (u - 5) % UR)
                if live(s, 3, T):
                    attend(s - 3, (u - 3) % UR, 0, 0)
                    attend(s - 3, (u - 3) % UR, 0, 1)
                    attend(s - 3, (u - 3) % UR, 1, 0)
                    weigh(s - 3, (u - 3) % UR, 0, 0)
                if live(s, 2, T):
                    scores(s - 2, (u - 2) % UR, 2)
                if live(s, 3, T):
                    attend(s - 3, (u - 3) % UR, 1, 1)
                    weigh(s - 3, (u - 3) % UR, 0, 1)
                if live(s, 5, T):
                    hidden_t(s - 5, (u - 5) % UR)
                if live(s, 3, T):
                    weigh(s - 3, (u - 3) % UR, 1, 0)

            pipelined(pe, step, T, LAG, UR, 8)
            pe.wait_ge(*dve_q.past(T - 1, "low"))
            pe.wait_ge(*dve_r.past(T - 1, "chosen"))
            pe.matmul(ps_tab[0:E, 2 * TILES:2 * TILES + 1], chosen[:, 0, :], ones[:, 0:1],
                      start=True, stop=True).then_inc(*pe_tab.up("count"))
            pe.wait_ge(*dve_tab.past(0, "tiles_b"))
            pe.matmul(ps_tab[0:E, 2 * TILES:2 * TILES + 1], upto[:, :], tiles_b[:, :],
                      start=True, stop=True).then_inc(*pe_tab.up("ends"))
            pe.wait_ge(*dve_tab.past(0, "where_r"))
            pe.matmul(ps_tab[:, 0:TILES], where_r[:, :], own[:, :], start=True, stop=True).then_inc(*pe_tab.up("row"))
            pe.matmul(ps_tab[:, TILES:2 * TILES], exp_id[:, :], own[:, :],
                      start=True, stop=True).then_inc(*pe_tab.up("expert"))

        @block.vector
        def _(dve):
            def load(s, u):
                dve.wait_ge(key_loaded[u], (s - u) * (16 // UR) + 16)
                if later(s, 1):
                    dve.wait_ge(*pe_key.past(s - 1, "t"))
                dve.tensor_copy(key_hl[:, 0, :], key_in[u][:, :]).then_inc(*dve_load.up("high"))

            def load_low(s, u):
                dve.wait_ge(*dve_load.past(s, "high"))
                dve.tensor_tensor(key_hl[:, 1, :], key_in[u][:, :], key_hl[:, 0, :].bitcast(F32),
                                  ALU.subtract).then_inc(*dve_load.up("low"))

            def q_low(s, u):
                if later(s, 2):
                    dve.wait_ge(*pe_t.past(s - 2, "t11"))
                    dve.wait_ge(*pe_s.past(s - 2, "s3"))
                dve.wait_ge(*act_q.past(s, "high"))
                dve.tensor_tensor(q_lo[u % 2][:, :, :, :], ps_qb, q_hi[u % 2][:, :, :, :].bitcast(F32),
                                  ALU.subtract).then_inc(*dve_q.up("low"))

            def spread(s, u):
                if later(s, 2):
                    dve.wait_ge(*pe_t.past(s - 2, "t11"))
                    dve.wait_ge(*pe_s.past(s - 2, "s3"))
                dve.wait_ge(*act_key.past(s, "copy"))
                half = [P, 2, KV // 2, KS]
                src = key_t[u % 2][:, :].rearrange("p (b o t) -> p b o t", b=2, o=1).broadcast_to(half)
                msk = kvmask[:, 0:KV // 2].rearrange("p (a v o) -> p a v o", a=1, o=1).broadcast_to(half)
                dve.tensor_tensor(keys[u % 2][:, :, 0:KV // 2, :], src, msk, ALU.mult).then_inc(*dve_keys.up("spread"))

            def maximum(s, i):
                dve.wait_ge(*pe_s.past(s, f"s{i}"))
                if i == 0 and later(s, 1):
                    dve.wait_ge(*pe_m.past(s - 1, "max"))
                dve.tensor_reduce(negmax[:, 0, i, :], ps_s[i % 2][:, :, :], AX, ALU.max, negate=True
                                  ).then_inc(*dve_s.up(f"s{i}"))

            def maxima_copy(s, u):
                dve.wait_ge(*dve_s.past(s, "s3"))
                dve.tensor_copy(negmax[:, 1, :, :], negmax[:, 0, :, :]).then_inc(*dve_s.up("copy"))

            def maxima_split(s, u):
                dve.wait_ge(*pe_m.past(s, "max"))
                if later(s, 1):
                    dve.wait_ge(*pe_t.past(s - 1, "t11"))
                dve.tensor_copy(negmax_t[:, :], ps_max).then_inc(*dve_m.up("high"))

            def maxima_low(s, u):
                dve.wait_ge(*dve_m.past(s, "high"))
                dve.tensor_tensor(negmax_t[32:64, :], ps_max[32:64, :], negmax_t[32:64, :].bitcast(F32),
                                  ALU.subtract).then_inc(*dve_m.up("low"))

            def divide(s, u):
                dve.wait_ge(*pe_v.past(s, "v11"))
                dve.reciprocal(rden[:, :, :], ps_pv[:, :, :, D]).then_inc(*dve_v.up("recip"))

            def weighted(s, u):
                dve.wait_ge(*dve_v.past(s, "recip"))
                for b in range(2):
                    for g in range(2):
                        rows = slice(g * S, (g + 1) * S)
                        o = attn[b * S:(b + 1) * S, :].rearrange("p (v h g d) -> p h v g d", h=2, g=2, d=D)
                        r = rden[rows, 2 * b:2 * b + 2, :].rearrange("p h (v o) -> p h v o", o=1)
                        ins = dve.tensor_tensor(o[:, :, :, g, :], ps_pv[rows, 2 * b:2 * b + 2, :, 0:D],
                                                r.broadcast_to([S, 2, KV, D]), ALU.mult)
                ins.then_inc(*dve_v.up("attn"))

            def residual(s, u):
                x_t = acc[:, at(s), :].rearrange("p o c -> p (o c)")
                dve.wait_ge(*act_load.past(s, "tokens"))
                dve.wait_ge(*dve_v.past(s, "attn"))
                dve.tensor_tensor(x_t, x_t, attn[:, :], ALU.add).then_inc(*dve_x.up("sum"))

            def statistics(s, u):
                dve.wait_ge(*dve_x.past(s, "sum"))
                hold(dve, passed)
                dve.bn_stats(st[:, :], acc[:, at(s), :].rearrange("p o c -> p (o c)")).then_inc(*dve_st.up("stats"))

            def variance(s, u):
                dve.wait_ge(*dve_st.past(s, "stats"))
                if later(s, 1):
                    dve.wait_ge(*dve_n.past(s - 1, "shift"))
                hold(dve, passed)
                dve.bn_aggr(mv[:, :], st[:, :]).then_inc(*dve_mv.up("mean"))

            def norm(s, u):
                dve.wait_ge(*act_n.past(s, "rstd"))
                if later(s, 1):
                    dve.wait_ge(*act_row.past(s - 1, "row"))
                na, nb = newton[:, 0:1], newton[:, 1:2]
                dve.scalar_tensor_tensor(out=na, in0=mv[:, 1:2], scalar=EPS, in1=rs2[:, :],
                                         op0=ALU.add, op1=ALU.mult).then_inc(*dve_n.up("a"))

            def norm_b(s, u):
                na, nb = newton[:, 0:1], newton[:, 1:2]
                dve.wait_ge(*dve_n.past(s, "a"))
                dve.scalar_tensor_tensor(out=nb, in0=na, scalar=-0.5, in1=rs2[:, :],
                                         op0=ALU.mult, op1=ALU.mult).then_inc(*dve_n.up("b"))

            def norm_c(s, u):
                dve.wait_ge(*dve_n.past(s, "b"))
                dve.scalar_tensor_tensor(out=rs_new[:, :], in0=newton[:, 1:2], scalar=1.5, in1=rs2[:, :],
                                         op0=ALU.add, op1=ALU.mult).then_inc(*dve_n.up("rstd"))

            def norm_d(s, u):
                dve.wait_ge(*dve_n.past(s, "rstd"))
                dve.scalar_tensor_tensor(out=shift2[:, :], in0=mv[:, 0:1], scalar=-1.0, in1=rs_new[:, :],
                                         op0=ALU.mult, op1=ALU.mult).then_inc(*dve_n.up("shift"))

            def logit_max(s, u):
                dve.wait_ge(*act_l.past(s, "logits"))
                if later(s, 1):
                    dve.wait_ge(*act_e.past(s - 1, "exp"))
                dve.tensor_reduce(nlmax[:, :], lg[:, 0:E], AX, ALU.max, negate=True).then_inc(*dve_lmax.up("nlmax"))

            def sigmoid_sum(s, u):
                dve.wait_ge(*act_g.past(s, "e_weight"))
                dve.tensor_scalar(den[:, :], eg[:, :], 1.0, None, ALU.add).then_inc(*dve_g.up("den"))

            def sigmoid(s, u):
                dve.wait_ge(*dve_g.past(s, "den"))
                dve.reciprocal(sig[u % 2][:, :], den[:, :]).then_inc(*dve_g.up("sig"))

            def hidden(s, u):
                dve.wait_ge(*dve_g.past(s, "sig"))
                dve.tensor_tensor(silu[:, :], lg[:, E:E + I], sig[u % 2][:, 0:I], ALU.mult
                                  ).then_inc(*dve_g.up("silu"))

            def hidden_up(s, u):
                dve.wait_ge(*dve_g.past(s, "silu"))
                if later(s, 1):
                    dve.wait_ge(*pe_hid.past(s - 1, "hid"))
                dve.tensor_tensor(hid[:, :], silu[:, :], lg[:, E + I:E + 2 * I], ALU.mult).then_inc(*dve_g.up("hid"))

            def choose(s, u):
                dve.wait_ge(*act_e.past(s, "exp"))
                hold(dve, passed)
                dve.max(top_e[:, :], ex[:, :]).then_inc(*dve_r.up("top_e"))

            def choose_mark(s, u):
                dve.wait_ge(*dve_r.past(s, "top_e"))
                hold(dve, passed)
                dve.match_replace(marked[:, :], top_e[:, :], ex[:, :], -1.0).then_inc(*dve_r.up("marked"))
                dve.max_index(idx[:, :], top_e[:, :], ex[:, :]).then_inc(*dve_r.up("index"))

            def choose_pick(s, u):
                dve.wait_ge(*dve_r.past(s, "marked"))
                if later(s, 2):
                    dve.wait_ge(*pe_r.past(s - 2, "rank"))
                dve.tensor_scalar(picked[u % 2][:, :], marked[:, :], 0.0, None, ALU.is_lt).then_inc(*dve_r.up("picked"))
                dve.tensor_copy(weights[:, at(s), :].rearrange("p o k -> p (o k)"), top_e[:, :]
                                ).then_inc(*dve_r.up("weights"))
                dve.wait_ge(*dve_r.past(s, "index"))
                dve.tensor_copy(row[u][:, C:C + TOPK], idx[:, :]).then_inc(*dve_r.up("idx"))
                dve.tensor_copy(row[u][:, C + TOPK:ROW], dest[:, at(s), :].rearrange("p o k -> p (o k)")
                                ).then_inc(*dve_r.up("dest"))

            def choose_count(s, u):
                dve.wait_ge(*dve_r.past(s, "picked"))
                if later(s, 1):
                    dve.wait_ge(*pe_r.past(s - 1, "rank"))
                dve.tensor_tensor(chosen[:, 1 - u % 2, :], chosen[:, u % 2, :], picked[u % 2][:, :], ALU.add
                                  ).then_inc(*dve_r.up("chosen"))

            def places(s, u):
                dve.wait_ge(*pe_r.past(s, "rank"))
                dve.wait_ge(*pe_sh.past(s, "shared"))
                dve.tensor_tensor(slot[:, :], ps_rank, list_base[:, :], ALU.add).then_inc(*dve_p.up("slot"))

            def places_masked(s, u):
                dve.wait_ge(*dve_p.past(s, "slot"))
                dve.tensor_tensor(placed[:, :], slot[:, :], picked[u % 2][:, :], ALU.mult).then_inc(*dve_p.up("placed"))

            def places_top(s, u):
                dve.wait_ge(*dve_p.past(s, "placed"))
                hold(dve, passed)
                dve.max(posf[:, :], placed[:, :]).then_inc(*dve_p.up("posf"))

            def places_int(s, u):
                dve.wait_ge(*dve_p.past(s, "posf"))
                if later(s, UR):
                    dve.wait_ge(scattered[u], (s - u) * (16 * TOPK // UR))
                dve.tensor_copy(pos[u][:, :], posf[:, :]).then_inc(*dve_p.up("pos"))

            def shared(s, u):
                dve.wait_ge(*pe_sh.past(s, "shared"))
                dve.wait_ge(*pe_r.past(s, "rank"))
                dve.wait_ge(*dve_g.past(s, "sig"))
                x_t = acc[:, at(s), :].rearrange("p o c -> p (o c)")
                dve.scalar_tensor_tensor(out=x_t, in0=ps_sh, scalar=sig[u % 2][:, I:I + 1], in1=x_t,
                                         op0=ALU.mult, op1=ALU.add).then_inc(*dve_sh.up("shared"))

            def step(s, u):
                if live(s, 4, T):
                    weighted(s - 4, (u - 4) % UR)
                if live(s, 6, T):
                    places(s - 6, (u - 6) % UR)
                    shared(s - 6, (u - 6) % UR)
                    places_masked(s - 6, (u - 6) % UR)
                if live(s, 3, T):
                    maxima_split(s - 3, (u - 3) % UR)
                if live(s, 6, T):
                    places_top(s - 6, (u - 6) % UR)
                if live(s, 3, T):
                    maxima_low(s - 3, (u - 3) % UR)
                if live(s, 6, T):
                    places_int(s - 6, (u - 6) % UR)
                    choose_count(s - 6, (u - 6) % UR)
                if live(s, 5, T):
                    logit_max(s - 5, (u - 5) % UR)
                if live(s, 2, T):
                    maximum(s - 2, 0)
                if live(s, 0, T):
                    load(s, u)
                if live(s, 4, T):
                    residual(s - 4, (u - 4) % UR)
                    statistics(s - 4, (u - 4) % UR)
                if live(s, 5, T):
                    choose(s - 5, (u - 5) % UR)
                if live(s, 4, T):
                    variance(s - 4, (u - 4) % UR)
                if live(s, 2, T):
                    maximum(s - 2, 1)
                if live(s, 5, T):
                    sigmoid_sum(s - 5, (u - 5) % UR)
                    sigmoid(s - 5, (u - 5) % UR)
                if live(s, 4, T):
                    norm(s - 4, (u - 4) % UR)
                if live(s, 5, T):
                    hidden(s - 5, (u - 5) % UR)
                    hidden_up(s - 5, (u - 5) % UR)
                    choose_mark(s - 5, (u - 5) % UR)
                if live(s, 4, T):
                    norm_b(s - 4, (u - 4) % UR)
                if live(s, 2, T):
                    maximum(s - 2, 2)
                if live(s, 4, T):
                    norm_c(s - 4, (u - 4) % UR)
                if live(s, 0, T):
                    load_low(s, u)
                if live(s, 1, T):
                    spread(s - 1, (u - 1) % UR)
                if live(s, 4, T):
                    norm_d(s - 4, (u - 4) % UR)
                if live(s, 1, T):
                    q_low(s - 1, (u - 1) % UR)
                if live(s, 5, T):
                    choose_pick(s - 5, (u - 5) % UR)
                if live(s, 2, T):
                    maximum(s - 2, 3)
                if live(s, 3, T):
                    divide(s - 3, (u - 3) % UR)
                if live(s, 2, T):
                    maxima_copy(s - 2, (u - 2) % UR)

            pipelined(dve, step, T, LAG, UR, 8)
            dve.wait_ge(*pe_tab.past(0, "count"))
            dve.tensor_copy(cnt[:, :], ps_tab[0:E, 2 * TILES:2 * TILES + 1]).then_inc(*dve_tab.up("count"))
            dve.wait_ge(*dve_tab.past(0, "count"))
            dve.wait_ge(table_const, 2)
            dve.tensor_scalar(fits[:, :], steps16[:, :], cnt[:, 0:1], None, ALU.is_lt).then_inc(*dve_tab.up("fits"))
            dve.wait_ge(*dve_tab.past(0, "fits"))
            dve.tensor_reduce(tiles[:, :], fits[:, :], AX, ALU.add).then_inc(*dve_tab.up("tiles"))
            dve.wait_ge(*dve_tab.past(0, "tiles"))
            dve.tensor_copy(tiles_b[:, :], tiles[:, :]).then_inc(*dve_tab.up("tiles_b"))
            dve.wait_ge(*dve_tab.past(0, "tiles_b"))
            dve.wait_ge(*pe_tab.past(0, "ends"))
            dve.tensor_copy(ends[:, :], ps_tab[0:E, 2 * TILES:2 * TILES + 1]).then_inc(*dve_tab.up("ends"))
            dve.wait_ge(*dve_tab.past(0, "ends"))
            dve.tensor_tensor(begins[:, :], ends[:, :], tiles[:, :], ALU.subtract).then_inc(*dve_tab.up("begins"))
            dve.wait_ge(*dve_tab.past(0, "begins"))
            dve.tensor_scalar(ended[:, :], iota_j[:, :], ends[:, 0:1], None, ALU.is_ge).then_inc(*dve_tab.up("ended"))
            dve.wait_ge(*dve_tab.past(0, "ended"))
            dve.scalar_tensor_tensor(out=own[:, :], in0=iota_j[:, :], scalar=begins[:, 0:1], in1=ended[:, :],
                                     op0=ALU.is_ge, op1=ALU.subtract).then_inc(*dve_tab.up("own"))
            dve.wait_ge(*dve_tab.past(0, "own"))
            dve.tensor_tensor(where[:, :], list_start[:, :], cnt[:, :], ALU.add).then_inc(*dve_tab.up("where"))
            dve.wait_ge(*dve_tab.past(0, "where"))
            dve.scalar_tensor_tensor(out=where2[:, :], in0=begins[:, :], scalar=float(P), in1=where[:, :],
                                     op0=ALU.mult, op1=ALU.add).then_inc(*dve_tab.up("where2"))
            dve.wait_ge(*dve_tab.past(0, "where2"))
            dve.tensor_scalar(where_r[:, :], ones[0:E, :], where2[:, 0:1], None, ALU.mult
                              ).then_inc(*dve_tab.up("where_r"))
            dve.wait_ge(*dve_tab.past(0, "where_r"))
            dve.wait_ge(*pe_tab.past(0, "expert"))
            dve.tensor_copy(tile_exp_f[:, :], ps_tab[:, TILES:2 * TILES]).then_inc(*dve_tab.up("exp_f"))
            dve.wait_ge(*dve_tab.past(0, "exp_f"))
            dve.tensor_scalar(tile_exp[:, BEHIND:BEHIND + TILES], tile_exp_f[0:1, :], float(C), None,
                              ALU.mult).then_inc(*dve_tab.up("exp"))
            dve.wait_ge(*dve_tab.past(0, "exp"))
            dve.tensor_tensor(trow[:, :], ps_tab[0:1, 0:TILES], iota_j128[:, :], ALU.subtract
                              ).then_inc(*dve_tab.up("trow"))
            dve.wait_ge(*dve_tab.past(0, "trow"))
            dve.tensor_scalar(tile_row[:, :], trow[:, :], 0.0, None, ALU.max).then_inc(*dve_tab.up("row"))
            dve.wait_ge(*dve_tab.past(0, "row"))

        @block.gpsimd
        def _(pool):
            for u in range(2):
                pool.memset(vals[u][:, :, :, :], 0.0).then_inc(zeroed, 1)
            pool.wait_ge(zeroed, 2)
            for u in range(2):
                for c in range(2):
                    ins = pool.memset(vals[u][c * KS:(c + 1) * KS, :, c:KV:2, D:D + 1], 1.0)
            ins.then_inc(zeroed, 1)

            pool.iota(steps16[:, :], [[P, T]], base=0, channel_multiplier=0, allow_small_or_imprecise_dtypes=True)
            pool.iota(iota_j[:, :], [[1, TILES]], base=0, channel_multiplier=0, allow_small_or_imprecise_dtypes=True)
            pool.iota(iota_j128[:, :], [[P, TILES]], base=0, channel_multiplier=0,
                      allow_small_or_imprecise_dtypes=True)
            pool.iota(list_start[:, :], [[0, 1]], base=0, channel_multiplier=CAP, allow_small_or_imprecise_dtypes=True)
            pool.iota(exp_id[:, :], [[0, P]], base=0, channel_multiplier=1, allow_small_or_imprecise_dtypes=True)
            pool.memset(tile_exp[:, :], 0)
            pool.memset(upto[:, :], 1.0).then_inc(table_chain, 1)
            pool.wait_ge(table_chain, 1)
            pool.affine_select(out=upto[:, :], in_=upto[:, :], compare_op=ALU.is_ge, fill=0.0, base=0,
                               pattern=[[1, E]], channel_multiplier=-1).then_inc(table_const, 2)

            def step(s, u):
                pool.wait_ge(*dve_p.past(s, "pos"))
                hold(pool, passed)
                for j in range(TOPK):
                    pool.indirect_dma_start(
                        out=lists, out_offset=bass.IndirectOffsetOnAxis(ap=pos[u][:, j:j + 1], axis=0),
                        in_=row[u][:, :], in_offset=None).then_inc(scattered[u], 16)

            pipelined(pool, step, T, 0, UR, UR)
            for u in range(UR):
                pool.wait_ge(scattered[u], T // UR * TOPK * 16)


def experts(nc, k, lists, results):
    w_gu_flat = k["w_gu"][:, :, :, :].rearrange("p e c f -> p (e c f)")
    w_dn_flat = k["w_dn"][:, :, :].rearrange("p e c -> p (e c)")
    ident = k["ident"]
    with ExitStack() as ctx:
        def sb(name, shape, dt=F32):
            return ctx.enter_context(nc.sbuf_tensor(f"experts_{name}", shape, dt))

        def sem(name):
            return ctx.enter_context(nc.semaphore(f"experts_{name}"))

        def psum(name, shape):
            return ctx.enter_context(nc.psum_tensor(f"experts_{name}", shape, F32))

        U = 8
        W = FETCH
        LAG = BEHIND
        rows = [sb(f"rows{u}", [P, ROW]) for u in range(U)]
        rows_t = [sb(f"rows_t{u}", [P, CH, P]) for u in range(2)]
        silu = [sb(f"silu{u}", [P, I]) for u in range(2)]
        hid = [sb(f"hid{u}", [P, 2, I]) for u in range(2)]
        hid_hi = [sb(f"hid_hi{u}", [P, P], F32R) for u in range(2)]
        hid_lo = [sb(f"hid_lo{u}", [P, P], F32R) for u in range(2)]
        made = [sb(f"made{u}", [P, C]) for u in range(U)]
        junk = sb("junk", [P, U, TOPK])
        goes_f = sb("goes_f", [P, U])
        goes = [sb(f"goes{u}", [P, 1], I32) for u in range(U)]
        ps_t = [psum(f"ps_t{u}", [P, CH, P]) for u in range(2)]
        ps_gu = [psum(f"ps_gu{u}", [P, 2 * I]) for u in range(2)]
        ps_h = [psum(f"ps_h{u}", [P, P]) for u in range(2)]
        ps_o = [psum(f"ps_o{u}", [P, C]) for u in range(2)]

        tile_row, tile_exp, tile_exp_f = k["tile_row"], k["tile_exp"], k["tile_exp_f"]

        passed = sem("passed")
        loaded = [sem(f"loaded{u}") for u in range(U)]
        stored = [sem(f"stored{u}") for u in range(U)]
        pe_t = Steps(sem("pe_t"), "t")
        act_t = Steps(sem("act_t"), "t")
        pe_gu = Steps(sem("pe_gu"), "gu")
        act_s = Steps(sem("act_s"), "silu")
        dve_h = Steps(sem("dve_h"), "hid")
        pe_h = Steps(sem("pe_h"), "h")
        dve_t = Steps(sem("dve_t"), "high", "low")
        pe_o = Steps(sem("pe_o"), "o")
        act_o = Steps(sem("act_o"), "o")
        dve_to = Steps(sem("dve_to"), "sum", "goes")
        block = ctx.enter_context(nc.Block())

        @block.gpsimd
        def _(pool):
            def step(s, u):
                pool.wait_ge(*dve_to.past(s, "goes"))
                pool.wait_ge(*act_o.past(s, "o"))
                hold(pool, passed)
                pool.indirect_dma_start(
                    out=results, out_offset=bass.IndirectOffsetOnAxis(ap=goes[u][:, 0:1], axis=0),
                    in_=made[u][:, :], in_offset=None, bounds_check=N * TOPK - 1, oob_is_err=False
                ).then_inc(stored[u], 16)

            pipelined(pool, step, TILES, 0, U, U)
            for u in range(U):
                pool.wait_ge(stored[u], TILES // U * 16)

        @block.sync
        def _(sp):
            def step(s, u):
                if later(s, U):
                    sp.wait_ge(*pe_t.past(s - U, "t"))
                    hold(sp, passed)
                    sp.wait_ge(*dve_to.past(s - U, "sum"))
                    hold(sp, passed)
                r = sp.snap(row_regs[u], min_val=0, max_val=E * CAP - P)
                sp.dma_start(rows[u % U][:, :], lists[bass.ds(r, P), :]).then_inc(loaded[u % U], 16)

            row_regs = [sp.alloc_register(f"row_reg{u}") for u in range(W)]

            def begin(s):
                sp.load(row_regs, tile_row[0:1, bass.ds(s, W)])

            pipelined(sp, step, TILES, 0, W, W, begin)

        @block.tensor
        def _(pe):
            exp_regs = [pe.alloc_register(f"exp_reg{u}") for u in range(LAG + W - 1)]

            def begin(s):
                pe.load(exp_regs, tile_exp[0:1, bass.ds(s, LAG + W - 1)])

            def expert(u, lag):
                return pe.snap(exp_regs[u + LAG - lag], min_val=0, max_val=(E - 1) * C)

            def step(s, u):
                b = u % 2
                if live(s, 3, TILES):
                    pe.wait_ge(*dve_h.past(s - 3, "hid"))
                    if later(s, 5):
                        pe.wait_ge(*dve_t.past(s - 5, "low"))
                    pe.transpose(ps_h[1 - b][:, :], hid[1 - b][:, :, :], ident[:, :]).then_inc(*pe_h.up("h"))
                if live(s, 0, TILES):
                    pe.wait_ge(loaded[u % U], (s - u % U) * (16 // U) + 16)
                    if later(s, 2):
                        pe.wait_ge(*act_t.past(s - 2, "t"))
                    for c in range(CH):
                        mm = pe.transpose(ps_t[b][:, c, :], rows[u % U][:, c * P:(c + 1) * P], ident[:, :])
                    mm.then_inc(*pe_t.up("t"))
                if live(s, 1, TILES):
                    e = expert(u, 1)
                    pe.wait_ge(*act_t.past(s - 1, "t"))
                    if later(s, 3):
                        pe.wait_ge(*dve_h.past(s - 3, "hid"))
                    for c in range(CH):
                        mm = pe.matmul(ps_gu[1 - b][:, :], rows_t[1 - b][:, c, :],
                                       w_gu_flat[:, bass.ds(e + c * P if c else e, P)],
                                       start=c == 0, stop=c == CH - 1)
                    mm.then_inc(*pe_gu.up("gu"))
                if live(s, 4, TILES):
                    pe.wait_ge(*dve_t.past(s - 4, "low"))
                    if later(s, 6):
                        pe.wait_ge(*act_o.past(s - 6, "o"))
                    w = w_dn_flat[:, bass.ds(expert(u, 4), C)]
                    pe.matmul(ps_o[b][:, :], hid_hi[b][:, :], w, start=True, stop=False)
                    pe.matmul(ps_o[b][:, :], hid_lo[b][:, :], w, start=False, stop=True).then_inc(*pe_o.up("o"))

            pipelined(pe, step, TILES, LAG, W, W, begin)

        @block.scalar
        def _(act):
            def step(s, u):
                b = u % 2
                if live(s, 0, TILES):
                    act.wait_ge(*pe_t.past(s, "t"))
                    if later(s, 2):
                        act.wait_ge(*pe_gu.past(s - 2, "gu"))
                    nc.scalar.copy(rows_t[b][:, :, :], ps_t[b][:, :, :]).then_inc(*act_t.up("t"))
                if live(s, 1, TILES):
                    act.wait_ge(*pe_gu.past(s - 1, "gu"))
                    if later(s, 3):
                        act.wait_ge(*dve_h.past(s - 3, "hid"))
                    nc.scalar.activation(silu[1 - b][:, :], ps_gu[1 - b][:, 0:I], ACT.Silu).then_inc(*act_s.up("silu"))
                if live(s, 4, TILES):
                    v = (u - 4) % U
                    act.wait_ge(*pe_o.past(s - 4, "o"))
                    if later(s, 4 + U):
                        act.wait_ge(stored[v], (s - 4 - v) * (16 // U))
                    nc.scalar.copy(made[v][:, :], ps_o[b][:, :]).then_inc(*act_o.up("o"))

            pipelined(act, step, TILES, LAG, U, 2 * U)

        @block.vector
        def _(dve):
            def step(s, u):
                b = u % 2
                if live(s, 3, TILES):
                    dve.wait_ge(*pe_h.past(s - 3, "h"))
                    if later(s, 5):
                        dve.wait_ge(*pe_o.past(s - 5, "o"))
                    dve.tensor_copy(hid_hi[1 - b][:, :], ps_h[1 - b][:, :]).then_inc(*dve_t.up("high"))
                if live(s, 0, TILES):
                    dve.wait_ge(loaded[u], (s - u) * (16 // U) + 16)
                    dve.scalar_tensor_tensor(
                        out=junk[:, u, :], in0=rows[u][:, C:C + TOPK], scalar=tile_exp_f[:, at(s)],
                        in1=rows[u][:, C + TOPK:ROW], op0=ALU.is_equal, op1=ALU.mult,
                        accum_out=goes_f[:, u:u + 1]).then_inc(*dve_to.up("sum"))
                if live(s, 3, TILES):
                    dve.wait_ge(*dve_t.past(s - 3, "high"))
                    dve.tensor_tensor(hid_lo[1 - b][:, :], ps_h[1 - b][:, :], hid_hi[1 - b][:, :].bitcast(F32),
                                      ALU.subtract).then_inc(*dve_t.up("low"))
                if live(s, 1, TILES):
                    dve.wait_ge(*act_s.past(s - 1, "silu"))
                    if later(s, 3):
                        dve.wait_ge(*pe_h.past(s - 3, "h"))
                    dve.tensor_tensor(
                        hid[1 - b][:, :, :],
                        silu[1 - b][:, :].rearrange("p (o i) -> p o i", o=1).broadcast_to([P, 2, I]),
                        ps_gu[1 - b][:, I:2 * I].rearrange("p (o i) -> p o i", o=1).broadcast_to([P, 2, I]),
                        ALU.mult).then_inc(*dve_h.up("hid"))
                if live(s, 0, TILES):
                    dve.wait_ge(*dve_to.past(s, "sum"))
                    if later(s, U):
                        dve.wait_ge(stored[u], (s - u) * (16 // U))
                    dve.tensor_scalar(goes[u][:, :], goes_f[:, u:u + 1], BIG, None, ALU.add
                                      ).then_inc(*dve_to.up("goes"))

            pipelined(dve, step, TILES, LAG, U, 2 * U)


def combine(nc, k, results, out_tiles):
    acc, weights = k["acc"], k["weights"]
    with ExitStack() as ctx:
        def sem(name):
            return ctx.enter_context(nc.semaphore(f"combine_{name}"))

        U = 4
        got = [ctx.enter_context(nc.sbuf_tensor(f"got{u}", [P, TOPK, C], F32)) for u in range(U)]
        loaded = [[sem(f"loaded{u}_{h}") for h in range(2)] for u in range(U)]
        passed = sem("passed")
        summed = Steps(sem("summed"), *[f"k{j}" for j in range(TOPK)], "both")
        divided = Steps(sem("divided"), "softmax", "probs", "total", "inverse", "weights")
        stored = sem("stored")
        block = ctx.enter_context(nc.Block())
        by_tile = results.rearrange("(n p k) c -> n p k c", p=P, k=TOPK)

        @block.sync
        def _(sp):
            def step(s, u):
                if later(s, U):
                    sp.wait_ge(*summed.past(s - U, "both"))
                    hold(sp, passed)
                for h in range(2):
                    ks = slice(h * TOPK // 2, (h + 1) * TOPK // 2)
                    sp.dma_start(got[u][:, ks, :], by_tile[at(s), :, ks].rearrange("n p k c -> (n p) k c")
                                 ).then_inc(loaded[u][h], 16)

            pipelined(sp, step, T, 0, U, U)

        @block.vector
        def _(dve):
            total = k["esum"]
            over = total[:, :].rearrange("p (t o) -> p t o", o=1).broadcast_to([P, T, TOPK])
            dve.reciprocal(total[:, :], total[:, :]).then_inc(*divided.up("softmax"))
            dve.wait_ge(*divided.past(0, "softmax"))
            dve.tensor_tensor(weights[:, :, :], weights[:, :, :], over, ALU.mult).then_inc(*divided.up("probs"))
            dve.wait_ge(*divided.past(0, "probs"))
            dve.tensor_reduce(total[:, :], weights[:, :, :], AX, ALU.add).then_inc(*divided.up("total"))
            dve.wait_ge(*divided.past(0, "total"))
            dve.reciprocal(total[:, :], total[:, :]).then_inc(*divided.up("inverse"))
            dve.wait_ge(*divided.past(0, "inverse"))
            dve.tensor_tensor(weights[:, :, :], weights[:, :, :], over, ALU.mult).then_inc(*divided.up("weights"))
            dve.wait_ge(*divided.past(0, "weights"))

            def step(s, u):
                x_t = acc[:, at(s), :].rearrange("p o c -> p (o c)")
                odd = got[u][:, 1, :]
                for j in range(TOPK):
                    if j % (TOPK // 2) == 0:
                        dve.wait_ge(loaded[u][j // (TOPK // 2)], (s - u) * (16 // U) + 16)
                    w = weights[:, at(s), j:j + 1].rearrange("p o k -> p (o k)")
                    if j >= 2:
                        dve.wait_ge(*summed.past(s, f"k{j - 2}"))
                    if j == 1:
                        ins = dve.tensor_scalar(odd, odd, w, None, ALU.mult)
                    else:
                        to = odd if j % 2 else x_t
                        ins = dve.scalar_tensor_tensor(out=to, in0=got[u][:, j, :], scalar=w, in1=to,
                                                       op0=ALU.mult, op1=ALU.add)
                    ins.then_inc(*summed.up(f"k{j}"))
                dve.wait_ge(*summed.past(s, f"k{TOPK - 1}"))
                dve.tensor_tensor(x_t, x_t, odd, ALU.add).then_inc(*summed.up("both"))

            pipelined(dve, step, T, 0, U, U)

        @block.scalar
        def _(act):
            def step(s, u):
                act.wait_ge(*summed.past(s, "both"))
                hold(act, passed)
                act.dma_start(out_tiles[:, at(s), :], acc[:, at(s), :]).then_inc(stored, 16)

            pipelined(act, step, T, 0, U, U)
            act.wait_ge(stored, T * 16)


_INS = ["x", "ctx_512", "L0_ffn_router_w", "L0_ffn_gate_up_proj", "L0_ffn_down_proj", "L0_ffn_shared_gate_w",
        "L0_ffn_shared_up_w", "L0_ffn_shared_down_w", "L0_ffn_shared_expert_gate_w"]


def kernel(**inputs):
    import numpy as np
    import concourse.bacc as bacc
    from concourse.bass_utils import run_bass_kernel_spmd

    nc = bacc.Bacc("TRN2", target_bir_lowering=False, num_devices=1)
    arrays, args = {}, []
    for name in _INS:
        a = np.ascontiguousarray(inputs[name])
        arrays[f"in_{name}"] = a
        args.append(nc.dram_tensor(f"in_{name}", a.shape, mybir.dt.from_np(a.dtype), kind="ExternalInput").ap())
    out = nc.dram_tensor("out", (B, S, C), F32, kind="ExternalOutput").ap()
    moe_block(nc, *args, out)
    done = run_bass_kernel_spmd(nc, [arrays], core_ids=[0])
    return done.results[0]["out"]
```
